# Optimizing a Trainium2 kernel written in Bass

```python
import numpy as np
import jax
import jax.numpy as jnp

def _softmax(x, axis=-1):
    return jax.nn.softmax(x, axis=axis)

def _gelu(x):
    return jax.nn.gelu(x, approximate=True)

def _silu(x):
    return jax.nn.silu(x)

def _sigmoid(x):
    return jax.nn.sigmoid(x)

def _layernorm(x, axis=-1, eps=1e-05):
    m = jnp.mean(x, axis=axis, keepdims=True)
    v = jnp.var(x, axis=axis, keepdims=True)
    return (x - m) / jnp.sqrt(v + eps)

def _scatter_add(tgt, idx, src, axis=0):
    return tgt.at[idx].add(src)

def _segment_sum(src, seg, n):
    return jax.ops.segment_sum(src, seg, n)
kernel_name = 'mk_seq_postln_d2_jaxref_r8_33cdae'

def setup_inputs(seed: int=0):
    np.random.seed(seed)
    _w = jnp.asarray

    def _L0_attn_setup():
        import jax, jax.numpy as jnp
        import numpy as np
        N_HEADS = 16
        D_MODEL = 128
        key = jax.random.key(seed)
        kx, kw = jax.random.split(key)
        x = jax.random.normal(kx, (2, 256, 128), dtype=jnp.float32)
        W_qkv = jax.random.normal(kw, (128, 3 * 128), dtype=jnp.float32) * 0.02
        return {'x': x, 'W_qkv': W_qkv}
    _L0_attn_in = _L0_attn_setup()

    def _L0_ffn_setup():
        import jax, jax.numpy as jnp
        import numpy as np
        H = 128
        I = 64
        E = 32
        TOP_K = 6
        N_GROUP = 8
        TOPK_GROUP = 4
        SCALE = 2.5
        N_SHARED = 2
        SI = I * N_SHARED
        B, S = (2, 128)
        key = jax.random.key(seed)
        ks = jax.random.split(key, 8)
        x = jax.random.normal(ks[0], (B, S, H), jnp.float32)
        gate_weight = jax.random.normal(ks[1], (E, H), jnp.float32) * 0.02
        e_score_correction_bias = jax.random.normal(ks[2], (E,), jnp.float32) * 0.01
        experts_gate_up = jax.random.normal(ks[3], (E, 2 * I, H), jnp.float32) * 0.02
        experts_down = jax.random.normal(ks[4], (E, H, I), jnp.float32) * 0.02
        shared_gate_w = jax.random.normal(ks[5], (SI, H), jnp.float32) * 0.02
        shared_up_w = jax.random.normal(ks[6], (SI, H), jnp.float32) * 0.02
        shared_down_w = jax.random.normal(ks[7], (H, SI), jnp.float32) * 0.02
        return {'x': x, 'gate_weight': gate_weight, 'e_score_correction_bias': e_score_correction_bias, 'experts_gate_up': experts_gate_up, 'experts_down': experts_down, 'shared_gate_w': shared_gate_w, 'shared_up_w': shared_up_w, 'shared_down_w': shared_down_w}
    _L0_ffn_in = _L0_ffn_setup()

    def _L1_attn_setup():
        import jax, jax.numpy as jnp
        import numpy as np
        D = 128
        H = 16
        HD = D // H
        ROPE_BASE = 10000.0
        EPS_RMS = 1e-08
        EPS_RENORM = 1e-08

        def rms_norm(x, scale):
            norm = jnp.mean(x * x, axis=-1, keepdims=True)
            return scale * (x * jax.lax.rsqrt(norm + EPS_RMS))

        def rope_tables(seq_len):
            inv_freq = 1.0 / ROPE_BASE ** (jnp.arange(0, HD, 2, dtype=jnp.float32) / HD)
            t = jnp.arange(seq_len, dtype=jnp.float32)
            freqs = t[:, None] * inv_freq[None, :]
            emb = jnp.concatenate([freqs, freqs], axis=-1)
            return (jnp.cos(emb), jnp.sin(emb))

        def apply_rotary(x, cos, sin):
            x1 = x[..., ::2]
            x2 = x[..., 1::2]
            x_rot = jnp.stack([-x2, x1], axis=-1).reshape(x.shape)
            return x * cos + x_rot * sin
        key = jax.random.key(seed)
        ks = jax.random.split(key, 11)
        B, L = (2, 256)
        s = 1.0 / np.sqrt(D)
        inp = {'x': jax.random.normal(ks[0], (B, L, D), dtype=jnp.float32), 'q_w': jax.random.uniform(ks[1], (D, D), jnp.float32, -s, s), 'q_b': jax.random.uniform(ks[2], (D,), jnp.float32, -s, s), 'k_w': jax.random.uniform(ks[3], (D, D), jnp.float32, -s, s), 'k_b': jax.random.uniform(ks[4], (D,), jnp.float32, -s, s), 'v_w': jax.random.uniform(ks[5], (D, D), jnp.float32, -s, s), 'v_b': jax.random.uniform(ks[6], (D,), jnp.float32, -s, s), 'o_w': jax.random.uniform(ks[7], (D, D), jnp.float32, -s, s), 'o_b': jax.random.uniform(ks[8], (D,), jnp.float32, -s, s), 'qn_scale': jnp.ones((D,), dtype=jnp.float32), 'kn_scale': jnp.ones((D,), dtype=jnp.float32)}
        return inp
    _L1_attn_in = _L1_attn_setup()

    def _L1_ffn_setup():
        import jax, jax.numpy as jnp
        import numpy as np
        DIM = 128
        HIDDEN = 384
        SCALE = 1.0 / 127.0

        def _dequant(w_int, dtype):
            return w_int.astype(dtype) * jnp.asarray(SCALE, dtype)
        key = jax.random.key(seed)
        k_x, k_g, k_u, k_d = jax.random.split(key, 4)
        x = jax.random.normal(k_x, (4, 256, DIM), dtype=jnp.float32)
        w_gate = jax.random.randint(k_g, (HIDDEN, DIM), -127, 128, dtype=jnp.int32)
        w_up = jax.random.randint(k_u, (HIDDEN, DIM), -127, 128, dtype=jnp.int32)
        w_down = jax.random.randint(k_d, (DIM, HIDDEN), -127, 128, dtype=jnp.int32)
        return {'x': x, 'w_gate': w_gate, 'w_up': w_up, 'w_down': w_down}
    _L1_ffn_in = _L1_ffn_setup()
    _d = {'L0_attn_x': _L0_attn_in['x'], 'L0_attn_W_qkv': _L0_attn_in['W_qkv'], 'L0_ffn_gate_weight': _L0_ffn_in['gate_weight'], 'L0_ffn_e_score_correction_bias': _L0_ffn_in['e_score_correction_bias'], 'L0_ffn_experts_gate_up': _L0_ffn_in['experts_gate_up'], 'L0_ffn_experts_down': _L0_ffn_in['experts_down'], 'L0_ffn_shared_gate_w': _L0_ffn_in['shared_gate_w'], 'L0_ffn_shared_up_w': _L0_ffn_in['shared_up_w'], 'L0_ffn_shared_down_w': _L0_ffn_in['shared_down_w'], 'L1_attn_q_w': _L1_attn_in['q_w'], 'L1_attn_q_b': _L1_attn_in['q_b'], 'L1_attn_k_w': _L1_attn_in['k_w'], 'L1_attn_k_b': _L1_attn_in['k_b'], 'L1_attn_v_w': _L1_attn_in['v_w'], 'L1_attn_v_b': _L1_attn_in['v_b'], 'L1_attn_o_w': _L1_attn_in['o_w'], 'L1_attn_o_b': _L1_attn_in['o_b'], 'L1_attn_qn_scale': _L1_attn_in['qn_scale'], 'L1_attn_kn_scale': _L1_attn_in['kn_scale'], 'L1_ffn_w_gate': _L1_ffn_in['w_gate'], 'L1_ffn_w_up': _L1_ffn_in['w_up'], 'L1_ffn_w_down': _L1_ffn_in['w_down']}
    _x0 = _d['L0_attn_x']
    _d['L0_attn_x'] = jax.random.normal(jax.random.fold_in(jax.random.key(seed), 1), (8, 512, 128), dtype=_x0.dtype)
    del _x0
    return _d

def reference(L0_attn_x, L0_attn_W_qkv, L0_ffn_gate_weight, L0_ffn_e_score_correction_bias, L0_ffn_experts_gate_up, L0_ffn_experts_down, L0_ffn_shared_gate_w, L0_ffn_shared_up_w, L0_ffn_shared_down_w, L1_attn_q_w, L1_attn_q_b, L1_attn_k_w, L1_attn_k_b, L1_attn_v_w, L1_attn_v_b, L1_attn_o_w, L1_attn_o_b, L1_attn_qn_scale, L1_attn_kn_scale, L1_ffn_w_gate, L1_ffn_w_up, L1_ffn_w_down):

    def _L0_attn_ref(x, W_qkv):
        import jax, jax.numpy as jnp
        import numpy as np
        N_HEADS = 16
        D_MODEL = 128
        B, N, C = x.shape
        hd = D_MODEL // N_HEADS
        qkv = x @ W_qkv
        q, k, v = jnp.split(qkv, 3, axis=-1)

        def heads(t):
            return t.reshape(B, N, N_HEADS, hd).transpose(0, 2, 1, 3)
        q, k, v = (heads(q), heads(k), heads(v))
        scores = jnp.einsum('bhnd,bhmd->bhnm', q, k) / jnp.sqrt(jnp.float32(D_MODEL))
        attn = jax.nn.softmax(scores, axis=-1)
        out = jnp.einsum('bhnm,bhmd->bhnd', attn, v)
        out = out.transpose(0, 2, 1, 3).reshape(B, N, D_MODEL)
        return out

    def _L0_ffn_ref(x, gate_weight, e_score_correction_bias, experts_gate_up, experts_down, shared_gate_w, shared_up_w, shared_down_w):
        import jax, jax.numpy as jnp
        import numpy as np
        H = 128
        I = 64
        E = 32
        TOP_K = 6
        N_GROUP = 8
        TOPK_GROUP = 4
        SCALE = 2.5
        N_SHARED = 2
        SI = I * N_SHARED
        B, S = (2, 128)
        b, s, h = x.shape
        xf = x.reshape(-1, h)
        T = xf.shape[0]
        logits = xf.astype(jnp.float32) @ gate_weight.astype(jnp.float32).T
        scores = jax.nn.sigmoid(logits)
        sfc = scores + e_score_correction_bias[None, :]
        gs = E // N_GROUP
        group_scores = sfc.reshape(T, N_GROUP, gs).max(axis=-1)
        _, gidx = jax.lax.top_k(group_scores, TOPK_GROUP)
        gmask = jnp.zeros((T, N_GROUP), bool).at[jnp.arange(T)[:, None], gidx].set(True)
        smask = jnp.repeat(gmask, gs, axis=1)
        masked = jnp.where(smask, sfc, 0.0)
        _, topk_idx = jax.lax.top_k(masked, TOP_K)
        tw = jnp.take_along_axis(scores, topk_idx, axis=1)
        tw = tw / (tw.sum(-1, keepdims=True) + 1e-20)
        tw = (tw * SCALE).astype(xf.dtype)
        combine = jnp.zeros((T, E), xf.dtype).at[jnp.arange(T)[:, None], topk_idx].add(tw)

        def expert_step(acc, inp):
            gu, dn, c = inp
            g = xf @ gu[:I].T
            u = xf @ gu[I:].T
            o = jax.nn.silu(g) * u @ dn.T
            return (acc + c[:, None] * o, None)
        routed, _ = jax.lax.scan(expert_step, jnp.zeros_like(xf), (experts_gate_up, experts_down, combine.T))
        sh = jax.nn.silu(xf @ shared_gate_w.T) * (xf @ shared_up_w.T)
        shared_out = sh @ shared_down_w.T
        return (routed + shared_out).reshape(b, s, h)

    def _L1_attn_ref(x, q_w, q_b, k_w, k_b, v_w, v_b, o_w, o_b, qn_scale, kn_scale):
        import jax, jax.numpy as jnp
        import numpy as np
        D = 128
        H = 16
        HD = D // H
        ROPE_BASE = 10000.0
        EPS_RMS = 1e-08
        EPS_RENORM = 1e-08

        def rms_norm(x, scale):
            norm = jnp.mean(x * x, axis=-1, keepdims=True)
            return scale * (x * jax.lax.rsqrt(norm + EPS_RMS))

        def rope_tables(seq_len):
            inv_freq = 1.0 / ROPE_BASE ** (jnp.arange(0, HD, 2, dtype=jnp.float32) / HD)
            t = jnp.arange(seq_len, dtype=jnp.float32)
            freqs = t[:, None] * inv_freq[None, :]
            emb = jnp.concatenate([freqs, freqs], axis=-1)
            return (jnp.cos(emb), jnp.sin(emb))

        def apply_rotary(x, cos, sin):
            x1 = x[..., ::2]
            x2 = x[..., 1::2]
            x_rot = jnp.stack([-x2, x1], axis=-1).reshape(x.shape)
            return x * cos + x_rot * sin
        B, L, _ = x.shape
        q = rms_norm(x, qn_scale) @ q_w.T + q_b
        k = rms_norm(x, kn_scale) @ k_w.T + k_b
        v = x @ v_w.T + v_b
        q = q.reshape(B, L, H, HD).transpose(0, 2, 1, 3)
        k = k.reshape(B, L, H, HD).transpose(0, 2, 1, 3)
        v = v.reshape(B, L, H, HD).transpose(0, 2, 1, 3)
        cos, sin = rope_tables(L)
        q = apply_rotary(q, cos, sin)
        k = apply_rotary(k, cos, sin)
        scale = 1.0 / np.sqrt(HD)
        scores = jnp.einsum('bhqd,bhkd->bhqk', q, k) * scale
        weights = jax.nn.sigmoid(scores)
        weights = weights / (jnp.sum(weights, axis=-1, keepdims=True) + EPS_RENORM)
        attn = jnp.einsum('bhqk,bhkd->bhqd', weights, v)
        attn = attn.transpose(0, 2, 1, 3).reshape(B, L, D)
        return attn @ o_w.T + o_b

    def _L1_ffn_ref(x, w_gate, w_up, w_down):
        import jax, jax.numpy as jnp
        import numpy as np
        DIM = 128
        HIDDEN = 384
        SCALE = 1.0 / 127.0

        def _dequant(w_int, dtype):
            return w_int.astype(dtype) * jnp.asarray(SCALE, dtype)
        wg = _dequant(w_gate, x.dtype)
        wu = _dequant(w_up, x.dtype)
        wd = _dequant(w_down, x.dtype)
        gate = jnp.einsum('bsd,hd->bsh', x, wg)
        up = jnp.einsum('bsd,hd->bsh', x, wu)
        h = jax.nn.silu(gate) * up
        return jnp.einsum('bsh,dh->bsd', h, wd)
    x = L0_attn_x
    x = _layernorm(x + _L0_attn_ref(x, L0_attn_W_qkv), axis=-1)
    x = _layernorm(x + _L0_ffn_ref(x, L0_ffn_gate_weight, L0_ffn_e_score_correction_bias, L0_ffn_experts_gate_up, L0_ffn_experts_down, L0_ffn_shared_gate_w, L0_ffn_shared_up_w, L0_ffn_shared_down_w), axis=-1)
    x = _layernorm(x + _L1_attn_ref(x, L1_attn_q_w, L1_attn_q_b, L1_attn_k_w, L1_attn_k_b, L1_attn_v_w, L1_attn_v_b, L1_attn_o_w, L1_attn_o_b, L1_attn_qn_scale, L1_attn_kn_scale), axis=-1)
    x = _layernorm(x + _L1_ffn_ref(x, L1_ffn_w_gate, L1_ffn_w_up, L1_ffn_w_down), axis=-1)
    return x

_drawn_inputs = setup_inputs


def setup_inputs(seed=0):
    import zlib

    import numpy as np

    out = dict(_drawn_inputs(seed))
    spreads = {'L1_attn_qn_scale': (1.0, 0.6), 'L1_attn_kn_scale': (1.0, 0.6)}
    factors = {'L0_attn_W_qkv': 3.77,
     'L0_ffn_gate_weight': 8.0,
     'L0_ffn_e_score_correction_bias': 8.0,
     'L0_ffn_experts_gate_up': 8.0,
     'L0_ffn_experts_down': 8.0,
     'L0_ffn_shared_gate_w': 6.864,
     'L0_ffn_shared_up_w': 6.813,
     'L0_ffn_shared_down_w': 6.762,
     'L1_attn_q_w': 8.0,
     'L1_attn_q_b': 200.0,
     'L1_attn_k_w': 8.0,
     'L1_attn_k_b': 200.0}
    for name, (base, spread) in spreads.items():
        noise = np.random.default_rng([zlib.crc32(name.encode()), seed]).standard_normal(out[name].shape)
        drawn = base * np.exp(spread * noise) if base else spread * noise
        out[name] = jnp.asarray(drawn.astype(out[name].dtype))
    for name, factor in factors.items():
        out[name] = (out[name] * factor).astype(out[name].dtype)
    return out
```

```python
from contextlib import ExitStack

import concourse.bass as bass
from concourse import mybir

F32 = mybir.dt.float32
BF16 = mybir.dt.bfloat16
U32 = mybir.dt.uint32
I32 = mybir.dt.int32
ALU = mybir.AluOpType
ACT = mybir.ActivationFunctionType
AX = mybir.AxisListType

P = 128
NB = 8
T = 512
NT = T // P
H = 16
HD = P // H
HG = 4
NG = H // HG
CT = P // HG
PARTS = 3
QKR = PARTS * PARTS * HD
QKP = 96
MXR = QKP + PARTS
UN = 2
NU = NG * NT * (HG // UN)
PSLOTS = 8
NE = NG * NT
E = 32
EI = 64
NPAIR = E // 2
FF = NPAIR + 1
TOPG, TOPK, NGRP = 4, 6, 8
ROUTE_SCALE = 2.5
HID = 384
NH3 = HID // P
LN_EPS = 1e-5
RMS_EPS = 1e-8
RENORM_EPS = 1e-8
WEIGHT_SCALE = 1.0 / 127.0
S1_FROM = 4
S1_N = H * NT
MT_AT = 40
HH = H // 2


def s1_range(u):
    units = NU - S1_FROM
    at = lambda k: max(0, -(-S1_N * k // units))
    return range(at(u - S1_FROM), at(u - S1_FROM + 1)) if u >= S1_FROM else range(0)




def layernorm_buffers(ctx, nc, name):
    def sb(n, shape):
        return ctx.enter_context(nc.sbuf_tensor(f"{name}_{n}", shape, F32))

    def sem(n):
        return ctx.enter_context(nc.semaphore(f"{name}_{n}"))

    return {"st": sb("st", [P, NT, 6]), "mv": sb("mv", [P, NT, 2]), "ve": sb("ve", [P, NT]),
            "rstd": sb("rstd", [P, NT]), "gate": sb("gate", [P, 1]),
            "dve": sem("ln_dve"), "pool": sem("ln_pool"), "x_done": sem("x_done")}


def layernorm_dve(nc, dve, g, ln, b, y):
    X = g["X"]
    for k in range(NT):
        nc.vector.bn_stats(ln["st"][:, k, :], y[:, k, :]).then_inc(ln["dve"], 1)
    dve.wait_ge(ln["dve"], 2 * NT * b + NT)
    nc.vector.memset(ln["gate"][:, :], 0.0)
    for k in range(NT):
        nc.vector.bn_aggr(ln["mv"][:, k, :], ln["st"][:, k, :]).then_inc(ln["dve"], 1)
    dve.wait_ge(ln["pool"], 2 * b + 2)
    for k in range(NT):
        ins = nc.vector.tensor_scalar(X[:, b, k, :], y[:, k, :], ln["mv"][:, k, 0:1], ln["rstd"][:, k:k + 1],
                                      ALU.subtract, ALU.mult)
    ins.then_inc(ln["x_done"], 1)


def layernorm_pool(nc, pool, g, ln, b):
    pool.wait_ge(ln["dve"], 2 * NT * (b + 1))
    nc.gpsimd.tensor_tensor(ln["ve"][:, :], ln["mv"][:, :, 1], g["eps"][:, :], ALU.add).then_inc(ln["pool"], 1)
    pool.wait_ge(ln["pool"], 2 * b + 1)
    nc.gpsimd.tensor_tensor(ln["rstd"][:, :], ln["ve"][:, :], g["neg_half"][:, :], ALU.pow).then_inc(ln["pool"], 1)


def attention0(nc, g, x_t, w_qkv):
    X, ident = g["X"], g["ident"]
    scratch = [[nc.dram_tensor(f"parts_{n}{i}", [5, P, T], BF16).ap() for i in range(2)] for n in "qk"]
    with ExitStack() as ctx:
        def sb(name, shape, dt=F32):
            return ctx.enter_context(nc.sbuf_tensor("a0_" + name, shape, dt))

        def sem(name):
            return ctx.enter_context(nc.semaphore("a0_" + name))

        w = sb("w", [P, 3, P])
        xt = [sb(f"xt{i}", [P, T]) for i in range(2)]
        qk = sb("qk", [P, 2, T])
        rest = sb("rest", [P, 2, T])
        parts = sb("parts", [P, 2, PARTS, T], BF16)
        qs = [sb(f"qs{i}", [P, H, T], BF16) for i in range(2)]
        ks = [sb(f"ks{i}", [P, H, T], BF16) for i in range(2)]
        va = [sb(f"va{i}", [P, NT, H, CT]) for i in range(2)]
        prob = sb("prob", [P, PSLOTS, UN, T])
        osb = sb("osb", [P, 2, T])
        nmax = sb("nmax", [P, H, NT])
        mrest = sb("mrest", [HH * NT, P])
        mparts = sb("mparts", [HH * NT, PARTS, P], BF16)
        rec = sb("rec", [P, NT, HG])
        att = sb("att", [P, NT, P])
        ln = layernorm_buffers(ctx, nc, "a0")
        ps_s = ctx.enter_context(nc.psum_tensor("a0_ps_s", [P, 2, UN, T], F32))
        ps_f = ctx.enter_context(nc.psum_tensor("a0_ps_f", [P, 2, T], F32))
        ps_o = ctx.enter_context(nc.psum_tensor("a0_ps_o", [P, T], F32))
        ps_t = ctx.enter_context(nc.psum_tensor("a0_ps_t", [P, NT, P], F32))

        w_in, x_in, xt_in = sem("w_in"), g["x_in"], [sem(f"xt_in{i}") for i in range(2)]
        cleared = sem("cleared")
        q_done, k_done, v_done = sem("q_done"), sem("k_done"), sem("v_done")
        q_taken, k_taken, v_taken = sem("q_taken"), sem("k_taken"), sem("v_taken")
        split, parts_done = sem("split"), sem("parts_done")
        parts_out, stack_in, max_in = sem("parts_out"), sem("stack_in"), sem("max_in")
        s1_done, max_done = sem("s1_done"), sem("max_done")
        mt_done, mt_chain, mt_split, mt_parts = (sem(f"mt_{n}") for n in ("done", "chain", "split", "parts"))
        s2_done, exp_done, pv_done = sem("s2_done"), sem("exp_done"), sem("pv_done")
        o_taken, ot_done, rec_done, att_done, sum_done = (
            sem(n) for n in ("o_taken", "ot_done", "rec_done", "att_done", "sum_done"))
        S2_C, EXP_C, PV_C, O_C, OT_C, ATT_C = NU, 2, PSLOTS // 2, 1, 2, 1
        FILL = 6 * 16
        PARTS_C, OUT_C, MAX_C = 2, 3 * 16, PARTS * 16

        block = ctx.enter_context(nc.Block())

        @block.sync
        def _(sp):
            sp.dma_start(w[:, :, :], w_qkv.rearrange("d (a c) -> d a c", a=3)).then_inc(w_in, 16)

            def load_xt(b, p):
                sp.dma_start(xt[p][:, :], x_t[:, bass.ds(b * T, T)]).then_inc(xt_in[p], 16)

            def parts_to_dram(b, p):
                for n, seg in ((0, 0), (1, 0), (1, 1)):
                    if seg == 0:
                        sp.wait_ge(parts_done, 2 * b + n + 1 + PARTS_C)
                    dst = scratch[n][p].rearrange("r p t -> p r t")
                    if seg == 0:
                        sp.dma_start(dst[:, 0:PARTS, :], parts[:, n, :, :]).then_inc(parts_out, 16)
                    else:
                        sp.dma_start(dst[:, PARTS:5, :], parts[:, n, 0:2, :]).then_inc(parts_out, 16)

            def stack(b, p):
                sp.wait_ge(parts_out, 48 * (b + 1) + OUT_C)
                for n, dst in ((0, qs), (1, ks)):
                    src = scratch[n][p]
                    rows = PARTS * HD
                    src = bass.AP(tensor=src.tensor, offset=0,
                                  ap=[[n * HD * H * T, PARTS], [H * T, rows], [1, H * T]])
                    sp.dma_start(dst[p][0:QKR, :, :], src).then_inc(stack_in, 16)

            def max_rows(b, p, half_no):
                sp.wait_ge(mt_parts, 2 * b + half_no + 1)
                for r in range(PARTS):
                    sp.dma_start(qs[p][QKP + r:QKP + r + 1, half_no * HH:(half_no + 1) * HH, :],
                                 mparts[:, r, :]).then_inc(max_in, 16)

            def step(b, p, qk_on, front, back):
                if qk_on:
                    sp.wait_ge(v_done, b + 1)
                    load_xt(b + 2, p)
                if back:
                    max_rows(b, p, 1)
                if front:
                    sp.wait_ge(s2_done, NU * b + S2_C)
                    stack(b + 1, 1 - p)
                if qk_on:
                    parts_to_dram(b + 2, p)
                if front:
                    max_rows(b + 1, 1 - p, 0)

            sp.dma_start(X[:, :, :, :], g["x"].rearrange("b (k p) d -> p b k d", p=P)).then_inc(x_in, 16)
            load_xt(0, 0)
            load_xt(1, 1)
            for i in range(2):
                for dst, value, r0, r1 in ((qs, 0, QKR, QKP), (ks, 0, QKR, QKP), (ks, 1, QKP, MXR)):
                    src = bass.AP(tensor=g["fill"].tensor, offset=value * H * T, ap=[[0, r1 - r0], [1, H * T]])
                    sp.dma_start(dst[i][r0:r1, :, :], src).then_inc(stack_in, 16)
            parts_to_dram(0, 0)
            stack(0, 0)
            parts_to_dram(1, 1)
            max_rows(0, 0, 0)
            with sp.Fori(0, (NB - 2) // 2) as i:
                step(2 * i, 0, True, True, True)
                step(2 * i + 1, 1, True, True, True)
            step(NB - 2, 0, False, True, True)
            step(NB - 1, 1, False, False, True)

        @block.scalar
        def _(act):
            def take(dst, src, ready, value, done):
                act.wait_ge(ready, value)
                nc.scalar.activation(dst, src, ACT.Copy).then_inc(done, 1)

            def take_v(b, p):
                take(va[p][:, :, :, 0:HD],
                     ps_f[:, 1, :].rearrange("p (k h d) -> p k h d", k=NT, h=H), v_done, b + 1, v_taken)

            def take_qk(b, n):
                act.wait_ge(parts_done, 2 * b + n - 1 + PARTS_C)
                take(qk[:, n, :], ps_f[:, n, :], (q_done, k_done)[n], b + 1, (q_taken, k_taken)[n])

            def take_o(b, grp):
                act.wait_ge(ot_done, NG * b + grp - 1 + OT_C)
                take(osb[:, grp % 2, :], ps_o[:, :], pv_done, NE * b + NT * (grp + 1) + PV_C, o_taken)

            def step(b, p, qk_on, front, back):
                if front:
                    take_v(b + 1, 1 - p)
                for u in range(NU):
                    if back:
                        act.wait_ge(s2_done, NU * b + u + 1 + S2_C)
                        if u % 2 == 0:
                            act.wait_ge(pv_done, NE * b + u // 2 - PSLOTS // 2 + 1 + PV_C)
                        nc.scalar.activation(prob[:, u % PSLOTS, :, :], ps_s[:, u % 2, :, :], ACT.Exp,
                                             scale=float(P) ** -0.5).then_inc(exp_done, 1)
                        if u % 8 == 1 and u > 8:
                            take_o(b, u // 8 - 1)
                    if qk_on and u in (2, 3):
                        take_qk(b + 2, u - 2)
                if back:
                    take_o(b, NG - 1)

            act.sem_inc(exp_done, EXP_C)
            act.sem_inc(o_taken, O_C)
            act.wait_ge(cleared, 4)
            step(-2, 0, True, False, False)
            step(-1, 1, True, True, False)
            with act.Fori(0, (NB - 2) // 2) as i:
                step(2 * i, 0, True, True, True)
                step(2 * i + 1, 1, True, True, True)
            step(NB - 2, 0, False, True, True)
            step(NB - 1, 1, False, False, True)

        @block.tensor
        def _(pe):
            pe.sem_inc(s2_done, S2_C)
            pe.sem_inc(pv_done, PV_C)
            pe.sem_inc(ot_done, OT_C)
            pe.wait_ge(w_in, 16)
            pe.wait_ge(g["consts_in"], 16)

            def turn_max(b, half_no):
                if half_no:
                    pe.wait_ge(max_done, S1_N * (b + 1))
                else:
                    pe.wait_ge(max_done, S1_N * b + MT_AT - 1)
                nc.tensor.transpose(ps_f[0:HH * NT, 0, 0:P], nmax[:, half_no * HH:(half_no + 1) * HH, :],
                                    ident[:, :]).then_inc(mt_done, 1)

            def v_product(b, p, after_k):
                if after_k:
                    pe.wait_ge(k_taken, b + 1)
                pe.wait_ge(xt_in[p], 8 * (b - p) + 16)
                for kt in range(NT):
                    mm = nc.tensor.matmul(ps_f[:, 1, kt * P:(kt + 1) * P], xt[p][:, kt * P:(kt + 1) * P],
                                          w[:, 2, :], start=True, stop=True)
                mm.then_inc(v_done, 1)

            def qk_product(b, p, n, mt, front):
                pe.wait_ge(xt_in[p], 8 * (b - p) + 16)
                if n == 0 and mt:
                    pe.wait_ge(mt_split, 2 * (b - 2) + 2)
                if n == 0 and front and not mt:
                    pe.wait_ge(q_taken, b)
                if n == 1 and front:
                    pe.wait_ge(v_taken, b)
                nc.tensor.matmul(ps_f[:, n, :], w[:, n, :], xt[p][:, :], start=True,
                                 stop=True).then_inc((q_done, k_done)[n], 1)

            def s1(b, p, n, qk_on):
                h, qt = n // NT, n % NT
                if n == 0:
                    pe.wait_ge(stack_in, 32 * (b + 1) + FILL)
                if n < 2:
                    if qk_on:
                        pe.wait_ge((q_taken, k_taken)[n], b + 2)
                    elif n == 0:
                        pe.wait_ge(mt_split, 2 * b)
                    else:
                        pe.wait_ge(v_taken, b + 1)
                else:
                    pe.wait_ge(max_done, S1_N * b + n - 1)
                if n == MT_AT:
                    pe.wait_ge(mt_split, 2 * b + 1)
                nc.tensor.matmul(ps_f[:, n % 2, :], qs[p][0:QKP, h, qt * P:(qt + 1) * P], ks[p][0:QKP, h, :],
                                 start=True, stop=True).then_inc(s1_done, 1)

            def s2(b, p, u):
                grp, kt, pair = u // (2 * NT), u // 2 % NT, u % 2
                if u in (0, NU // 2):
                    pe.wait_ge(max_in, MAX_C * (2 * b + u // (NU // 2) + 1) + MAX_C)
                pe.wait_ge(exp_done, NU * b + u - 1 + EXP_C)
                for i in range(UN):
                    h = grp * HG + pair * UN + i
                    mm = nc.tensor.matmul(ps_s[:, u % 2, i, :], ks[p][0:MXR, h, kt * P:(kt + 1) * P],
                                          qs[p][0:MXR, h, :], start=True, stop=True)
                mm.then_inc(s2_done, 1)

            def pv(b, p, e):
                grp, kt = e // NT, e % NT
                if e == 0:
                    pe.wait_ge(v_taken, b + 1)
                if kt == 0:
                    pe.wait_ge(o_taken, NG * b + grp + O_C)
                pe.wait_ge(exp_done, NU * b + 2 * e + 2 + EXP_C)
                for j in range(HG):
                    mm = nc.tensor.matmul(ps_o[j * CT:(j + 1) * CT, :], va[p][:, kt, grp * HG + j, :],
                                          prob[:, (2 * e + j // UN) % PSLOTS, j % UN, :],
                                          start=(kt == 0), stop=(kt == NT - 1))
                mm.then_inc(pv_done, 1)

            def turn_o(b, grp):
                pe.wait_ge(o_taken, NG * b + grp + 1 + O_C)
                pe.wait_ge(att_done, NG * b + grp + ATT_C)
                for qt in range(NT):
                    mm = nc.tensor.transpose(ps_t[:, qt, :], osb[:, grp % 2, qt * P:(qt + 1) * P], ident[:, :])
                mm.then_inc(ot_done, 1)

            def step(b, p, qk_on, front, back):
                if back:
                    turn_max(b, 1)
                if front:
                    v_product(b + 1, 1 - p, not back)
                for u in range(NU):
                    if back:
                        s2(b, p, u)
                        if u % 2 == 1 and u > 1:
                            pv(b, p, (u - 3) // 2)
                        if u % 8 == 5 and u > 8:
                            turn_o(b, u // 8 - 1)
                    if qk_on and u in (2, 3):
                        qk_product(b + 2, p, u - 2, back, front)
                    if front:
                        for n in s1_range(u):
                            if n == MT_AT:
                                turn_max(b + 1, 0)
                            s1(b + 1, 1 - p, n, qk_on)
                if back:
                    pv(b, p, NE - 1)
                    turn_o(b, NG - 1)

            step(-2, 0, True, False, False)
            step(-1, 1, True, True, False)
            with pe.Fori(0, (NB - 2) // 2) as i:
                step(2 * i, 0, True, True, True)
                step(2 * i + 1, 1, True, True, True)
            step(NB - 2, 0, False, True, True)
            step(NB - 1, 1, False, False, True)

        @block.vector
        def _(dve):
            dve.sem_inc(max_in, MAX_C)
            dve.sem_inc(att_done, ATT_C)

            for i in range(2):
                nc.vector.memset(va[i][:, :, :, HD + 1:CT], 0.0).then_inc(cleared, 1)
                nc.vector.memset(va[i][:, :, :, HD:HD + 1], 1.0).then_inc(cleared, 1)

            def reduce_max(b, n):
                dve.wait_ge(s1_done, S1_N * b + n + 1)
                nc.vector.tensor_reduce(nmax[:, n // NT, n % NT:n % NT + 1], ps_f[:, n % 2, :], AX.X, ALU.max,
                                        negate=True).then_inc(max_done, 1)

            def split_max(b, half_no):
                k = 2 * b + half_no
                src = ps_f[0:HH * NT, 0, 0:P]
                dve.wait_ge(max_in, MAX_C * k + MAX_C)
                dve.wait_ge(mt_done, k + 1)
                nc.vector.tensor_copy(mparts[:, 0, :], src).then_inc(mt_chain, 1)
                dve.wait_ge(mt_chain, 2 * k + 1)
                nc.vector.tensor_tensor(mrest[:, :], src, mparts[:, 0, :], ALU.subtract).then_inc(mt_split, 1)
                dve.wait_ge(mt_split, k + 1)
                nc.vector.tensor_copy(mparts[:, 1, :], mrest[:, :]).then_inc(mt_chain, 1)
                dve.wait_ge(mt_chain, 2 * k + 2)
                nc.vector.tensor_tensor(mparts[:, 2, :], mrest[:, :], mparts[:, 1, :],
                                        ALU.subtract).then_inc(mt_parts, 1)

            def divide(b, grp):
                o = ps_t[:, :, :].rearrange("p k (j c) -> p k j c", c=CT)
                dve.wait_ge(ot_done, NG * b + grp + 1 + OT_C)
                nc.vector.reciprocal(rec[:, :, :], o[:, :, :, HD]).then_inc(rec_done, 1)
                dve.wait_ge(rec_done, NG * b + grp + 1)
                dst = att[:, :, grp * HG * HD:(grp + 1) * HG * HD].rearrange("p k (j c) -> p k j c", c=HD)
                nc.vector.tensor_tensor(dst, o[:, :, :, 0:HD],
                                        rec[:, :, :].unsqueeze(3).broadcast_to([P, NT, HG, HD]),
                                        ALU.mult).then_inc(att_done, 1)

            def step(b, p, qk_on, front, back):
                if back:
                    split_max(b, 1)
                for u in range(NU):
                    if back and u % 8 == 5 and u > 8:
                        divide(b, u // 8 - 1)
                    if front:
                        for n in s1_range(u):
                            if n == MT_AT:
                                split_max(b + 1, 0)
                            reduce_max(b + 1, n)
                if back:
                    divide(b, NG - 1)
                    dve.wait_ge(att_done, NG * (b + 1) + ATT_C)
                    nc.vector.tensor_tensor(att[:, :, :], att[:, :, :], X[:, b, :, :], ALU.add).then_inc(sum_done, 1)
                    dve.wait_ge(sum_done, b + 1)
                    layernorm_dve(nc, dve, g, ln, b, att)

            step(-1, 1, True, True, False)
            dve.wait_ge(x_in, 16)
            with dve.Fori(0, (NB - 2) // 2) as i:
                step(2 * i, 0, True, True, True)
                step(2 * i + 1, 1, True, True, True)
            step(NB - 2, 0, False, True, True)
            step(NB - 1, 1, False, False, True)

        @block.gpsimd
        def _(pool):
            pool.sem_inc(parts_done, PARTS_C)
            pool.sem_inc(parts_out, OUT_C)

            def split_qk(b, n):
                k = 2 * b + n
                zero = g["zero"][:, :].broadcast_to([P, T])
                pool.wait_ge(parts_out, OUT_C * b + OUT_C)
                pool.wait_ge((q_taken, k_taken)[n], b + 1)
                nc.gpsimd.tensor_tensor(parts[:, n, 0, :], qk[:, n, :], zero, ALU.add).then_inc(split, 1)
                pool.wait_ge(split, 3 * k + 1)
                nc.gpsimd.tensor_tensor(rest[:, n, :], qk[:, n, :], parts[:, n, 0, :],
                                        ALU.subtract).then_inc(split, 1)
                pool.wait_ge(split, 3 * k + 2)
                nc.gpsimd.tensor_tensor(parts[:, n, 1, :], rest[:, n, :], zero, ALU.add).then_inc(split, 1)
                pool.wait_ge(split, 3 * k + 3)
                nc.gpsimd.tensor_tensor(parts[:, n, 2, :], rest[:, n, :], parts[:, n, 1, :],
                                        ALU.subtract).then_inc(parts_done, 1)

            def step(b, qk_on, back):
                if qk_on:
                    split_qk(b + 2, 0)
                    split_qk(b + 2, 1)
                if back:
                    layernorm_pool(nc, pool, g, ln, b)

            step(-2, True, False)
            step(-1, True, False)
            with pool.Fori(0, (NB - 2) // 2) as i:
                step(2 * i, True, True)
                step(2 * i + 1, True, True)
            step(NB - 2, False, True)
            step(NB - 1, False, True)


def attention1(nc, g, w_all, b_qk, v_b, o_b, qn, kn, cos_t, sin_t):
    X, ident = g["X"], g["ident"]
    scratch = [[nc.dram_tensor(f"parts1_{n}{i}", [5, P, T], BF16).ap() for i in range(2)] for n in "qk"]
    with ExitStack() as ctx:
        def sb(name, shape, dt=F32):
            return ctx.enter_context(nc.sbuf_tensor("a1_" + name, shape, dt))

        def sem(name):
            return ctx.enter_context(nc.semaphore("a1_" + name))

        w = sb("w", [P, 6, P])
        bqk = sb("bqk", [P, 4])
        norm_scale = sb("norm_scale", [P, 2])
        vb = sb("vb", [P, P])
        ob = sb("ob", [P, P])
        cos = sb("cos", [P, T])
        sin = sb("sin", [P, T])
        xb = sb("xb", [P, NT, P])
        sq = sb("sq", [P, NT, P])
        xr = sb("xr", [P, NT, P])
        ms = sb("ms", [P, NT])
        rr = sb("rr", [P, NT])
        xrt = sb("xrt", [P, T])
        turned = sb("turned", [P, 2, T])
        att_t = sb("att_t", [P, T])
        xt = [sb(f"xt{i}", [P, T]) for i in range(2)]
        qk = sb("qk", [P, 2, T])
        rest = sb("rest", [P, 2, T])
        parts = sb("parts", [P, 2, PARTS, T], BF16)
        qs = [sb(f"qs{i}", [P, H, T], BF16) for i in range(2)]
        ks = [sb(f"ks{i}", [P, H, T], BF16) for i in range(2)]
        va = [sb(f"va{i}", [P, NT, H, CT]) for i in range(2)]
        prob = sb("prob", [P, PSLOTS, UN, T])
        osb = sb("osb", [P, 2, T])
        rec = sb("rec", [P, NT, HG])
        att = sb("att", [P, NT, P])
        ln = layernorm_buffers(ctx, nc, "a1")
        ps_s = ctx.enter_context(nc.psum_tensor("a1_ps_s", [P, 2, UN, T], F32))
        ps_f = ctx.enter_context(nc.psum_tensor("a1_ps_f", [P, 2, T], F32))
        ps_o = ctx.enter_context(nc.psum_tensor("a1_ps_o", [P, T], F32))
        ps_t = ctx.enter_context(nc.psum_tensor("a1_ps_t", [P, NT, P], F32))

        w_in, w_scaled, cleared = sem("w_in"), sem("w_scaled"), sem("cleared")
        x_step, x_pow, xr_done = sem("x_step"), sem("x_pow"), sem("xr_done")
        f_done, f_taken, rope_step, rope_done = sem("f_done"), sem("f_taken"), sem("rope_step"), sem("rope_done")
        v_done, v_taken, split, parts_done = sem("v_done"), sem("v_taken"), sem("split"), sem("parts_done")
        parts_out, stack_in = sem("parts_out"), [sem(f"stack_in{i}") for i in range(2)]
        at_done, at_taken, y_done, y_taken = sem("at_done"), sem("at_taken"), sem("y_done"), sem("y_taken")
        s2_done, exp_done, pv_done = sem("s2_done"), sem("exp_done"), sem("pv_done")
        o_taken, ot_done, rec_done, att_done, sum_done = (
            sem(n) for n in ("o_taken", "ot_done", "rec_done", "att_done", "sum_done"))
        S2_C, EXP_C, PV_C, O_C, OT_C, ATT_C = NU, 2, PSLOTS // 2, 1, 2, 1
        FILL = 2 * 16
        PARTS_C, OUT_C = 2, 3 * 16
        FN = 6
        Y_C, R_C = 1, 1

        block = ctx.enter_context(nc.Block())

        @block.sync
        def _(sp):
            for dst, src in ((w[:, :, :], w_all), (bqk[:, :], b_qk), (norm_scale[:, 0:1], qn), (norm_scale[:, 1:2], kn),
                             (vb[:, :], bass.AP(tensor=v_b.tensor, offset=0, ap=[[0, P], [1, P]])),
                             (ob[:, :], bass.AP(tensor=o_b.tensor, offset=0, ap=[[0, P], [1, P]])),
                             (cos[:, :], cos_t), (sin[:, :], sin_t)):
                sp.dma_start(dst, src).then_inc(w_in, 16)

            def parts_to_dram(b, p):
                for n, seg in ((0, 0), (1, 0), (1, 1)):
                    if seg == 0:
                        sp.wait_ge(parts_done, 2 * b + n + 1 + PARTS_C)
                    dst = scratch[n][p].rearrange("r p t -> p r t")
                    if seg == 0:
                        sp.dma_start(dst[:, 0:PARTS, :], parts[:, n, :, :]).then_inc(parts_out, 16)
                    else:
                        sp.dma_start(dst[:, PARTS:5, :], parts[:, n, 0:2, :]).then_inc(parts_out, 16)

            def stack(b, p):
                sp.wait_ge(parts_out, 48 * (b + 1) + OUT_C)
                for n, dst in ((0, qs), (1, ks)):
                    src = scratch[n][p]
                    rows = PARTS * HD
                    src = bass.AP(tensor=src.tensor, offset=0,
                                  ap=[[n * HD * H * T, PARTS], [H * T, rows], [1, H * T]])
                    sp.dma_start(dst[p][0:QKR, :, :], src).then_inc(stack_in[p], 16)

            def step(b, p, qk_on, front):
                if front:
                    sp.wait_ge(s2_done, NU * b + S2_C)
                    stack(b + 1, 1 - p)
                if qk_on:
                    parts_to_dram(b + 2, p)

            for i in range(2):
                for dst in (qs, ks):
                    src = bass.AP(tensor=g["fill"].tensor, offset=0, ap=[[0, QKP - QKR], [1, H * T]])
                    sp.dma_start(dst[i][QKR:QKP, :, :], src).then_inc(stack_in[i], 16)
            parts_to_dram(0, 0)
            stack(0, 0)
            parts_to_dram(1, 1)
            with sp.Fori(0, (NB - 2) // 2) as i:
                step(2 * i, 0, True, True)
                step(2 * i + 1, 1, True, True)
            step(NB - 2, 0, False, True)

        @block.scalar
        def _(act):
            def take(dst, src, ready, value, done):
                act.wait_ge(ready, value)
                nc.scalar.activation(dst, src, ACT.Copy).then_inc(done, 1)

            def take_o(b, grp):
                act.wait_ge(ot_done, NG * b + grp - 1 + OT_C)
                take(osb[:, grp % 2, :], ps_o[:, :], pv_done, NE * b + NT * (grp + 1) + PV_C, o_taken)

            def step(b):
                for u in range(NU):
                    act.wait_ge(s2_done, NU * b + u + 1 + S2_C)
                    if u % 2 == 0:
                        act.wait_ge(pv_done, NE * b + u // 2 - PSLOTS // 2 + 1 + PV_C)
                    nc.scalar.activation(prob[:, u % PSLOTS, :, :], ps_s[:, u % 2, :, :], ACT.Sigmoid,
                                         scale=float(HD) ** -0.5).then_inc(exp_done, 1)
                    if u % 8 == 1 and u > 8:
                        take_o(b, u // 8 - 1)
                take_o(b, NG - 1)

            act.sem_inc(exp_done, EXP_C)
            act.sem_inc(o_taken, O_C)
            with act.Fori(0, NB) as b:
                step(b)

        @block.tensor
        def _(pe):
            pe.sem_inc(s2_done, S2_C)
            pe.sem_inc(pv_done, PV_C)
            pe.sem_inc(ot_done, OT_C)
            pe.wait_ge(w_scaled, 2)

            def v_product(b, p):
                pe.wait_ge(f_taken, FN * (b + 1))
                for kt in range(NT):
                    mm = nc.tensor.matmul(ps_f[:, 1, kt * P:(kt + 1) * P], xt[p][:, kt * P:(kt + 1) * P],
                                          w[:, 4, :], start=True, stop=True)
                mm.then_inc(v_done, 1)

            def front_use(b, p, k, v_too):
                if k == 0:
                    pe.wait_ge(x_step, 4 * b + 1)
                elif k == 1:
                    pe.wait_ge(xr_done, b + 1)
                    if v_too:
                        pe.wait_ge(v_taken, b)
                if k >= 2:
                    pe.wait_ge(f_taken, FN * b + max(k - 1, 2))
                if k < 2:
                    src = (xb, xr)[k]
                    for kt in range(NT):
                        mm = nc.tensor.transpose(ps_f[:, k, kt * P:(kt + 1) * P], src[:, kt, :], g["ident"][:, :])
                else:
                    mm = nc.tensor.matmul(ps_f[:, k % 2, :], w[:, k - 2, :], xrt[:, :], start=True, stop=True)
                mm.then_inc(f_done, 1)

            def s2(b, p, u):
                grp, kt, pair = u // (2 * NT), u // 2 % NT, u % 2
                if u == 0:
                    pe.wait_ge(stack_in[p], 16 * (b - p) + 32 + FILL)
                pe.wait_ge(exp_done, NU * b + u - 1 + EXP_C)
                for i in range(UN):
                    h = grp * HG + pair * UN + i
                    mm = nc.tensor.matmul(ps_s[:, u % 2, i, :], ks[p][0:QKP, h, kt * P:(kt + 1) * P],
                                          qs[p][0:QKP, h, :], start=True, stop=True)
                mm.then_inc(s2_done, 1)

            def pv(b, p, e):
                grp, kt = e // NT, e % NT
                if e == 0:
                    pe.wait_ge(v_taken, b + 1)
                if kt == 0:
                    pe.wait_ge(o_taken, NG * b + grp + O_C)
                pe.wait_ge(exp_done, NU * b + 2 * e + 2 + EXP_C)
                for j in range(HG):
                    mm = nc.tensor.matmul(ps_o[j * CT:(j + 1) * CT, :], va[p][:, kt, grp * HG + j, :],
                                          prob[:, (2 * e + j // UN) % PSLOTS, j % UN, :],
                                          start=(kt == 0), stop=(kt == NT - 1))
                mm.then_inc(pv_done, 1)

            def turn_o(b, grp):
                pe.wait_ge(o_taken, NG * b + grp + 1 + O_C)
                if grp == 0:
                    pe.wait_ge(y_taken, b + Y_C)
                else:
                    pe.wait_ge(att_done, NG * b + grp + ATT_C)
                for qt in range(NT):
                    mm = nc.tensor.transpose(ps_t[:, qt, :], osb[:, grp % 2, qt * P:(qt + 1) * P], ident[:, :])
                mm.then_inc(ot_done, 1)

            def project(b):
                pe.wait_ge(att_done, NG * (b + 1) + ATT_C)
                for kt in range(NT):
                    mm = nc.tensor.transpose(ps_t[:, kt, :], att[:, kt, :], ident[:, :])
                mm.then_inc(at_done, 1)
                pe.wait_ge(at_taken, b + 1)
                for kt in range(NT):
                    mm = nc.tensor.matmul(ps_t[:, kt, :], att_t[:, kt * P:(kt + 1) * P], w[:, 5, :],
                                          start=True, stop=True)
                mm.then_inc(y_done, 1)

            def step(b, p, qk_on, front, back):
                if front:
                    v_product(b + 1, 1 - p)
                for u in range(NU):
                    if back:
                        s2(b, p, u)
                        if u % 2 == 1 and u > 1:
                            pv(b, p, (u - 3) // 2)
                        if u % 8 == 5 and u > 8:
                            turn_o(b, u // 8 - 1)
                    if qk_on and u % 3 == 2 and u < 3 * FN:
                        front_use(b + 2, p, u // 3, front)
                if back:
                    pv(b, p, NE - 1)
                    turn_o(b, NG - 1)
                    project(b)

            step(-2, 0, True, False, False)
            step(-1, 1, True, True, False)
            with pe.Fori(0, (NB - 2) // 2) as i:
                step(2 * i, 0, True, True, True)
                step(2 * i + 1, 1, True, True, True)
            step(NB - 2, 0, False, True, True)
            step(NB - 1, 1, False, False, True)

        @block.vector
        def _(dve):
            dve.sem_inc(y_taken, Y_C)
            dve.sem_inc(rope_done, R_C)
            dve.sem_inc(att_done, ATT_C)

            for i in range(2):
                nc.vector.memset(va[i][:, :, :, HD + 1:CT], 0.0).then_inc(cleared, 1)
                nc.vector.memset(va[i][:, :, :, HD:HD + 1], 1.0).then_inc(cleared, 1)

            dve.wait_ge(w_in, 8 * 16)
            for n in range(2):
                nc.vector.tensor_scalar(w[:, 2 * n:2 * n + 2, :], w[:, 2 * n:2 * n + 2, :], norm_scale[:, n:n + 1],
                                        None, ALU.mult).then_inc(w_scaled, 1)

            def rms(b):
                c = 4 * b
                nc.vector.tensor_copy(xb[:, :, :], X[:, b, :, :]).then_inc(x_step, 1)
                dve.wait_ge(x_step, c + 1)
                nc.vector.tensor_tensor(sq[:, :, :], xb[:, :, :], xb[:, :, :], ALU.mult).then_inc(x_step, 1)
                dve.wait_ge(x_step, c + 2)
                nc.vector.tensor_reduce(ms[:, :], sq[:, :, :], AX.X, ALU.add).then_inc(x_step, 1)
                dve.wait_ge(x_step, c + 3)
                nc.vector.tensor_scalar(ms[:, :], ms[:, :], 1.0 / P, RMS_EPS, ALU.mult, ALU.add).then_inc(x_step, 1)

            def scale_x(b):
                dve.wait_ge(x_pow, b + 1)
                nc.vector.tensor_tensor(xr[:, :, :], xb[:, :, :],
                                        rr[:, :].unsqueeze(2).broadcast_to([P, NT, P]), ALU.mult).then_inc(xr_done, 1)

            def take_front(b, p, k):
                dve.wait_ge(f_done, FN * b + k + 1)
                if k < 2:
                    nc.vector.tensor_copy((xt[p], xrt)[k][:, :], ps_f[:, k, :]).then_inc(f_taken, 1)
                    return
                n = (k - 2) // 2
                if k % 2 == 0:
                    dve.wait_ge(parts_done, 2 * b + n - 1 + PARTS_C)
                    dve.wait_ge(rope_done, 2 * b + n + R_C)
                nc.vector.scalar_tensor_tensor(turned[:, k % 2, :], ps_f[:, k % 2, :], bqk[:, k - 2:k - 1],
                                               (cos, sin)[k % 2][:, :], ALU.add, ALU.mult).then_inc(f_taken, 1)
                if k % 2:
                    dve.wait_ge(f_taken, FN * b + k + 1)
                    nc.vector.tensor_tensor(qk[:, n, :], turned[:, 0, :], turned[:, 1, :],
                                            ALU.add).then_inc(rope_done, 1)

            def take_v(b, p):
                dve.wait_ge(v_done, b + 1)
                nc.vector.tensor_tensor(va[p][:, :, :, 0:HD],
                                        ps_f[:, 1, :].rearrange("p (k h d) -> p k h d", k=NT, h=H),
                                        vb[:, :].rearrange("p (h d) -> p h d", h=H).unsqueeze(1).broadcast_to(
                                            [P, NT, H, HD]), ALU.add).then_inc(v_taken, 1)

            def divide(b, grp):
                o = ps_t[:, :, :].rearrange("p k (j c) -> p k j c", c=CT)
                dve.wait_ge(ot_done, NG * b + grp + 1 + OT_C)
                nc.vector.tensor_scalar_add(rec[:, :, :], o[:, :, :, HD], RENORM_EPS).then_inc(rec_done, 1)
                dve.wait_ge(rec_done, 2 * (NG * b + grp) + 1)
                nc.vector.reciprocal(rec[:, :, :], rec[:, :, :]).then_inc(rec_done, 1)
                dve.wait_ge(rec_done, 2 * (NG * b + grp) + 2)
                dst = att[:, :, grp * HG * HD:(grp + 1) * HG * HD].rearrange("p k (j c) -> p k j c", c=HD)
                nc.vector.tensor_tensor(dst, o[:, :, :, 0:HD],
                                        rec[:, :, :].unsqueeze(3).broadcast_to([P, NT, HG, HD]),
                                        ALU.mult).then_inc(att_done, 1)

            def finish(b):
                dve.wait_ge(at_done, b + 1)
                nc.vector.tensor_copy(att_t[:, :], ps_t[:, :, :]).then_inc(at_taken, 1)
                dve.wait_ge(y_done, b + 1)
                nc.vector.tensor_tensor(att[:, :, :], ps_t[:, :, :],
                                        ob[:, :].unsqueeze(1).broadcast_to([P, NT, P]), ALU.add).then_inc(y_taken, 1)
                dve.wait_ge(y_taken, b + 1 + Y_C)
                nc.vector.tensor_tensor(att[:, :, :], att[:, :, :], X[:, b, :, :], ALU.add).then_inc(sum_done, 1)
                dve.wait_ge(sum_done, b + 1)
                layernorm_dve(nc, dve, g, ln, b, att)

            def step(b, p, qk_on, front, back):
                if qk_on:
                    rms(b + 2)
                if front:
                    take_v(b + 1, 1 - p)
                if qk_on:
                    scale_x(b + 2)
                for u in range(NU):
                    if back and u % 8 == 5 and u > 8:
                        divide(b, u // 8 - 1)
                    if qk_on and u % 3 == 2 and u < 3 * FN:
                        take_front(b + 2, p, u // 3)
                if back:
                    divide(b, NG - 1)
                    finish(b)

            step(-2, 0, True, False, False)
            step(-1, 1, True, True, False)
            with dve.Fori(0, (NB - 2) // 2) as i:
                step(2 * i, 0, True, True, True)
                step(2 * i + 1, 1, True, True, True)
            step(NB - 2, 0, False, True, True)
            step(NB - 1, 1, False, False, True)

        @block.gpsimd
        def _(pool):
            pool.sem_inc(parts_done, PARTS_C)
            pool.sem_inc(parts_out, OUT_C)

            def split_qk(b, n):
                k = 2 * b + n
                zero = g["zero"][:, :].broadcast_to([P, T])
                pool.wait_ge(parts_out, OUT_C * b + OUT_C)
                pool.wait_ge(rope_done, 2 * b + n + 1 + R_C)
                nc.gpsimd.tensor_tensor(parts[:, n, 0, :], qk[:, n, :], zero, ALU.add).then_inc(split, 1)
                pool.wait_ge(split, 3 * k + 1)
                nc.gpsimd.tensor_tensor(rest[:, n, :], qk[:, n, :], parts[:, n, 0, :],
                                        ALU.subtract).then_inc(split, 1)
                pool.wait_ge(split, 3 * k + 2)
                nc.gpsimd.tensor_tensor(parts[:, n, 1, :], rest[:, n, :], zero, ALU.add).then_inc(split, 1)
                pool.wait_ge(split, 3 * k + 3)
                nc.gpsimd.tensor_tensor(parts[:, n, 2, :], rest[:, n, :], parts[:, n, 1, :],
                                        ALU.subtract).then_inc(parts_done, 1)

            def step(b, qk_on, back):
                if qk_on:
                    pool.wait_ge(x_step, 4 * (b + 3))
                    nc.gpsimd.tensor_tensor(rr[:, :], ms[:, :], g["neg_half"][:, :], ALU.pow).then_inc(x_pow, 1)
                    split_qk(b + 2, 0)
                    split_qk(b + 2, 1)
                if back:
                    layernorm_pool(nc, pool, g, ln, b)

            step(-2, True, False)
            step(-1, True, False)
            with pool.Fori(0, (NB - 2) // 2) as i:
                step(2 * i, True, True)
                step(2 * i + 1, True, True)
            step(NB - 2, False, True)
            step(NB - 1, False, True)


def shared(ctx, nc, x, ident_in, fill):
    def sb(name, shape):
        return ctx.enter_context(nc.sbuf_tensor("g_" + name, shape, F32))

    def sem(name):
        return ctx.enter_context(nc.semaphore(name))

    return {"X": sb("X", [P, NB, NT, P]), "ident": sb("ident", [P, P]), "eps": sb("eps", [P, NT]),
            "neg_half": sb("neg_half", [P, NT]), "zero": sb("zero", [P, 1]), "x": x, "fill": fill, "ident_in": ident_in,
            "x_in": sem("x_in"), "consts_in": sem("consts_in"), "consts": sem("consts")}


def setup(nc, g):
    with nc.Block() as block:
        @block.sync
        def _(sp):
            sp.dma_start(g["ident"][:, :], g["ident_in"]).then_inc(g["consts_in"], 16)

        @block.gpsimd
        def _(pool):
            nc.gpsimd.memset(g["eps"][:, :], LN_EPS).then_inc(g["consts"], 1)
            nc.gpsimd.memset(g["neg_half"][:, :], -0.5).then_inc(g["consts"], 1)
            nc.gpsimd.memset(g["zero"][:, :], 0.0).then_inc(g["consts"], 1)
            pool.wait_ge(g["consts"], 3)


def turn_x(nc, g, ps, xt, name, ctx):
    X = g["X"]
    turned = ctx.enter_context(nc.semaphore(name + "_turned"))
    copied = ctx.enter_context(nc.semaphore(name + "_copied"))
    with nc.Block() as block:
        @block.tensor
        def _(pe):
            for b in range(NB):
                if b >= 2:
                    pe.wait_ge(copied, b - 1)
                for k in range(NT):
                    mm = nc.tensor.transpose(ps[:, b % 2, k * P:(k + 1) * P], X[:, b, k, :], g["ident"][:, :])
                mm.then_inc(turned, 1)

        @block.vector
        def _(dve):
            for b in range(NB):
                dve.wait_ge(turned, b + 1)
                nc.vector.tensor_copy(xt[:, b, :], ps[:, b % 2, :]).then_inc(copied, 1)


def route(nc, g, xt, ct, gate_t, bias):
    NTL = NB * NT
    with ExitStack() as ctx:
        def sb(name, shape, dt=F32):
            return ctx.enter_context(nc.sbuf_tensor("r_" + name, shape, dt))

        def sem(name):
            return ctx.enter_context(nc.semaphore("r_" + name))

        gate_sb = sb("gate", [P, E])
        bias_sb = sb("bias", [P, E])
        iota = sb("iota", [P, E])
        identb = sb("identb", [P, P], BF16)
        e1 = sb("e1", [P, NTL, E])
        score = sb("score", [P, NTL, E])
        sfc = sb("sfc", [P, NTL, E])
        gmax = sb("gmax", [P, NTL, NGRP])
        top = sb("top", [P, NTL, 8])
        topi = sb("topi", [P, NTL, 8], U32)
        topf = sb("topf", [P, NTL, 8])
        gmask = sb("gmask", [P, NTL, NGRP])
        hit = sb("hit", [P, NTL, TOPK, E])
        den = sb("den", [P, NTL])
        cpart = sb("cpart", [P, NTL, PARTS, E], BF16)
        ps_l = ctx.enter_context(nc.psum_tensor("r_ps_l", [P, NTL, E], F32))
        ps_c = ctx.enter_context(nc.psum_tensor("r_ps_c", [PARTS * E, 2, 2 * T], BF16))
        r_in, logits, exp_done, vec, c_turned, c_taken = (
            sem(n) for n in ("in", "logits", "exp_done", "vec", "c_turned", "c_taken"))

        with nc.Block() as block:
            @block.sync
            def _(sp):
                sp.dma_start(gate_sb[:, :], gate_t).then_inc(r_in, 16)
                sp.dma_start(bias_sb[:, :], bass.AP(tensor=bias.tensor, offset=0, ap=[[0, P], [1, E]])).then_inc(r_in, 16)
                sp.dma_start(iota[:, :], bass.AP(tensor=g["iota_in"].tensor, offset=0,
                                                 ap=[[0, P], [1, E]])).then_inc(r_in, 16)

            @block.tensor
            def _(pe):
                pe.wait_ge(r_in, 48)
                for k in range(NTL):
                    mm = nc.tensor.matmul(ps_l[:, k, :], xt[:, k // NT, k % NT * P:(k % NT + 1) * P],
                                          gate_sb[:, :], start=True, stop=True)
                mm.then_inc(logits, 1)
                pe.wait_ge(vec, STEPS)
                for b in range(NB):
                    if b >= 2:
                        pe.wait_ge(c_taken, b - 1)
                    for k in range(NT):
                        mm = nc.tensor.transpose(ps_c[:, b % 2, k * P:(k + 1) * P],
                                                 cpart[:, b * NT + k, :, :], identb[:, :])
                    mm.then_inc(c_turned, 1)

            @block.scalar
            def _(act):
                act.wait_ge(logits, 1)
                nc.scalar.activation(e1[:, :, :], ps_l[:, :, :], ACT.Exp, scale=-1.0).then_inc(exp_done, 1)

            count = [0]

            @block.vector
            def _(dve):
                def link(ins):
                    count[0] += 1
                    ins.then_inc(vec, 1)
                    dve.wait_ge(vec, count[0])

                def pick(values, n):
                    for k in range(NTL):
                        ins = nc.vector.max(top[:, k, :], values[:, k, :])
                    link(ins)
                    for k in range(NTL):
                        ins = nc.vector.max_index(topi[:, k, :], top[:, k, :], values[:, k, :])
                    link(ins)
                    link(nc.vector.tensor_copy(topf[:, :, :], topi[:, :, :]))

                def mark(dst, n, width):
                    h = hit[:, :, 0:n, 0:width]
                    for q in range(0, NTL, 8):
                        for j in range(n):
                            ins = nc.vector.tensor_tensor(
                                h[:, q:q + 8, j, :], topf[:, q:q + 8, j:j + 1].broadcast_to([P, 8, width]),
                                iota[:, 0:width].unsqueeze(1).broadcast_to([P, 8, width]), ALU.is_equal)
                    link(ins)
                    link(nc.vector.tensor_reduce(dst, h.rearrange("p t k e -> p t e k"), AX.X, ALU.add))

                dve.wait_ge(r_in, 48)
                dve.wait_ge(g["consts_in"], 16)
                nc.vector.tensor_copy(identb[:, :], g["ident"][:, :])
                dve.wait_ge(exp_done, 1)
                link(nc.vector.tensor_scalar_add(e1[:, :, :], e1[:, :, :], 1.0))
                link(nc.vector.reciprocal(score[:, :, :], e1[:, :, :]))
                link(nc.vector.tensor_tensor(sfc[:, :, :], score[:, :, :],
                                             bias_sb[:, :].unsqueeze(1).broadcast_to([P, NTL, E]), ALU.add))
                link(nc.vector.tensor_reduce(gmax[:, :, :], sfc[:, :, :].rearrange("p t (g e) -> p t g e", g=NGRP),
                                             AX.X, ALU.max))
                pick(gmax, TOPG)
                mark(gmask[:, :, :], TOPG, NGRP)
                gs = E // NGRP
                link(nc.vector.tensor_tensor(
                    sfc[:, :, :].rearrange("p t (g e) -> p t g e", g=NGRP),
                    sfc[:, :, :].rearrange("p t (g e) -> p t g e", g=NGRP),
                    gmask[:, :, :].unsqueeze(3).broadcast_to([P, NTL, NGRP, gs]), ALU.mult))
                pick(sfc, TOPK)
                mark(e1[:, :, :], TOPK, E)
                link(nc.vector.tensor_tensor(score[:, :, :], score[:, :, :], e1[:, :, :], ALU.mult))
                link(nc.vector.tensor_reduce(den[:, :], score[:, :, :], AX.X, ALU.add))
                link(nc.vector.tensor_scalar_add(den[:, :], den[:, :], 1e-20))
                link(nc.vector.reciprocal(den[:, :], den[:, :]))
                link(nc.vector.tensor_scalar(den[:, :], den[:, :], ROUTE_SCALE, None, ALU.mult))
                link(nc.vector.tensor_tensor(score[:, :, :], score[:, :, :],
                                             den[:, :].unsqueeze(2).broadcast_to([P, NTL, E]), ALU.mult))
                link(nc.vector.tensor_copy(cpart[:, :, 0, :], score[:, :, :]))
                link(nc.vector.tensor_tensor(e1[:, :, :], score[:, :, :], cpart[:, :, 0, :], ALU.subtract))
                link(nc.vector.tensor_copy(cpart[:, :, 1, :], e1[:, :, :]))
                link(nc.vector.tensor_tensor(cpart[:, :, 2, :], e1[:, :, :], cpart[:, :, 1, :], ALU.subtract))
                assert count[0] == STEPS, count[0]
                for b in range(NB):
                    dve.wait_ge(c_turned, b + 1)
                    nc.vector.tensor_copy(ct[:, b, :], ps_c[:, b % 2, 0:T]).then_inc(c_taken, 1)


STEPS = 25


def feed_forward(nc, g, name, n_un, xt, wg, wu, wd, ct=None, sel=None, ready=None):
    with ExitStack() as ctx:
        def sb(n, shape, dt=F32):
            return ctx.enter_context(nc.sbuf_tensor(f"{name}_{n}", shape, dt))

        def sem(n):
            return ctx.enter_context(nc.semaphore(f"{name}_{n}"))

        X = g["X"]
        LAG = 2
        RH = 3
        n_c = n_un - 1 if ct is not None else 0
        gated = sb("gated", [P, 2, T])
        prod = sb("prod", [P, 2, T])
        hid = sb("hid", [P, RH, T])
        dsb = sb("dsb", [P, T])
        y = sb("y", [P, NT, P])
        ln = layernorm_buffers(ctx, nc, name)
        ps = ctx.enter_context(nc.psum_tensor(f"{name}_ps", [P, 8, T], F32))
        ps_g, ps_u, ps_c, ps_d, ps_t = ps[:, 0:2, :], ps[:, 2:4, :], ps[:, 4:6, :], ps[:, 6, :], ps[:, 7, :]
        g_done, u_done, c_done, silu_done, prod_done, hid_done, d_done, d_taken, t_done, t_taken = (
            sem(n) for n in ("g_done", "u_done", "c_done", "silu_done", "prod_done", "hid_done", "d_done",
                             "d_taken", "t_done", "t_taken"))
        C = 4

        def since(j, ring, limit=n_un):
            before = [j - q for q in range(j) if q % ring == j % ring and q < limit]
            last = [n_un + j - q for q in range(limit) if q % ring == j % ring]
            return min(before or last)

        block = ctx.enter_context(nc.Block())

        @block.tensor
        def _(pe):
            pe.sem_inc(d_done, C)

            def unit(b, j):
                rhs = xt[:, b, :]
                n = n_un * b + j
                pe.wait_ge(silu_done, n - since(j, 2) + 1 + C)
                nc.tensor.matmul(ps_g[:, j % 2, :], wg[:, j, :], rhs, start=True, stop=True).then_inc(g_done, 1)
                pe.wait_ge(prod_done, n - since(j, 2) + 1 + C)
                nc.tensor.matmul(ps_u[:, j % 2, :], wu[:, j, :], rhs, start=True, stop=True).then_inc(u_done, 1)
                if j < n_c:
                    pe.wait_ge(hid_done, n - since(j, 2, n_c) + 1 + C)
                    nc.tensor.matmul(ps_c[:, j % 2, :], sel[:, j, :], ct[:, b, :], start=True,
                                     stop=True).then_inc(c_done, 1)

            def down(b, j):
                n = n_un * b + j
                pe.wait_ge(hid_done, n + 1 + C)
                if j == 0:
                    pe.wait_ge(d_taken, b + C)
                nc.tensor.matmul(ps_d, wd[:, j, :], hid[:, j % RH, :], start=(j == 0),
                                 stop=(j == n_un - 1)).then_inc(d_done, 1)

            def turn(b):
                pe.wait_ge(d_taken, b + 1 + C)
                pe.wait_ge(t_taken, b + C)
                for q in range(NT):
                    mm = nc.tensor.transpose(ps_t[:, q * P:(q + 1) * P], dsb[:, q * P:(q + 1) * P], g["ident"][:, :])
                mm.then_inc(t_done, 1)

            if ready is not None:
                ready(pe)
            walk_ff(pe, n_un, LAG, unit, down, turn)

        @block.scalar
        def _(act):
            act.sem_inc(silu_done, C)
            act.sem_inc(d_taken, C)

            def unit(b, j):
                n = n_un * b + j
                act.wait_ge(g_done, n + 1)
                act.wait_ge(prod_done, n - since(j, 2) + 1 + C)
                nc.scalar.activation(gated[:, j % 2, :], ps_g[:, j % 2, :], ACT.Silu).then_inc(silu_done, 1)

            def turn(b):
                act.wait_ge(d_done, n_un * (b + 1) + C)
                nc.scalar.activation(dsb[:, :], ps_d, ACT.Copy).then_inc(d_taken, 1)

            walk_ff(act, n_un, LAG, unit, None, turn)

        @block.vector
        def _(dve):
            dve.sem_inc(prod_done, C)
            dve.sem_inc(hid_done, C)
            dve.sem_inc(t_taken, C)
            dve.sem_inc(ln["x_done"], 1)

            def unit(b, j):
                n = n_un * b + j
                dve.wait_ge(silu_done, n + 1 + C)
                dve.wait_ge(u_done, n + 1)
                dve.wait_ge(d_done, n - since(j, RH) + 1 + C)
                if j < n_c:
                    nc.vector.tensor_tensor(prod[:, j % 2, :], gated[:, j % 2, :], ps_u[:, j % 2, :],
                                            ALU.mult).then_inc(prod_done, 1)
                    dve.wait_ge(prod_done, n + 1 + C)
                    dve.wait_ge(c_done, n_c * b + j + 1)
                    nc.vector.tensor_tensor(hid[:, j % RH, :], prod[:, j % 2, :], ps_c[:, j % 2, :],
                                            ALU.mult).then_inc(hid_done, 1)
                else:
                    nc.vector.tensor_tensor(hid[:, j % RH, :], gated[:, j % 2, :], ps_u[:, j % 2, :],
                                            ALU.mult).then_inc(prod_done, 1)
                    dve.wait_ge(prod_done, n + 1 + C)
                    nc.vector.memset(ln["gate"][:, :], 0.0).then_inc(hid_done, 1)

            def turn(b):
                dve.wait_ge(ln["x_done"], b + 1)
                dve.wait_ge(t_done, b + 1)
                nc.vector.tensor_tensor(y[:, :, :], ps_t.rearrange("p (k d) -> p k d", k=NT), X[:, b, :, :],
                                        ALU.add).then_inc(t_taken, 1)
                dve.wait_ge(t_taken, b + 1 + C)
                layernorm_dve(nc, dve, g, ln, b, y)

            walk_ff(dve, n_un, LAG, unit, None, turn)

        @block.gpsimd
        def _(pool):
            with pool.Fori(0, NB) as b:
                layernorm_pool(nc, pool, g, ln, b)


def walk_ff(eng, n_un, lag, unit, down, turn):
    def batch(b, before):
        for j in range(n_un):
            unit(b, j)
            if down is not None:
                if j >= lag:
                    down(b, j - lag)
                elif before:
                    down(b - 1, n_un - lag + j)
            if before and j == lag:
                turn(b - 1)

    batch(0, False)
    with eng.Fori(1, NB) as b:
        batch(b, True)
    if down is not None:
        for j in range(n_un - lag, n_un):
            down(NB - 1, j)
    turn(NB - 1)


def ffn_weights(nc, g, ints, floats, ctx):
    w_in = ctx.enter_context(nc.semaphore("i_in"))
    w_conv = ctx.enter_context(nc.semaphore("i_conv"))
    with nc.Block() as block:
        @block.sync
        def _(sp):
            for src, ib, _ in ints:
                sp.dma_start(ib[:, :, :], src).then_inc(w_in, 16)

        @block.vector
        def _(dve):
            dve.wait_ge(w_in, 16 * len(ints))
            for n, (_, ib, fb) in enumerate(ints):
                nc.vector.tensor_copy(fb[:, :, :], ib[:, :, :]).then_inc(w_conv, 1)
            dve.wait_ge(w_conv, len(ints))
            for n, (_, ib, fb) in enumerate(ints):
                nc.vector.tensor_scalar(fb[:, :, :], fb[:, :, :], WEIGHT_SCALE, None, ALU.mult).then_inc(w_conv, 1)
            dve.wait_ge(w_conv, 2 * len(ints))


def program(nc, ident, fill, iota, sel, x, x_t, w_qkv, gate_t, bias, wg, wu, wd, w1, b1, v_b, o_b, qn, kn, cos, sin,
            fg, fu, fd, out):
    with ExitStack() as ctx:
        g = shared(ctx, nc, x, ident, fill)
        g["iota_in"] = iota
        setup(nc, g)
        attention0(nc, g, x_t, w_qkv)
        with ExitStack() as part:
            def sb(name, shape, dt=F32):
                return part.enter_context(nc.sbuf_tensor(name, shape, dt))

            xt = sb("moe_xt", [P, NB, T])
            ct = sb("moe_ct", [PARTS * E, NB, T], BF16)
            with ExitStack() as ps_ctx:
                ps = ps_ctx.enter_context(nc.psum_tensor("turn_ps", [P, 2, T], F32))
                turn_x(nc, g, ps, xt, "moe", part)
            route(nc, g, xt, ct, gate_t, bias)
            wg_sb, wu_sb, wd_sb = (sb(n, [P, FF, P]) for n in ("moe_wg", "moe_wu", "moe_wd"))
            sel_sb = sb("moe_sel", [PARTS * E, NPAIR, P], BF16)
            moe_in = part.enter_context(nc.semaphore("moe_in"))
            with nc.Block() as block:
                @block.sync
                def _(sp):
                    for dst, src in ((wg_sb, wg), (wu_sb, wu), (wd_sb, wd), (sel_sb, sel)):
                        sp.dma_start(dst[:, :, :], src).then_inc(moe_in, 16)
            feed_forward(nc, g, "moe", FF, xt, wg_sb, wu_sb, wd_sb, ct, sel_sb,
                         lambda pe: pe.wait_ge(moe_in, 4 * 16))
        attention1(nc, g, w1, b1, v_b, o_b, qn, kn, cos, sin)
        with ExitStack() as part:
            def sb(name, shape, dt=F32):
                return part.enter_context(nc.sbuf_tensor(name, shape, dt))

            xt = sb("ff_xt", [P, NB, T])
            ints, floats = [], []
            for n, src in (("g", fg), ("u", fu), ("d", fd)):
                ints.append((src, sb("ff_i" + n, [P, NH3, P], I32), sb("ff_w" + n, [P, NH3, P])))
            ffn_weights(nc, g, ints, floats, part)
            with ExitStack() as ps_ctx:
                ps = ps_ctx.enter_context(nc.psum_tensor("turn2_ps", [P, 2, T], F32))
                turn_x(nc, g, ps, xt, "ff", part)
            feed_forward(nc, g, "ff", NH3, xt, ints[0][2], ints[1][2], ints[2][2])
        x_out = ctx.enter_context(nc.semaphore("x_out"))
        with nc.Block() as block:
            @block.sync
            def _(sp):
                sp.dma_start(out.rearrange("b (k p) d -> p b k d", p=P), g["X"][:, :, :, :]).then_inc(x_out, 16)
                sp.wait_ge(x_out, 16)


def layouts(i):
    import numpy as np
    r = {}
    r["ident"] = np.eye(P, dtype=np.float32)
    r["fill"] = np.stack([np.zeros(H * T), np.ones(H * T)]).astype("bfloat16")
    r["iota"] = np.arange(E, dtype=np.float32)
    sel = np.zeros((PARTS, E, NPAIR, P), np.float32)
    for j in range(NPAIR):
        sel[:, 2 * j, j, :EI] = 1
        sel[:, 2 * j + 1, j, EI:] = 1
    r["sel"] = sel.reshape(PARTS * E, NPAIR, P).astype("bfloat16")
    x = np.asarray(i["L0_attn_x"])
    r["x"] = x
    r["x_t"] = np.ascontiguousarray(x.reshape(NB * T, P).T)
    dims, heads = np.divmod(np.arange(P), H)
    order = heads * HD + dims
    turned = heads * HD + (dims ^ 1)
    w = np.asarray(i["L0_attn_W_qkv"])
    r["w_qkv"] = np.ascontiguousarray(np.concatenate([w[:, :P][:, order], w[:, P:2 * P][:, order], w[:, 2 * P:]], 1))
    r["gate_t"] = np.ascontiguousarray(np.asarray(i["L0_ffn_gate_weight"]).T)
    r["bias"] = np.asarray(i["L0_ffn_e_score_correction_bias"])
    gu = np.asarray(i["L0_ffn_experts_gate_up"])
    for n, (a, shared_w) in {"wg": (gu[:, :EI], i["L0_ffn_shared_gate_w"]),
                             "wu": (gu[:, EI:], i["L0_ffn_shared_up_w"])}.items():
        rows = np.concatenate([a.reshape(E * EI, P), np.asarray(shared_w)], 0)
        r[n] = np.ascontiguousarray(rows.T.reshape(P, FF, P))
    down = np.asarray(i["L0_ffn_experts_down"]).transpose(0, 2, 1).reshape(E * EI, P)
    down = np.concatenate([down, np.asarray(i["L0_ffn_shared_down_w"]).T], 0)
    r["wd"] = np.ascontiguousarray(down.reshape(FF, P, P).transpose(1, 0, 2))
    q, k, v, o = (np.asarray(i[f"L1_attn_{n}_w"]).T for n in "qkvo")
    r["w1"] = np.ascontiguousarray(np.stack([q[:, order], q[:, turned], k[:, order], k[:, turned], v, o], 1))
    qb, kb = np.asarray(i["L1_attn_q_b"]), np.asarray(i["L1_attn_k_b"])
    r["b1"] = np.ascontiguousarray(np.stack([qb[order], qb[turned], kb[order], kb[turned]], 1))
    r["v_b"], r["o_b"] = np.asarray(i["L1_attn_v_b"]), np.asarray(i["L1_attn_o_b"])
    r["qn"] = np.asarray(i["L1_attn_qn_scale"]).reshape(P, 1)
    r["kn"] = np.asarray(i["L1_attn_kn_scale"]).reshape(P, 1)
    inv = (1.0 / np.float32(10000.0) ** (np.arange(0, HD, 2, dtype=np.float32) / np.float32(HD))).astype(np.float32)
    freq = inv[dims % (HD // 2)][:, None] * np.arange(T, dtype=np.float32)[None, :]
    r["cos"] = np.cos(freq).astype(np.float32)
    r["sin"] = (np.sin(freq) * np.where(dims % 2, 1, -1)[:, None]).astype(np.float32)
    for n, a in (("fg", "gate"), ("fu", "up")):
        r[n] = np.ascontiguousarray(np.asarray(i["L1_ffn_w_" + a]).T.reshape(P, NH3, P))
    r["fd"] = np.ascontiguousarray(np.asarray(i["L1_ffn_w_down"]).T.reshape(NH3, P, P).transpose(1, 0, 2))
    return r


def kernel(**inputs):
    import concourse.bacc as _bacc
    from concourse import mybir as _mybir
    from concourse.bass_utils import run_bass_kernel_spmd as _run

    nc = _bacc.Bacc("TRN2", target_bir_lowering=False, num_devices=1)
    arrays, args = {}, []
    for name, a in layouts(inputs).items():
        arrays[f"in_{name}"] = a
        args.append(nc.dram_tensor(f"in_{name}", a.shape, _mybir.dt.from_np(a.dtype), kind="ExternalInput").ap())
    out = nc.dram_tensor("out_x", (NB, T, P), F32, kind="ExternalOutput").ap()
    program(nc, *args, out)
    r = _run(nc, [arrays], core_ids=[0])
    return r.results[0]["out_x"]
```

```python
from contextlib import ExitStack

import concourse.bass as bass
from concourse import mybir

F32 = mybir.dt.float32
BF16 = mybir.dt.bfloat16
U32 = mybir.dt.uint32
I32 = mybir.dt.int32
ALU = mybir.AluOpType
ACT = mybir.ActivationFunctionType
AX = mybir.AxisListType

P = 128
NB = 8
T = 512
NT = T // P
H = 16
HD = P // H
HG = 4
NG = H // HG
CT = P // HG
PARTS = 3
QKR = PARTS * PARTS * HD
QKP = 96
MXR = QKP + PARTS
UN = 2
NU = NG * NT * (HG // UN)
PSLOTS = 8
NE = NG * NT
E = 32
EI = 64
NPAIR = E // 2
FF = NPAIR + 1
TOPG, TOPK, NGRP = 4, 6, 8
ROUTE_SCALE = 2.5
HID = 384
NH3 = HID // P
LN_EPS = 1e-5
RMS_EPS = 1e-8
RENORM_EPS = 1e-8
WEIGHT_SCALE = 1.0 / 127.0
S1_N = H * NT
FB = 3
V_AT, Q_AT, K_AT = 17, 20, 23
MT_AT = (40, 5)
OT_AT = (26, 42, 58, 10)
SUM_AT, STATS_AT, NORM_AT = 11, 12, 15
LOOP_U = 8
HH = H // 2
GUEST_AT = {"v": V_AT, "q": Q_AT, "k": K_AT, "max0": MT_AT[0], "max1": MT_AT[1],
            "o0": OT_AT[0], "o1": OT_AT[1], "o2": OT_AT[2], "o3": OT_AT[3]}
TURNS = [t for n in range(S1_N) for t in [g for g, at in GUEST_AT.items() if at == n] + [n]]
BANK = {t: i % FB for i, t in enumerate(TURNS)}


def exists(turn, b):
    if not isinstance(b, int):
        return True
    first, last = {"q": (0, NB - 2), "k": (0, NB - 2), "v": (0, NB - 1), "max0": (0, NB - 1),
                   "o3": (2, NB)}.get(turn, (0, NB - 1) if isinstance(turn, int) else (1, NB))
    return first <= b <= last


def turn_before(turn, b):
    order = TURNS[:TURNS.index(turn)]
    for back in range(2):
        for t in reversed(order):
            if BANK[t] == BANK[turn] and exists(t, b - back):
                return t, back
        order = TURNS
    return None


def turns_of(u, second):
    return [t for n in s1_range(u, second) for t in TURNS if t == n or GUEST_AT.get(t) == n]


def s1_range(u, second):
    at = lambda k: -(-S1_N * k // (2 * NU))
    return range(at(2 * u + second), at(2 * u + second + 1))


def layernorm_buffers(ctx, nc, name):
    def sb(n, shape):
        return ctx.enter_context(nc.sbuf_tensor(f"{name}_{n}", shape, F32))

    def sem(n):
        return ctx.enter_context(nc.semaphore(f"{name}_{n}"))

    return {"st": sb("st", [P, NT, 6]), "mv": sb("mv", [P, NT, 2]), "ve": sb("ve", [P, NT]),
            "rstd": sb("rstd", [P, NT]), "gate": sb("gate", [P, 1]),
            "dve": sem("ln_dve"), "pool": sem("ln_pool"), "x_done": sem("x_done")}


def layernorm_dve(nc, dve, g, ln, b, y):
    layernorm_stats(nc, dve, ln, b, y)
    layernorm_apply(nc, dve, g, ln, b, y)


def layernorm_stats(nc, dve, ln, b, y):
    for k in range(NT):
        nc.vector.bn_stats(ln["st"][:, k, :], y[:, k, :]).then_inc(ln["dve"], 1)
    dve.wait_ge(ln["dve"], 2 * NT * b + NT)
    nc.vector.memset(ln["gate"][:, :], 0.0)
    for k in range(NT):
        nc.vector.bn_aggr(ln["mv"][:, k, :], ln["st"][:, k, :]).then_inc(ln["dve"], 1)


def layernorm_apply(nc, dve, g, ln, b, y):
    X = g["X"]
    dve.wait_ge(ln["pool"], 2 * b + 2)
    for k in range(NT):
        ins = nc.vector.tensor_scalar(X[:, b, k, :], y[:, k, :], ln["mv"][:, k, 0:1], ln["rstd"][:, k:k + 1],
                                      ALU.subtract, ALU.mult)
    ins.then_inc(ln["x_done"], 1)


def layernorm_pool(nc, pool, g, ln, b):
    pool.wait_ge(ln["dve"], 2 * NT * (b + 1))
    nc.gpsimd.tensor_tensor(ln["ve"][:, :], ln["mv"][:, :, 1], g["eps"][:, :], ALU.add).then_inc(ln["pool"], 1)
    pool.wait_ge(ln["pool"], 2 * b + 1)
    nc.gpsimd.tensor_tensor(ln["rstd"][:, :], ln["ve"][:, :], g["neg_half"][:, :], ALU.pow).then_inc(ln["pool"], 1)


def walk(eng, units):
    units(-1, 1, 0, NU, True, True, False, False)
    units(0, 0, 0, LOOP_U, False, True, True, False)
    with eng.Fori(0, (NB - 2) // 2) as i:
        for q in range(2):
            units(2 * i + q, q, LOOP_U, NU, True, True, True, False)
            units(2 * i + q + 1, 1 - q, 0, LOOP_U, False, True, True, True)
    units(NB - 2, 0, LOOP_U, NU, False, True, True, False)
    units(NB - 1, 1, 0, LOOP_U, False, False, True, True)
    units(NB - 1, 1, LOOP_U, NU, False, False, True, False)


def attention0(nc, g, x_t, w_qkv):
    X, ident = g["X"], g["ident"]
    scratch = [[nc.dram_tensor(f"parts_{n}{i}", [5, P, T], BF16).ap() for i in range(2)] for n in "qk"]
    with ExitStack() as ctx:
        def sb(name, shape, dt=F32):
            return ctx.enter_context(nc.sbuf_tensor("a0_" + name, shape, dt))

        def sem(name):
            return ctx.enter_context(nc.semaphore("a0_" + name))

        w = sb("w", [P, 3, P])
        xt = [sb(f"xt{i}", [P, T]) for i in range(2)]
        qk = sb("qk", [P, 2, T])
        rest = sb("rest", [P, 2, T])
        parts = sb("parts", [P, 2, PARTS, T], BF16)
        qs = [sb(f"qs{i}", [P, H, T], BF16) for i in range(2)]
        ks = [sb(f"ks{i}", [P, H, T], BF16) for i in range(2)]
        va = [sb(f"va{i}", [P, NT, H, CT]) for i in range(2)]
        prob = sb("prob", [P, PSLOTS, UN, T])
        osb = sb("osb", [P, 2, T])
        nmax = sb("nmax", [P, H, NT])
        mrest = sb("mrest", [HH * NT, P])
        mparts = sb("mparts", [HH * NT, PARTS, P], BF16)
        rec = sb("rec", [P, NT, HG])
        att = sb("att", [P, NT, P])
        ln = layernorm_buffers(ctx, nc, "a0")
        ps_s = ctx.enter_context(nc.psum_tensor("a0_ps_s", [P, 2, UN, T], F32))
        ps_f = ctx.enter_context(nc.psum_tensor("a0_ps_f", [P, FB, T], F32))
        ps_o = ctx.enter_context(nc.psum_tensor("a0_ps_o", [P, T], F32))

        w_in, x_in, xt_in = sem("w_in"), g["x_in"], [sem(f"xt_in{i}") for i in range(2)]
        cleared = sem("cleared")
        q_done, k_done, v_done = sem("q_done"), sem("k_done"), sem("v_done")
        q_taken, k_taken, v_taken = sem("q_taken"), sem("k_taken"), sem("v_taken")
        split, parts_done = sem("split"), sem("parts_done")
        parts_out, fill_in, max_in = sem("parts_out"), sem("fill_in"), sem("max_in")
        stack_in = [sem(f"stack_in{i}") for i in range(NG)]
        s1_done, max_done = sem("s1_done"), sem("max_done")
        mt_done, mt_chain, mt_split, mt_parts = (sem(f"mt_{n}") for n in ("done", "chain", "split", "parts"))
        s2_done, exp_done, pv_done = sem("s2_done"), sem("exp_done"), sem("pv_done")
        o_taken, ot_done, rec_done, att_done, sum_done = (
            sem(n) for n in ("o_taken", "ot_done", "rec_done", "att_done", "sum_done"))
        S2_C, EXP_C, PV_C, O_C, OT_C, ATT_C = NU, 2, PSLOTS // 2, 1, 2, 1
        PARTS_C, OUT_C, MAX_C = 2, 3 * 16, PARTS * 16

        block = ctx.enter_context(nc.Block())

        @block.sync
        def _(sp):
            sp.dma_start(w[:, :, :], w_qkv.rearrange("d (a c) -> d a c", a=3)).then_inc(w_in, 16)

            def load_xt(b, p):
                sp.dma_start(xt[p][:, :], x_t[:, bass.ds(b * T, T)]).then_inc(xt_in[p], 16)

            def parts_to_dram(b, p):
                for n, seg in ((0, 0), (1, 0), (1, 1)):
                    if seg == 0:
                        sp.wait_ge(parts_done, 2 * b + n + 1 + PARTS_C)
                    dst = scratch[n][p].rearrange("r p t -> p r t")
                    if seg == 0:
                        sp.dma_start(dst[:, 0:PARTS, :], parts[:, n, :, :]).then_inc(parts_out, 16)
                    else:
                        sp.dma_start(dst[:, PARTS:5, :], parts[:, n, 0:2, :]).then_inc(parts_out, 16)

            def stack(b, p, grp, before=False):
                if before:
                    sp.wait_ge(s2_done, NU * (b - 2) + (grp + 1) * (NU // NG) + S2_C)
                for n, dst in ((0, qs), (1, ks)):
                    src = scratch[n][p]
                    src = bass.AP(tensor=src.tensor, offset=grp * HG * T,
                                  ap=[[n * HD * H * T, PARTS], [H * T, PARTS * HD], [1, HG * T]])
                    sp.dma_start(dst[p][0:QKR, grp * HG:(grp + 1) * HG, :], src).then_inc(stack_in[grp], 16)

            def max_rows(b, p, half_no):
                sp.wait_ge(mt_parts, 2 * b + half_no + 1)
                for r in range(PARTS):
                    sp.dma_start(qs[p][QKP + r:QKP + r + 1, half_no * HH:(half_no + 1) * HH, :],
                                 mparts[:, r, :]).then_inc(max_in, 16)

            def step(b, p, qk_on, front, back):
                if back:
                    max_rows(b, p, 1)
                if front and back:
                    stack(b + 1, 1 - p, NG - 1, True)
                if qk_on:
                    sp.wait_ge(v_done, b + 1)
                    load_xt(b + 2, p)
                    parts_to_dram(b + 2, p)
                if front:
                    max_rows(b + 1, 1 - p, 0)
                if qk_on:
                    sp.wait_ge(parts_out, 48 * (b + 3) + OUT_C)
                    for grp in range(NG - 1):
                        stack(b + 2, p, grp, True)

            sp.dma_start(X[:, :, :, :], g["x"].rearrange("b (k p) d -> p b k d", p=P)).then_inc(x_in, 16)
            load_xt(0, 0)
            load_xt(1, 1)
            for i in range(2):
                for dst, value, r0, r1 in ((qs, 0, QKR, QKP), (ks, 0, QKR, QKP), (ks, 1, QKP, MXR)):
                    src = bass.AP(tensor=g["fill"].tensor, offset=value * H * T, ap=[[0, r1 - r0], [1, H * T]])
                    sp.dma_start(dst[i][r0:r1, :, :], src).then_inc(fill_in, 16)
            parts_to_dram(0, 0)
            sp.wait_ge(parts_out, 48 + OUT_C)
            for grp in range(NG):
                stack(0, 0, grp)
            parts_to_dram(1, 1)
            max_rows(0, 0, 0)
            sp.wait_ge(parts_out, 96 + OUT_C)
            for grp in range(NG - 1):
                stack(1, 1, grp)
            with sp.Fori(0, (NB - 2) // 2) as i:
                step(2 * i, 0, True, True, True)
                step(2 * i + 1, 1, True, True, True)
            step(NB - 2, 0, False, True, True)
            step(NB - 1, 1, False, False, True)

        @block.scalar
        def _(act):
            def take(dst, src, ready, value, done):
                act.wait_ge(ready, value)
                nc.scalar.activation(dst, src, ACT.Copy).then_inc(done, 1)

            def take_v(b, p):
                take(va[p][:, :, :, 0:HD],
                     ps_f[:, BANK["v"], :].rearrange("p (k h d) -> p k h d", k=NT, h=H), v_done, b + 1, v_taken)

            def take_qk(b, n):
                act.wait_ge(parts_done, 2 * b + n - 1 + PARTS_C)
                take(qk[:, n, :], ps_f[:, BANK["qk"[n]], :], (q_done, k_done)[n], b + 1, (q_taken, k_taken)[n])

            def take_o(b, grp):
                act.wait_ge(ot_done, NG * b + grp - 1 + OT_C)
                take(osb[:, grp % 2, :], ps_o[:, :], pv_done, NE * b + NT * (grp + 1) + PV_C, o_taken)

            def units(b, p, u0, u1, qk_on, front, back, tail):
                for u in range(u0, u1):
                    if back:
                        act.wait_ge(s2_done, NU * b + u + 1 + S2_C)
                        if u % 2 == 0:
                            act.wait_ge(pv_done, NE * b + u // 2 - PSLOTS // 2 + 1 + PV_C)
                        nc.scalar.activation(prob[:, u % PSLOTS, :, :], ps_s[:, u % 2, :, :], ACT.Exp,
                                             scale=float(P) ** -0.5).then_inc(exp_done, 1)
                    for second in range(2):
                        if second and u % 8 == 1 and (back if u > 8 else tail):
                            take_o(*((b, u // 8 - 1) if u > 8 else (b - 1, NG - 1)))
                        for t in turns_of(u, second):
                            if front and t == "v":
                                take_v(b + 1, 1 - p)
                            if qk_on and t == "q":
                                take_qk(b + 2, 0)
                            if qk_on and t == "k":
                                take_qk(b + 2, 1)

            act.sem_inc(exp_done, EXP_C)
            act.sem_inc(o_taken, O_C)
            act.wait_ge(cleared, 4)
            take_qk(0, 0)
            take_qk(0, 1)
            walk(act, units)
            take_o(NB - 1, NG - 1)

        @block.tensor
        def _(pe):
            pe.sem_inc(s2_done, S2_C)
            pe.sem_inc(pv_done, PV_C)
            pe.sem_inc(ot_done, OT_C)
            pe.wait_ge(w_in, 16)
            pe.wait_ge(g["consts_in"], 16)
            pe.wait_ge(fill_in, 6 * 16)

            def turn_max(b, half_no):
                pe.wait_ge(max_done, S1_N * b + HH * NT * (half_no + 1))
                nc.tensor.transpose(ps_f[0:HH * NT, BANK[f"max{half_no}"], 0:P], nmax[:, half_no * HH:(half_no + 1) * HH, :],
                                    ident[:, :]).then_inc(mt_done, 1)

            def v_product(b, p):
                pe.wait_ge(xt_in[p], 8 * (b - p) + 16)
                for kt in range(NT):
                    mm = nc.tensor.matmul(ps_f[:, BANK["v"], kt * P:(kt + 1) * P], xt[p][:, kt * P:(kt + 1) * P],
                                          w[:, 2, :], start=True, stop=True)
                mm.then_inc(v_done, 1)

            def qk_product(b, p, n):
                pe.wait_ge(xt_in[p], 8 * (b - p) + 16)
                nc.tensor.matmul(ps_f[:, BANK["qk"[n]], :], w[:, n, :], xt[p][:, :], start=True,
                                 stop=True).then_inc((q_done, k_done)[n], 1)

            def s1(b, p, n):
                h, qt = n // NT, n % NT
                if n % (S1_N // NG) == 0:
                    pe.wait_ge(stack_in[h // HG], 32 * (b + 1))
                nc.tensor.matmul(ps_f[:, BANK[n], :], qs[p][0:QKP, h, qt * P:(qt + 1) * P], ks[p][0:QKP, h, :],
                                 start=True, stop=True).then_inc(s1_done, 1)

            def free_bank(b, t):
                before = turn_before(t, b)
                if before is None:
                    return
                t, b = before[0], b - before[1]
                if isinstance(t, int):
                    pe.wait_ge(max_done, S1_N * b + t + 1)
                elif t in "qk":
                    pe.wait_ge(q_taken if t == "q" else k_taken, b + 2)
                elif t == "v":
                    pe.wait_ge(v_taken, b + 1)
                elif t in ("max0", "max1"):
                    pe.wait_ge(mt_split, 2 * b + (t == "max0"))
                else:
                    pe.wait_ge(att_done, NG * (b - 1) + (int(t[1]) + 1) % NG + ATT_C)

            def take_turn(b, p, t, qk_on, front, back, tail):
                if isinstance(t, int):
                    if front:
                        free_bank(b, t)
                        s1(b, p, t)
                elif t == "v":
                    if front:
                        free_bank(b, t)
                        v_product(b, p)
                elif t in "qk":
                    if qk_on:
                        free_bank(b, t)
                        qk_product(b + 1, 1 - p, "qk".index(t))
                elif t == "max0":
                    if front:
                        free_bank(b, t)
                        turn_max(b, 0)
                elif t == "max1":
                    if back:
                        free_bank(b, t)
                        turn_max(b - 1, 1)
                elif t == "o3":
                    if tail:
                        free_bank(b, t)
                        turn_o(b - 2, NG - 1)
                elif back:
                    free_bank(b, t)
                    turn_o(b - 1, int(t[1]))

            def s2(b, p, u):
                grp, kt, pair = u // (2 * NT), u // 2 % NT, u % 2
                if u in (0, NU // 2):
                    pe.wait_ge(max_in, MAX_C * (2 * b + u // (NU // 2) + 1) + MAX_C)
                pe.wait_ge(exp_done, NU * b + u - 1 + EXP_C)
                for i in range(UN):
                    h = grp * HG + pair * UN + i
                    mm = nc.tensor.matmul(ps_s[:, u % 2, i, :], ks[p][0:MXR, h, kt * P:(kt + 1) * P],
                                          qs[p][0:MXR, h, :], start=True, stop=True)
                mm.then_inc(s2_done, 1)

            def pv(b, p, e):
                grp, kt = e // NT, e % NT
                if e == 0:
                    pe.wait_ge(v_taken, b + 1)
                if kt == 0:
                    pe.wait_ge(o_taken, NG * b + grp + O_C)
                pe.wait_ge(exp_done, NU * b + 2 * e + 2 + EXP_C)
                for j in range(HG):
                    mm = nc.tensor.matmul(ps_o[j * CT:(j + 1) * CT, :], va[p][:, kt, grp * HG + j, :],
                                          prob[:, (2 * e + j // UN) % PSLOTS, j % UN, :],
                                          start=(kt == 0), stop=(kt == NT - 1))
                mm.then_inc(pv_done, 1)

            def turn_o(b, grp):
                pe.wait_ge(o_taken, NG * b + grp + 1 + O_C)
                for qt in range(NT):
                    mm = nc.tensor.transpose(ps_f[:, BANK[f"o{grp}"], qt * P:(qt + 1) * P],
                                             osb[:, grp % 2, qt * P:(qt + 1) * P], ident[:, :])
                mm.then_inc(ot_done, 1)

            def units(b, p, u0, u1, qk_on, front, back, tail):
                for u in range(u0, u1):
                    if back:
                        s2(b, p, u)
                    for second in range(2):
                        if second and u % 2 and (back if u > 1 else tail):
                            if u > 1:
                                pv(b, p, u // 2 - 1)
                            else:
                                pv(b - 1, 1 - p, NE - 1)
                        for t in turns_of(u, second):
                            take_turn(b + 1, 1 - p, t, qk_on, front, back, tail)

            qk_product(0, 0, 0)
            if BANK["q"] == BANK["k"]:
                pe.wait_ge(q_taken, 1)
            qk_product(0, 0, 1)
            pe.wait_ge(q_taken, 1)
            pe.wait_ge(k_taken, 1)
            walk(pe, units)
            pv(NB - 1, 1, NE - 1)
            pe.wait_ge(att_done, NG * NB - 1 + ATT_C)
            turn_o(NB - 1, NG - 1)

        @block.vector
        def _(dve):
            dve.sem_inc(max_in, MAX_C)
            dve.sem_inc(att_done, ATT_C)

            for i in range(2):
                nc.vector.memset(va[i][:, :, :, HD + 1:CT], 0.0).then_inc(cleared, 1)
                nc.vector.memset(va[i][:, :, :, HD:HD + 1], 1.0).then_inc(cleared, 1)

            def reduce_max(b, n):
                dve.wait_ge(s1_done, S1_N * b + n + 1)
                nc.vector.tensor_reduce(nmax[:, n // NT, n % NT:n % NT + 1], ps_f[:, BANK[n], :], AX.X, ALU.max,
                                        negate=True).then_inc(max_done, 1)

            def split_max(b, half_no):
                k = 2 * b + half_no
                src = ps_f[0:HH * NT, BANK[f"max{half_no}"], 0:P]
                dve.wait_ge(max_in, MAX_C * k + MAX_C)
                dve.wait_ge(mt_done, k + 1)
                nc.vector.tensor_copy(mparts[:, 0, :], src).then_inc(mt_chain, 1)
                dve.wait_ge(mt_chain, 2 * k + 1)
                nc.vector.tensor_tensor(mrest[:, :], src, mparts[:, 0, :], ALU.subtract).then_inc(mt_split, 1)
                dve.wait_ge(mt_split, k + 1)
                nc.vector.tensor_copy(mparts[:, 1, :], mrest[:, :]).then_inc(mt_chain, 1)
                dve.wait_ge(mt_chain, 2 * k + 2)
                nc.vector.tensor_tensor(mparts[:, 2, :], mrest[:, :], mparts[:, 1, :],
                                        ALU.subtract).then_inc(mt_parts, 1)

            def divide(b, grp):
                o = ps_f[:, BANK[f"o{grp}"], :].rearrange("p (k j c) -> p k j c", k=NT, c=CT)
                dve.wait_ge(ot_done, NG * b + grp + 1 + OT_C)
                dve.wait_ge(att_done, NG * b + grp + ATT_C)
                nc.vector.reciprocal(rec[:, :, :], o[:, :, :, HD]).then_inc(rec_done, 1)
                dve.wait_ge(rec_done, NG * b + grp + 1)
                dst = att[:, :, grp * HG * HD:(grp + 1) * HG * HD].rearrange("p k (j c) -> p k j c", c=HD)
                nc.vector.tensor_tensor(dst, o[:, :, :, 0:HD],
                                        rec[:, :, :].unsqueeze(3).broadcast_to([P, NT, HG, HD]),
                                        ALU.mult).then_inc(att_done, 1)

            def add_x(b):
                dve.wait_ge(att_done, NG * (b + 1) + ATT_C)
                nc.vector.tensor_tensor(att[:, :, :], att[:, :, :], X[:, b, :, :], ALU.add).then_inc(sum_done, 1)

            def stats(b):
                dve.wait_ge(sum_done, b + 1)
                layernorm_stats(nc, dve, ln, b, att)

            def units(b, p, u0, u1, qk_on, front, back, tail):
                for u in range(u0, u1):
                    for second in range(2):
                        for t in turns_of(u, second):
                            if front and t == "max0":
                                split_max(b + 1, 0)
                            if back and t == "max1":
                                split_max(b, 1)
                            if back and t in ("o0", "o1", "o2"):
                                divide(b, int(t[1]))
                            if tail and t == "o3":
                                divide(b - 1, NG - 1)
                            if tail and t == SUM_AT:
                                add_x(b - 1)
                            if tail and t == STATS_AT:
                                stats(b - 1)
                            if tail and t == NORM_AT:
                                layernorm_apply(nc, dve, g, ln, b - 1, att)
                            if front and isinstance(t, int):
                                reduce_max(b + 1, t)

            dve.wait_ge(x_in, 16)
            walk(dve, units)
            divide(NB - 1, NG - 1)
            add_x(NB - 1)
            stats(NB - 1)
            layernorm_apply(nc, dve, g, ln, NB - 1, att)

        @block.gpsimd
        def _(pool):
            pool.sem_inc(parts_done, PARTS_C)
            pool.sem_inc(parts_out, OUT_C)

            def split_qk(b, n):
                k = 2 * b + n
                zero = g["zero"][:, :].broadcast_to([P, T])
                pool.wait_ge(parts_out, OUT_C * b + OUT_C)
                pool.wait_ge((q_taken, k_taken)[n], b + 1)
                nc.gpsimd.tensor_tensor(parts[:, n, 0, :], qk[:, n, :], zero, ALU.add).then_inc(split, 1)
                pool.wait_ge(split, 3 * k + 1)
                nc.gpsimd.tensor_tensor(rest[:, n, :], qk[:, n, :], parts[:, n, 0, :],
                                        ALU.subtract).then_inc(split, 1)
                pool.wait_ge(split, 3 * k + 2)
                nc.gpsimd.tensor_tensor(parts[:, n, 1, :], rest[:, n, :], zero, ALU.add).then_inc(split, 1)
                pool.wait_ge(split, 3 * k + 3)
                nc.gpsimd.tensor_tensor(parts[:, n, 2, :], rest[:, n, :], parts[:, n, 1, :],
                                        ALU.subtract).then_inc(parts_done, 1)

            def units(b, p, u0, u1, qk_on, front, back, tail):
                if u0 == 0 and tail:
                    layernorm_pool(nc, pool, g, ln, b - 1)
                if u1 == NU and qk_on:
                    split_qk(b + 2, 0)
                    split_qk(b + 2, 1)

            split_qk(0, 0)
            split_qk(0, 1)
            walk(pool, units)
            layernorm_pool(nc, pool, g, ln, NB - 1)


def attention1(nc, g, w_all, b_qk, v_b, o_b, qn, kn, cos_t, sin_t):
    X, ident = g["X"], g["ident"]
    scratch = [[nc.dram_tensor(f"parts1_{n}{i}", [5, P, T], BF16).ap() for i in range(2)] for n in "qk"]
    with ExitStack() as ctx:
        def sb(name, shape, dt=F32):
            return ctx.enter_context(nc.sbuf_tensor("a1_" + name, shape, dt))

        def sem(name):
            return ctx.enter_context(nc.semaphore("a1_" + name))

        w = sb("w", [P, 6, P])
        bqk = sb("bqk", [P, 4])
        norm_scale = sb("norm_scale", [P, 2])
        vb = sb("vb", [P, P])
        ob = sb("ob", [P, P])
        cos = sb("cos", [P, T])
        sin = sb("sin", [P, T])
        xb = sb("xb", [P, NT, P])
        sq = sb("sq", [P, NT, P])
        xr = sb("xr", [P, NT, P])
        ms = sb("ms", [P, NT])
        rr = sb("rr", [P, NT])
        xrt = sb("xrt", [P, T])
        turned = sb("turned", [P, 2, T])
        att_t = sb("att_t", [P, T])
        xt = [sb(f"xt{i}", [P, T]) for i in range(2)]
        qk = sb("qk", [P, 2, T])
        rest = sb("rest", [P, 2, T])
        parts = sb("parts", [P, 2, PARTS, T], BF16)
        qs = [sb(f"qs{i}", [P, H, T], BF16) for i in range(2)]
        ks = [sb(f"ks{i}", [P, H, T], BF16) for i in range(2)]
        va = [sb(f"va{i}", [P, NT, H, CT]) for i in range(2)]
        prob = sb("prob", [P, PSLOTS, UN, T])
        osb = sb("osb", [P, 2, T])
        rec = sb("rec", [P, NT, HG])
        att = sb("att", [P, NT, P])
        ln = layernorm_buffers(ctx, nc, "a1")
        ps_s = ctx.enter_context(nc.psum_tensor("a1_ps_s", [P, 2, UN, T], F32))
        ps_f = ctx.enter_context(nc.psum_tensor("a1_ps_f", [P, 2, T], F32))
        ps_o = ctx.enter_context(nc.psum_tensor("a1_ps_o", [P, T], F32))
        ps_t = ctx.enter_context(nc.psum_tensor("a1_ps_t", [P, NT, P], F32))

        w_in, w_scaled, cleared = sem("w_in"), sem("w_scaled"), sem("cleared")
        x_step, x_pow, xr_done = sem("x_step"), sem("x_pow"), sem("xr_done")
        f_done, f_taken, rope_step, rope_done = sem("f_done"), sem("f_taken"), sem("rope_step"), sem("rope_done")
        v_done, v_taken, split, parts_done = sem("v_done"), sem("v_taken"), sem("split"), sem("parts_done")
        parts_out, stack_in = sem("parts_out"), [sem(f"stack_in{i}") for i in range(2)]
        at_done, at_taken, y_done, y_taken = sem("at_done"), sem("at_taken"), sem("y_done"), sem("y_taken")
        s2_done, exp_done, pv_done = sem("s2_done"), sem("exp_done"), sem("pv_done")
        o_taken, ot_done, rec_done, att_done, sum_done = (
            sem(n) for n in ("o_taken", "ot_done", "rec_done", "att_done", "sum_done"))
        S2_C, EXP_C, PV_C, O_C, OT_C, ATT_C = NU, 2, PSLOTS // 2, 1, 2, 1
        FILL = 2 * 16
        PARTS_C, OUT_C = 2, 3 * 16
        FN = 6
        Y_C, R_C = 1, 1

        block = ctx.enter_context(nc.Block())

        @block.sync
        def _(sp):
            for dst, src in ((w[:, :, :], w_all), (bqk[:, :], b_qk), (norm_scale[:, 0:1], qn), (norm_scale[:, 1:2], kn),
                             (vb[:, :], bass.AP(tensor=v_b.tensor, offset=0, ap=[[0, P], [1, P]])),
                             (ob[:, :], bass.AP(tensor=o_b.tensor, offset=0, ap=[[0, P], [1, P]])),
                             (cos[:, :], cos_t), (sin[:, :], sin_t)):
                sp.dma_start(dst, src).then_inc(w_in, 16)

            def parts_to_dram(b, p):
                for n, seg in ((0, 0), (1, 0), (1, 1)):
                    if seg == 0:
                        sp.wait_ge(parts_done, 2 * b + n + 1 + PARTS_C)
                    dst = scratch[n][p].rearrange("r p t -> p r t")
                    if seg == 0:
                        sp.dma_start(dst[:, 0:PARTS, :], parts[:, n, :, :]).then_inc(parts_out, 16)
                    else:
                        sp.dma_start(dst[:, PARTS:5, :], parts[:, n, 0:2, :]).then_inc(parts_out, 16)

            def stack(b, p):
                sp.wait_ge(parts_out, 48 * (b + 1) + OUT_C)
                for n, dst in ((0, qs), (1, ks)):
                    src = scratch[n][p]
                    rows = PARTS * HD
                    src = bass.AP(tensor=src.tensor, offset=0,
                                  ap=[[n * HD * H * T, PARTS], [H * T, rows], [1, H * T]])
                    sp.dma_start(dst[p][0:QKR, :, :], src).then_inc(stack_in[p], 16)

            def step(b, p, qk_on, front):
                if front:
                    sp.wait_ge(s2_done, NU * b + S2_C)
                    stack(b + 1, 1 - p)
                if qk_on:
                    parts_to_dram(b + 2, p)

            for i in range(2):
                for dst in (qs, ks):
                    src = bass.AP(tensor=g["fill"].tensor, offset=0, ap=[[0, QKP - QKR], [1, H * T]])
                    sp.dma_start(dst[i][QKR:QKP, :, :], src).then_inc(stack_in[i], 16)
            parts_to_dram(0, 0)
            stack(0, 0)
            parts_to_dram(1, 1)
            with sp.Fori(0, (NB - 2) // 2) as i:
                step(2 * i, 0, True, True)
                step(2 * i + 1, 1, True, True)
            step(NB - 2, 0, False, True)

        @block.scalar
        def _(act):
            def take(dst, src, ready, value, done):
                act.wait_ge(ready, value)
                nc.scalar.activation(dst, src, ACT.Copy).then_inc(done, 1)

            def take_o(b, grp):
                act.wait_ge(ot_done, NG * b + grp - 1 + OT_C)
                take(osb[:, grp % 2, :], ps_o[:, :], pv_done, NE * b + NT * (grp + 1) + PV_C, o_taken)

            def step(b):
                for u in range(NU):
                    act.wait_ge(s2_done, NU * b + u + 1 + S2_C)
                    if u % 2 == 0:
                        act.wait_ge(pv_done, NE * b + u // 2 - PSLOTS // 2 + 1 + PV_C)
                    nc.scalar.activation(prob[:, u % PSLOTS, :, :], ps_s[:, u % 2, :, :], ACT.Sigmoid,
                                         scale=float(HD) ** -0.5).then_inc(exp_done, 1)
                    if u % 8 == 1 and u > 8:
                        take_o(b, u // 8 - 1)
                take_o(b, NG - 1)

            act.sem_inc(exp_done, EXP_C)
            act.sem_inc(o_taken, O_C)
            with act.Fori(0, NB) as b:
                step(b)

        @block.tensor
        def _(pe):
            pe.sem_inc(s2_done, S2_C)
            pe.sem_inc(pv_done, PV_C)
            pe.sem_inc(ot_done, OT_C)
            pe.wait_ge(w_scaled, 2)

            def v_product(b, p):
                pe.wait_ge(f_taken, FN * (b + 1))
                for kt in range(NT):
                    mm = nc.tensor.matmul(ps_f[:, 1, kt * P:(kt + 1) * P], xt[p][:, kt * P:(kt + 1) * P],
                                          w[:, 4, :], start=True, stop=True)
                mm.then_inc(v_done, 1)

            def front_use(b, p, k, v_too):
                if k == 0:
                    pe.wait_ge(x_step, 4 * b + 1)
                elif k == 1:
                    pe.wait_ge(xr_done, b + 1)
                    if v_too:
                        pe.wait_ge(v_taken, b)
                if k >= 2:
                    pe.wait_ge(f_taken, FN * b + max(k - 1, 2))
                if k < 2:
                    src = (xb, xr)[k]
                    for kt in range(NT):
                        mm = nc.tensor.transpose(ps_f[:, k, kt * P:(kt + 1) * P], src[:, kt, :], g["ident"][:, :])
                else:
                    mm = nc.tensor.matmul(ps_f[:, k % 2, :], w[:, k - 2, :], xrt[:, :], start=True, stop=True)
                mm.then_inc(f_done, 1)

            def s2(b, p, u):
                grp, kt, pair = u // (2 * NT), u // 2 % NT, u % 2
                if u == 0:
                    pe.wait_ge(stack_in[p], 16 * (b - p) + 32 + FILL)
                pe.wait_ge(exp_done, NU * b + u - 1 + EXP_C)
                for i in range(UN):
                    h = grp * HG + pair * UN + i
                    mm = nc.tensor.matmul(ps_s[:, u % 2, i, :], ks[p][0:QKP, h, kt * P:(kt + 1) * P],
                                          qs[p][0:QKP, h, :], start=True, stop=True)
                mm.then_inc(s2_done, 1)

            def pv(b, p, e):
                grp, kt = e // NT, e % NT
                if e == 0:
                    pe.wait_ge(v_taken, b + 1)
                if kt == 0:
                    pe.wait_ge(o_taken, NG * b + grp + O_C)
                pe.wait_ge(exp_done, NU * b + 2 * e + 2 + EXP_C)
                for j in range(HG):
                    mm = nc.tensor.matmul(ps_o[j * CT:(j + 1) * CT, :], va[p][:, kt, grp * HG + j, :],
                                          prob[:, (2 * e + j // UN) % PSLOTS, j % UN, :],
                                          start=(kt == 0), stop=(kt == NT - 1))
                mm.then_inc(pv_done, 1)

            def turn_o(b, grp):
                pe.wait_ge(o_taken, NG * b + grp + 1 + O_C)
                if grp == 0:
                    pe.wait_ge(y_taken, b + Y_C)
                else:
                    pe.wait_ge(att_done, NG * b + grp + ATT_C)
                for qt in range(NT):
                    mm = nc.tensor.transpose(ps_t[:, qt, :], osb[:, grp % 2, qt * P:(qt + 1) * P], ident[:, :])
                mm.then_inc(ot_done, 1)

            def project(b):
                pe.wait_ge(att_done, NG * (b + 1) + ATT_C)
                for kt in range(NT):
                    mm = nc.tensor.transpose(ps_t[:, kt, :], att[:, kt, :], ident[:, :])
                mm.then_inc(at_done, 1)
                pe.wait_ge(at_taken, b + 1)
                for kt in range(NT):
                    mm = nc.tensor.matmul(ps_t[:, kt, :], att_t[:, kt * P:(kt + 1) * P], w[:, 5, :],
                                          start=True, stop=True)
                mm.then_inc(y_done, 1)

            def step(b, p, qk_on, front, back):
                if front:
                    v_product(b + 1, 1 - p)
                for u in range(NU):
                    if back:
                        s2(b, p, u)
                        if u % 2 == 1 and u > 1:
                            pv(b, p, (u - 3) // 2)
                        if u % 8 == 5 and u > 8:
                            turn_o(b, u // 8 - 1)
                    if qk_on and u % 3 == 2 and u < 3 * FN:
                        front_use(b + 2, p, u // 3, front)
                if back:
                    pv(b, p, NE - 1)
                    turn_o(b, NG - 1)
                    project(b)

            step(-2, 0, True, False, False)
            step(-1, 1, True, True, False)
            with pe.Fori(0, (NB - 2) // 2) as i:
                step(2 * i, 0, True, True, True)
                step(2 * i + 1, 1, True, True, True)
            step(NB - 2, 0, False, True, True)
            step(NB - 1, 1, False, False, True)

        @block.vector
        def _(dve):
            dve.sem_inc(y_taken, Y_C)
            dve.sem_inc(rope_done, R_C)
            dve.sem_inc(att_done, ATT_C)

            for i in range(2):
                nc.vector.memset(va[i][:, :, :, HD + 1:CT], 0.0).then_inc(cleared, 1)
                nc.vector.memset(va[i][:, :, :, HD:HD + 1], 1.0).then_inc(cleared, 1)

            dve.wait_ge(w_in, 8 * 16)
            for n in range(2):
                nc.vector.tensor_scalar(w[:, 2 * n:2 * n + 2, :], w[:, 2 * n:2 * n + 2, :], norm_scale[:, n:n + 1],
                                        None, ALU.mult).then_inc(w_scaled, 1)

            def rms(b):
                c = 4 * b
                nc.vector.tensor_copy(xb[:, :, :], X[:, b, :, :]).then_inc(x_step, 1)
                dve.wait_ge(x_step, c + 1)
                nc.vector.tensor_tensor(sq[:, :, :], xb[:, :, :], xb[:, :, :], ALU.mult).then_inc(x_step, 1)
                dve.wait_ge(x_step, c + 2)
                nc.vector.tensor_reduce(ms[:, :], sq[:, :, :], AX.X, ALU.add).then_inc(x_step, 1)
                dve.wait_ge(x_step, c + 3)
                nc.vector.tensor_scalar(ms[:, :], ms[:, :], 1.0 / P, RMS_EPS, ALU.mult, ALU.add).then_inc(x_step, 1)

            def scale_x(b):
                dve.wait_ge(x_pow, b + 1)
                nc.vector.tensor_tensor(xr[:, :, :], xb[:, :, :],
                                        rr[:, :].unsqueeze(2).broadcast_to([P, NT, P]), ALU.mult).then_inc(xr_done, 1)

            def take_front(b, p, k):
                dve.wait_ge(f_done, FN * b + k + 1)
                if k < 2:
                    nc.vector.tensor_copy((xt[p], xrt)[k][:, :], ps_f[:, k, :]).then_inc(f_taken, 1)
                    return
                n = (k - 2) // 2
                if k % 2 == 0:
                    dve.wait_ge(parts_done, 2 * b + n - 1 + PARTS_C)
                    dve.wait_ge(rope_done, 2 * b + n + R_C)
                nc.vector.scalar_tensor_tensor(turned[:, k % 2, :], ps_f[:, k % 2, :], bqk[:, k - 2:k - 1],
                                               (cos, sin)[k % 2][:, :], ALU.add, ALU.mult).then_inc(f_taken, 1)
                if k % 2:
                    dve.wait_ge(f_taken, FN * b + k + 1)
                    nc.vector.tensor_tensor(qk[:, n, :], turned[:, 0, :], turned[:, 1, :],
                                            ALU.add).then_inc(rope_done, 1)

            def take_v(b, p):
                dve.wait_ge(v_done, b + 1)
                nc.vector.tensor_tensor(va[p][:, :, :, 0:HD],
                                        ps_f[:, 1, :].rearrange("p (k h d) -> p k h d", k=NT, h=H),
                                        vb[:, :].rearrange("p (h d) -> p h d", h=H).unsqueeze(1).broadcast_to(
                                            [P, NT, H, HD]), ALU.add).then_inc(v_taken, 1)

            def divide(b, grp):
                o = ps_t[:, :, :].rearrange("p k (j c) -> p k j c", c=CT)
                dve.wait_ge(ot_done, NG * b + grp + 1 + OT_C)
                nc.vector.tensor_scalar_add(rec[:, :, :], o[:, :, :, HD], RENORM_EPS).then_inc(rec_done, 1)
                dve.wait_ge(rec_done, 2 * (NG * b + grp) + 1)
                nc.vector.reciprocal(rec[:, :, :], rec[:, :, :]).then_inc(rec_done, 1)
                dve.wait_ge(rec_done, 2 * (NG * b + grp) + 2)
                dst = att[:, :, grp * HG * HD:(grp + 1) * HG * HD].rearrange("p k (j c) -> p k j c", c=HD)
                nc.vector.tensor_tensor(dst, o[:, :, :, 0:HD],
                                        rec[:, :, :].unsqueeze(3).broadcast_to([P, NT, HG, HD]),
                                        ALU.mult).then_inc(att_done, 1)

            def finish(b):
                dve.wait_ge(at_done, b + 1)
                nc.vector.tensor_copy(att_t[:, :], ps_t[:, :, :]).then_inc(at_taken, 1)
                dve.wait_ge(y_done, b + 1)
                nc.vector.tensor_tensor(att[:, :, :], ps_t[:, :, :],
                                        ob[:, :].unsqueeze(1).broadcast_to([P, NT, P]), ALU.add).then_inc(y_taken, 1)
                dve.wait_ge(y_taken, b + 1 + Y_C)
                nc.vector.tensor_tensor(att[:, :, :], att[:, :, :], X[:, b, :, :], ALU.add).then_inc(sum_done, 1)
                dve.wait_ge(sum_done, b + 1)
                layernorm_dve(nc, dve, g, ln, b, att)

            def step(b, p, qk_on, front, back):
                if qk_on:
                    rms(b + 2)
                if front:
                    take_v(b + 1, 1 - p)
                if qk_on:
                    scale_x(b + 2)
                for u in range(NU):
                    if back and u % 8 == 5 and u > 8:
                        divide(b, u // 8 - 1)
                    if qk_on and u % 3 == 2 and u < 3 * FN:
                        take_front(b + 2, p, u // 3)
                if back:
                    divide(b, NG - 1)
                    finish(b)

            step(-2, 0, True, False, False)
            step(-1, 1, True, True, False)
            with dve.Fori(0, (NB - 2) // 2) as i:
                step(2 * i, 0, True, True, True)
                step(2 * i + 1, 1, True, True, True)
            step(NB - 2, 0, False, True, True)
            step(NB - 1, 1, False, False, True)

        @block.gpsimd
        def _(pool):
            pool.sem_inc(parts_done, PARTS_C)
            pool.sem_inc(parts_out, OUT_C)

            def split_qk(b, n):
                k = 2 * b + n
                zero = g["zero"][:, :].broadcast_to([P, T])
                pool.wait_ge(parts_out, OUT_C * b + OUT_C)
                pool.wait_ge(rope_done, 2 * b + n + 1 + R_C)
                nc.gpsimd.tensor_tensor(parts[:, n, 0, :], qk[:, n, :], zero, ALU.add).then_inc(split, 1)
                pool.wait_ge(split, 3 * k + 1)
                nc.gpsimd.tensor_tensor(rest[:, n, :], qk[:, n, :], parts[:, n, 0, :],
                                        ALU.subtract).then_inc(split, 1)
                pool.wait_ge(split, 3 * k + 2)
                nc.gpsimd.tensor_tensor(parts[:, n, 1, :], rest[:, n, :], zero, ALU.add).then_inc(split, 1)
                pool.wait_ge(split, 3 * k + 3)
                nc.gpsimd.tensor_tensor(parts[:, n, 2, :], rest[:, n, :], parts[:, n, 1, :],
                                        ALU.subtract).then_inc(parts_done, 1)

            def step(b, qk_on, back):
                if qk_on:
                    pool.wait_ge(x_step, 4 * (b + 3))
                    nc.gpsimd.tensor_tensor(rr[:, :], ms[:, :], g["neg_half"][:, :], ALU.pow).then_inc(x_pow, 1)
                    split_qk(b + 2, 0)
                    split_qk(b + 2, 1)
                if back:
                    layernorm_pool(nc, pool, g, ln, b)

            step(-2, True, False)
            step(-1, True, False)
            with pool.Fori(0, (NB - 2) // 2) as i:
                step(2 * i, True, True)
                step(2 * i + 1, True, True)
            step(NB - 2, False, True)
            step(NB - 1, False, True)


def shared(ctx, nc, x, ident_in, fill):
    def sb(name, shape):
        return ctx.enter_context(nc.sbuf_tensor("g_" + name, shape, F32))

    def sem(name):
        return ctx.enter_context(nc.semaphore(name))

    return {"X": sb("X", [P, NB, NT, P]), "ident": sb("ident", [P, P]), "eps": sb("eps", [P, NT]),
            "neg_half": sb("neg_half", [P, NT]), "zero": sb("zero", [P, 1]), "x": x, "fill": fill, "ident_in": ident_in,
            "x_in": sem("x_in"), "consts_in": sem("consts_in"), "consts": sem("consts")}


def setup(nc, g):
    with nc.Block() as block:
        @block.sync
        def _(sp):
            sp.dma_start(g["ident"][:, :], g["ident_in"]).then_inc(g["consts_in"], 16)

        @block.gpsimd
        def _(pool):
            nc.gpsimd.memset(g["eps"][:, :], LN_EPS).then_inc(g["consts"], 1)
            nc.gpsimd.memset(g["neg_half"][:, :], -0.5).then_inc(g["consts"], 1)
            nc.gpsimd.memset(g["zero"][:, :], 0.0).then_inc(g["consts"], 1)
            pool.wait_ge(g["consts"], 3)


def turn_x(nc, g, ps, xt, name, ctx):
    X = g["X"]
    turned = ctx.enter_context(nc.semaphore(name + "_turned"))
    copied = ctx.enter_context(nc.semaphore(name + "_copied"))
    with nc.Block() as block:
        @block.tensor
        def _(pe):
            for b in range(NB):
                if b >= 2:
                    pe.wait_ge(copied, b - 1)
                for k in range(NT):
                    mm = nc.tensor.transpose(ps[:, b % 2, k * P:(k + 1) * P], X[:, b, k, :], g["ident"][:, :])
                mm.then_inc(turned, 1)

        @block.vector
        def _(dve):
            for b in range(NB):
                dve.wait_ge(turned, b + 1)
                nc.vector.tensor_copy(xt[:, b, :], ps[:, b % 2, :]).then_inc(copied, 1)


def route(nc, g, xt, ct, gate_t, bias):
    NTL = NB * NT
    with ExitStack() as ctx:
        def sb(name, shape, dt=F32):
            return ctx.enter_context(nc.sbuf_tensor("r_" + name, shape, dt))

        def sem(name):
            return ctx.enter_context(nc.semaphore("r_" + name))

        gate_sb = sb("gate", [P, E])
        bias_sb = sb("bias", [P, E])
        iota = sb("iota", [P, E])
        identb = sb("identb", [P, P], BF16)
        e1 = sb("e1", [P, NTL, E])
        score = sb("score", [P, NTL, E])
        sfc = sb("sfc", [P, NTL, E])
        gmax = sb("gmax", [P, NTL, NGRP])
        top = sb("top", [P, NTL, 8])
        topi = sb("topi", [P, NTL, 8], U32)
        topf = sb("topf", [P, NTL, 8])
        gmask = sb("gmask", [P, NTL, NGRP])
        hit = sb("hit", [P, NTL, TOPK, E])
        den = sb("den", [P, NTL])
        cpart = sb("cpart", [P, NTL, PARTS, E], BF16)
        ps_l = ctx.enter_context(nc.psum_tensor("r_ps_l", [P, NTL, E], F32))
        ps_c = ctx.enter_context(nc.psum_tensor("r_ps_c", [PARTS * E, 2, 2 * T], BF16))
        r_in, logits, exp_done, vec, c_turned, c_taken = (
            sem(n) for n in ("in", "logits", "exp_done", "vec", "c_turned", "c_taken"))

        with nc.Block() as block:
            @block.sync
            def _(sp):
                sp.dma_start(gate_sb[:, :], gate_t).then_inc(r_in, 16)
                sp.dma_start(bias_sb[:, :], bass.AP(tensor=bias.tensor, offset=0, ap=[[0, P], [1, E]])).then_inc(r_in, 16)
                sp.dma_start(iota[:, :], bass.AP(tensor=g["iota_in"].tensor, offset=0,
                                                 ap=[[0, P], [1, E]])).then_inc(r_in, 16)

            @block.tensor
            def _(pe):
                pe.wait_ge(r_in, 48)
                for k in range(NTL):
                    mm = nc.tensor.matmul(ps_l[:, k, :], xt[:, k // NT, k % NT * P:(k % NT + 1) * P],
                                          gate_sb[:, :], start=True, stop=True)
                mm.then_inc(logits, 1)
                pe.wait_ge(vec, STEPS)
                for b in range(NB):
                    if b >= 2:
                        pe.wait_ge(c_taken, b - 1)
                    for k in range(NT):
                        mm = nc.tensor.transpose(ps_c[:, b % 2, k * P:(k + 1) * P],
                                                 cpart[:, b * NT + k, :, :], identb[:, :])
                    mm.then_inc(c_turned, 1)

            @block.scalar
            def _(act):
                act.wait_ge(logits, 1)
                nc.scalar.activation(e1[:, :, :], ps_l[:, :, :], ACT.Exp, scale=-1.0).then_inc(exp_done, 1)

            count = [0]

            @block.vector
            def _(dve):
                def link(ins):
                    count[0] += 1
                    ins.then_inc(vec, 1)
                    dve.wait_ge(vec, count[0])

                def pick(values, n):
                    for k in range(NTL):
                        ins = nc.vector.max(top[:, k, :], values[:, k, :])
                    link(ins)
                    for k in range(NTL):
                        ins = nc.vector.max_index(topi[:, k, :], top[:, k, :], values[:, k, :])
                    link(ins)
                    link(nc.vector.tensor_copy(topf[:, :, :], topi[:, :, :]))

                def mark(dst, n, width):
                    h = hit[:, :, 0:n, 0:width]
                    for q in range(0, NTL, 8):
                        for j in range(n):
                            ins = nc.vector.tensor_tensor(
                                h[:, q:q + 8, j, :], topf[:, q:q + 8, j:j + 1].broadcast_to([P, 8, width]),
                                iota[:, 0:width].unsqueeze(1).broadcast_to([P, 8, width]), ALU.is_equal)
                    link(ins)
                    link(nc.vector.tensor_reduce(dst, h.rearrange("p t k e -> p t e k"), AX.X, ALU.add))

                dve.wait_ge(r_in, 48)
                dve.wait_ge(g["consts_in"], 16)
                nc.vector.tensor_copy(identb[:, :], g["ident"][:, :])
                dve.wait_ge(exp_done, 1)
                link(nc.vector.tensor_scalar_add(e1[:, :, :], e1[:, :, :], 1.0))
                link(nc.vector.reciprocal(score[:, :, :], e1[:, :, :]))
                link(nc.vector.tensor_tensor(sfc[:, :, :], score[:, :, :],
                                             bias_sb[:, :].unsqueeze(1).broadcast_to([P, NTL, E]), ALU.add))
                link(nc.vector.tensor_reduce(gmax[:, :, :], sfc[:, :, :].rearrange("p t (g e) -> p t g e", g=NGRP),
                                             AX.X, ALU.max))
                pick(gmax, TOPG)
                mark(gmask[:, :, :], TOPG, NGRP)
                gs = E // NGRP
                link(nc.vector.tensor_tensor(
                    sfc[:, :, :].rearrange("p t (g e) -> p t g e", g=NGRP),
                    sfc[:, :, :].rearrange("p t (g e) -> p t g e", g=NGRP),
                    gmask[:, :, :].unsqueeze(3).broadcast_to([P, NTL, NGRP, gs]), ALU.mult))
                pick(sfc, TOPK)
                mark(e1[:, :, :], TOPK, E)
                link(nc.vector.tensor_tensor(score[:, :, :], score[:, :, :], e1[:, :, :], ALU.mult))
                link(nc.vector.tensor_reduce(den[:, :], score[:, :, :], AX.X, ALU.add))
                link(nc.vector.tensor_scalar_add(den[:, :], den[:, :], 1e-20))
                link(nc.vector.reciprocal(den[:, :], den[:, :]))
                link(nc.vector.tensor_scalar(den[:, :], den[:, :], ROUTE_SCALE, None, ALU.mult))
                link(nc.vector.tensor_tensor(score[:, :, :], score[:, :, :],
                                             den[:, :].unsqueeze(2).broadcast_to([P, NTL, E]), ALU.mult))
                link(nc.vector.tensor_copy(cpart[:, :, 0, :], score[:, :, :]))
                link(nc.vector.tensor_tensor(e1[:, :, :], score[:, :, :], cpart[:, :, 0, :], ALU.subtract))
                link(nc.vector.tensor_copy(cpart[:, :, 1, :], e1[:, :, :]))
                link(nc.vector.tensor_tensor(cpart[:, :, 2, :], e1[:, :, :], cpart[:, :, 1, :], ALU.subtract))
                assert count[0] == STEPS, count[0]
                for b in range(NB):
                    dve.wait_ge(c_turned, b + 1)
                    nc.vector.tensor_copy(ct[:, b, :], ps_c[:, b % 2, 0:T]).then_inc(c_taken, 1)


STEPS = 25


def feed_forward(nc, g, name, n_un, xt, wg, wu, wd, ct=None, sel=None, ready=None):
    with ExitStack() as ctx:
        def sb(n, shape, dt=F32):
            return ctx.enter_context(nc.sbuf_tensor(f"{name}_{n}", shape, dt))

        def sem(n):
            return ctx.enter_context(nc.semaphore(f"{name}_{n}"))

        X = g["X"]
        LAG = 2
        RH = 3
        n_c = n_un - 1 if ct is not None else 0
        gated = sb("gated", [P, 2, T])
        prod = sb("prod", [P, 2, T])
        hid = sb("hid", [P, RH, T])
        dsb = sb("dsb", [P, T])
        y = sb("y", [P, NT, P])
        ln = layernorm_buffers(ctx, nc, name)
        ps = ctx.enter_context(nc.psum_tensor(f"{name}_ps", [P, 8, T], F32))
        ps_g, ps_u, ps_c, ps_d, ps_t = ps[:, 0:2, :], ps[:, 2:4, :], ps[:, 4:6, :], ps[:, 6, :], ps[:, 7, :]
        g_done, u_done, c_done, silu_done, prod_done, hid_done, d_done, d_taken, t_done, t_taken = (
            sem(n) for n in ("g_done", "u_done", "c_done", "silu_done", "prod_done", "hid_done", "d_done",
                             "d_taken", "t_done", "t_taken"))
        C = 4

        def since(j, ring, limit=n_un):
            before = [j - q for q in range(j) if q % ring == j % ring and q < limit]
            last = [n_un + j - q for q in range(limit) if q % ring == j % ring]
            return min(before or last)

        block = ctx.enter_context(nc.Block())

        @block.tensor
        def _(pe):
            pe.sem_inc(d_done, C)

            def unit(b, j):
                rhs = xt[:, b, :]
                n = n_un * b + j
                pe.wait_ge(silu_done, n - since(j, 2) + 1 + C)
                nc.tensor.matmul(ps_g[:, j % 2, :], wg[:, j, :], rhs, start=True, stop=True).then_inc(g_done, 1)
                pe.wait_ge(prod_done, n - since(j, 2) + 1 + C)
                nc.tensor.matmul(ps_u[:, j % 2, :], wu[:, j, :], rhs, start=True, stop=True).then_inc(u_done, 1)
                if j < n_c:
                    pe.wait_ge(hid_done, n - since(j, 2, n_c) + 1 + C)
                    nc.tensor.matmul(ps_c[:, j % 2, :], sel[:, j, :], ct[:, b, :], start=True,
                                     stop=True).then_inc(c_done, 1)

            def down(b, j):
                n = n_un * b + j
                pe.wait_ge(hid_done, n + 1 + C)
                if j == 0:
                    pe.wait_ge(d_taken, b + C)
                nc.tensor.matmul(ps_d, wd[:, j, :], hid[:, j % RH, :], start=(j == 0),
                                 stop=(j == n_un - 1)).then_inc(d_done, 1)

            def turn(b):
                pe.wait_ge(d_taken, b + 1 + C)
                pe.wait_ge(t_taken, b + C)
                for q in range(NT):
                    mm = nc.tensor.transpose(ps_t[:, q * P:(q + 1) * P], dsb[:, q * P:(q + 1) * P], g["ident"][:, :])
                mm.then_inc(t_done, 1)

            if ready is not None:
                ready(pe)
            walk_ff(pe, n_un, LAG, unit, down, turn)

        @block.scalar
        def _(act):
            act.sem_inc(silu_done, C)
            act.sem_inc(d_taken, C)

            def unit(b, j):
                n = n_un * b + j
                act.wait_ge(g_done, n + 1)
                act.wait_ge(prod_done, n - since(j, 2) + 1 + C)
                nc.scalar.activation(gated[:, j % 2, :], ps_g[:, j % 2, :], ACT.Silu).then_inc(silu_done, 1)

            def turn(b):
                act.wait_ge(d_done, n_un * (b + 1) + C)
                nc.scalar.activation(dsb[:, :], ps_d, ACT.Copy).then_inc(d_taken, 1)

            walk_ff(act, n_un, LAG, unit, None, turn)

        @block.vector
        def _(dve):
            dve.sem_inc(prod_done, C)
            dve.sem_inc(hid_done, C)
            dve.sem_inc(t_taken, C)
            dve.sem_inc(ln["x_done"], 1)

            def unit(b, j):
                n = n_un * b + j
                dve.wait_ge(silu_done, n + 1 + C)
                dve.wait_ge(u_done, n + 1)
                dve.wait_ge(d_done, n - since(j, RH) + 1 + C)
                if j < n_c:
                    nc.vector.tensor_tensor(prod[:, j % 2, :], gated[:, j % 2, :], ps_u[:, j % 2, :],
                                            ALU.mult).then_inc(prod_done, 1)
                    dve.wait_ge(prod_done, n + 1 + C)
                    dve.wait_ge(c_done, n_c * b + j + 1)
                    nc.vector.tensor_tensor(hid[:, j % RH, :], prod[:, j % 2, :], ps_c[:, j % 2, :],
                                            ALU.mult).then_inc(hid_done, 1)
                else:
                    nc.vector.tensor_tensor(hid[:, j % RH, :], gated[:, j % 2, :], ps_u[:, j % 2, :],
                                            ALU.mult).then_inc(prod_done, 1)
                    dve.wait_ge(prod_done, n + 1 + C)
                    nc.vector.memset(ln["gate"][:, :], 0.0).then_inc(hid_done, 1)

            def turn(b):
                dve.wait_ge(ln["x_done"], b + 1)
                dve.wait_ge(t_done, b + 1)
                nc.vector.tensor_tensor(y[:, :, :], ps_t.rearrange("p (k d) -> p k d", k=NT), X[:, b, :, :],
                                        ALU.add).then_inc(t_taken, 1)
                dve.wait_ge(t_taken, b + 1 + C)
                layernorm_dve(nc, dve, g, ln, b, y)

            walk_ff(dve, n_un, LAG, unit, None, turn)

        @block.gpsimd
        def _(pool):
            with pool.Fori(0, NB) as b:
                layernorm_pool(nc, pool, g, ln, b)


def walk_ff(eng, n_un, lag, unit, down, turn):
    def batch(b, before):
        for j in range(n_un):
            unit(b, j)
            if down is not None:
                if j >= lag:
                    down(b, j - lag)
                elif before:
                    down(b - 1, n_un - lag + j)
            if before and j == lag:
                turn(b - 1)

    batch(0, False)
    with eng.Fori(1, NB) as b:
        batch(b, True)
    if down is not None:
        for j in range(n_un - lag, n_un):
            down(NB - 1, j)
    turn(NB - 1)


def ffn_weights(nc, g, ints, floats, ctx):
    w_in = ctx.enter_context(nc.semaphore("i_in"))
    w_conv = ctx.enter_context(nc.semaphore("i_conv"))
    with nc.Block() as block:
        @block.sync
        def _(sp):
            for src, ib, _ in ints:
                sp.dma_start(ib[:, :, :], src).then_inc(w_in, 16)

        @block.vector
        def _(dve):
            dve.wait_ge(w_in, 16 * len(ints))
            for n, (_, ib, fb) in enumerate(ints):
                nc.vector.tensor_copy(fb[:, :, :], ib[:, :, :]).then_inc(w_conv, 1)
            dve.wait_ge(w_conv, len(ints))
            for n, (_, ib, fb) in enumerate(ints):
                nc.vector.tensor_scalar(fb[:, :, :], fb[:, :, :], WEIGHT_SCALE, None, ALU.mult).then_inc(w_conv, 1)
            dve.wait_ge(w_conv, 2 * len(ints))


def program(nc, ident, fill, iota, sel, x, x_t, w_qkv, gate_t, bias, wg, wu, wd, w1, b1, v_b, o_b, qn, kn, cos, sin,
            fg, fu, fd, out):
    with ExitStack() as ctx:
        g = shared(ctx, nc, x, ident, fill)
        g["iota_in"] = iota
        setup(nc, g)
        attention0(nc, g, x_t, w_qkv)
        with ExitStack() as part:
            def sb(name, shape, dt=F32):
                return part.enter_context(nc.sbuf_tensor(name, shape, dt))

            xt = sb("moe_xt", [P, NB, T])
            ct = sb("moe_ct", [PARTS * E, NB, T], BF16)
            with ExitStack() as ps_ctx:
                ps = ps_ctx.enter_context(nc.psum_tensor("turn_ps", [P, 2, T], F32))
                turn_x(nc, g, ps, xt, "moe", part)
            route(nc, g, xt, ct, gate_t, bias)
            wg_sb, wu_sb, wd_sb = (sb(n, [P, FF, P]) for n in ("moe_wg", "moe_wu", "moe_wd"))
            sel_sb = sb("moe_sel", [PARTS * E, NPAIR, P], BF16)
            moe_in = part.enter_context(nc.semaphore("moe_in"))
            with nc.Block() as block:
                @block.sync
                def _(sp):
                    for dst, src in ((wg_sb, wg), (wu_sb, wu), (wd_sb, wd), (sel_sb, sel)):
                        sp.dma_start(dst[:, :, :], src).then_inc(moe_in, 16)
            feed_forward(nc, g, "moe", FF, xt, wg_sb, wu_sb, wd_sb, ct, sel_sb,
                         lambda pe: pe.wait_ge(moe_in, 4 * 16))
        attention1(nc, g, w1, b1, v_b, o_b, qn, kn, cos, sin)
        with ExitStack() as part:
            def sb(name, shape, dt=F32):
                return part.enter_context(nc.sbuf_tensor(name, shape, dt))

            xt = sb("ff_xt", [P, NB, T])
            ints, floats = [], []
            for n, src in (("g", fg), ("u", fu), ("d", fd)):
                ints.append((src, sb("ff_i" + n, [P, NH3, P], I32), sb("ff_w" + n, [P, NH3, P])))
            ffn_weights(nc, g, ints, floats, part)
            with ExitStack() as ps_ctx:
                ps = ps_ctx.enter_context(nc.psum_tensor("turn2_ps", [P, 2, T], F32))
                turn_x(nc, g, ps, xt, "ff", part)
            feed_forward(nc, g, "ff", NH3, xt, ints[0][2], ints[1][2], ints[2][2])
        x_out = ctx.enter_context(nc.semaphore("x_out"))
        with nc.Block() as block:
            @block.sync
            def _(sp):
                sp.dma_start(out.rearrange("b (k p) d -> p b k d", p=P), g["X"][:, :, :, :]).then_inc(x_out, 16)
                sp.wait_ge(x_out, 16)


def layouts(i):
    import numpy as np
    r = {}
    r["ident"] = np.eye(P, dtype=np.float32)
    r["fill"] = np.stack([np.zeros(H * T), np.ones(H * T)]).astype("bfloat16")
    r["iota"] = np.arange(E, dtype=np.float32)
    sel = np.zeros((PARTS, E, NPAIR, P), np.float32)
    for j in range(NPAIR):
        sel[:, 2 * j, j, :EI] = 1
        sel[:, 2 * j + 1, j, EI:] = 1
    r["sel"] = sel.reshape(PARTS * E, NPAIR, P).astype("bfloat16")
    x = np.asarray(i["L0_attn_x"])
    r["x"] = x
    r["x_t"] = np.ascontiguousarray(x.reshape(NB * T, P).T)
    dims, heads = np.divmod(np.arange(P), H)
    order = heads * HD + dims
    turned = heads * HD + (dims ^ 1)
    w = np.asarray(i["L0_attn_W_qkv"])
    r["w_qkv"] = np.ascontiguousarray(np.concatenate([w[:, :P][:, order], w[:, P:2 * P][:, order], w[:, 2 * P:]], 1))
    r["gate_t"] = np.ascontiguousarray(np.asarray(i["L0_ffn_gate_weight"]).T)
    r["bias"] = np.asarray(i["L0_ffn_e_score_correction_bias"])
    gu = np.asarray(i["L0_ffn_experts_gate_up"])
    for n, (a, shared_w) in {"wg": (gu[:, :EI], i["L0_ffn_shared_gate_w"]),
                             "wu": (gu[:, EI:], i["L0_ffn_shared_up_w"])}.items():
        rows = np.concatenate([a.reshape(E * EI, P), np.asarray(shared_w)], 0)
        r[n] = np.ascontiguousarray(rows.T.reshape(P, FF, P))
    down = np.asarray(i["L0_ffn_experts_down"]).transpose(0, 2, 1).reshape(E * EI, P)
    down = np.concatenate([down, np.asarray(i["L0_ffn_shared_down_w"]).T], 0)
    r["wd"] = np.ascontiguousarray(down.reshape(FF, P, P).transpose(1, 0, 2))
    q, k, v, o = (np.asarray(i[f"L1_attn_{n}_w"]).T for n in "qkvo")
    r["w1"] = np.ascontiguousarray(np.stack([q[:, order], q[:, turned], k[:, order], k[:, turned], v, o], 1))
    qb, kb = np.asarray(i["L1_attn_q_b"]), np.asarray(i["L1_attn_k_b"])
    r["b1"] = np.ascontiguousarray(np.stack([qb[order], qb[turned], kb[order], kb[turned]], 1))
    r["v_b"], r["o_b"] = np.asarray(i["L1_attn_v_b"]), np.asarray(i["L1_attn_o_b"])
    r["qn"] = np.asarray(i["L1_attn_qn_scale"]).reshape(P, 1)
    r["kn"] = np.asarray(i["L1_attn_kn_scale"]).reshape(P, 1)
    inv = (1.0 / np.float32(10000.0) ** (np.arange(0, HD, 2, dtype=np.float32) / np.float32(HD))).astype(np.float32)
    freq = inv[dims % (HD // 2)][:, None] * np.arange(T, dtype=np.float32)[None, :]
    r["cos"] = np.cos(freq).astype(np.float32)
    r["sin"] = (np.sin(freq) * np.where(dims % 2, 1, -1)[:, None]).astype(np.float32)
    for n, a in (("fg", "gate"), ("fu", "up")):
        r[n] = np.ascontiguousarray(np.asarray(i["L1_ffn_w_" + a]).T.reshape(P, NH3, P))
    r["fd"] = np.ascontiguousarray(np.asarray(i["L1_ffn_w_down"]).T.reshape(NH3, P, P).transpose(1, 0, 2))
    return r


def kernel(**inputs):
    import concourse.bacc as _bacc
    from concourse import mybir as _mybir
    from concourse.bass_utils import run_bass_kernel_spmd as _run

    nc = _bacc.Bacc("TRN2", target_bir_lowering=False, num_devices=1)
    arrays, args = {}, []
    for name, a in layouts(inputs).items():
        arrays[f"in_{name}"] = a
        args.append(nc.dram_tensor(f"in_{name}", a.shape, _mybir.dt.from_np(a.dtype), kind="ExternalInput").ap())
    out = nc.dram_tensor("out_x", (NB, T, P), F32, kind="ExternalOutput").ap()
    program(nc, *args, out)
    r = _run(nc, [arrays], core_ids=[0])
    return r.results[0]["out_x"]
```

```python
from contextlib import ExitStack

import concourse.bass as bass
from concourse import mybir

F32 = mybir.dt.float32
F32R = mybir.dt.float32r
BF16 = mybir.dt.bfloat16
U32 = mybir.dt.uint32
I32 = mybir.dt.int32
ALU = mybir.AluOpType
ACT = mybir.ActivationFunctionType
AX = mybir.AxisListType

P = 128
NB = 8
T = 512
NT = T // P
H = 16
HD = P // H
HG = 4
NG = H // HG
CT = P // HG
PARTS = 3
QKR = PARTS * PARTS * HD
QKP = 96
MXR = QKP + PARTS
UN = 2
NU = NG * NT * (HG // UN)
PSLOTS = 4
NE = NG * NT
E = 32
EI = 64
NPAIR = E // 2
FF = NPAIR + 1
TOPG, TOPK, NGRP = 4, 6, 8
ROUTE_SCALE = 2.5
HID = 384
NH3 = HID // P
LN_EPS = 1e-5
RMS_EPS = 1e-8
RENORM_EPS = 1e-8
WEIGHT_SCALE = 1.0 / 127.0
S1_N = H * NT
FB = 3
LATE = 8
V_AT, Q_AT, K_AT = 16, 24, 34
MT_AT = (48, 11)
OT_AT = (29, 46, 62, 9)
STATS_AT, NORM_AT = 16, 21
LOOP_U = 12
LOOP_U1 = 16
V1_AT, RMS_AT, SCALE_AT = 2, 16, 19
FRONT_AT = (18, 20, 22, 24, 26, 28)
TURN_AT, ALL_AT, PROJECT_AT, NORM1_AT, X_AT = 4, 6, 8, 10, 15
HH = H // 2
ATT1_SHAPES = {"w": [P, 6, P], "bqk": [P, 4], "norm_scale": [P, 2], "vb": [P, P], "ob": [P, P], "cos": [P, T],
               "sin": [P, T]}
GUEST_AT = {"v": V_AT, "q": Q_AT, "k": K_AT, "max0": MT_AT[0], "max1": MT_AT[1],
            "o0": OT_AT[0], "o1": OT_AT[1], "o2": OT_AT[2], "o3": OT_AT[3]}
TURNS = [t for n in range(S1_N) for t in [g for g, at in GUEST_AT.items() if at == n] + [n]]
BANK = {t: i % FB for i, t in enumerate(TURNS)}


def exists(turn, b):
    if not isinstance(b, int):
        return True
    if isinstance(turn, int):
        first, last = (1, NB) if turn < LATE else (0, NB - 1)
    else:
        first, last = {"q": (0, NB - 2), "k": (0, NB - 2), "v": (0, NB - 1), "max0": (0, NB - 1),
                       "o3": (2, NB)}.get(turn, (1, NB))
    return first <= b <= last


def score_of(turn, b):
    return (b, turn + S1_N - LATE) if turn < LATE else (b + 1, turn - LATE)


def turn_before(turn, b):
    order = TURNS[:TURNS.index(turn)]
    for back in range(2):
        for t in reversed(order):
            if BANK[t] == BANK[turn] and exists(t, b - back):
                return t, back
        order = TURNS
    return None


def turns_of(u, second):
    return [t for n in s1_range(u, second) for t in TURNS if t == n or GUEST_AT.get(t) == n]


def s1_range(u, second):
    at = lambda k: -(-S1_N * k // (2 * NU))
    return range(at(2 * u + second), at(2 * u + second + 1))


def layernorm_buffers(ctx, nc, name):
    def sb(n, shape):
        return ctx.enter_context(nc.sbuf_tensor(f"{name}_{n}", shape, F32))

    def sem(n):
        return ctx.enter_context(nc.semaphore(f"{name}_{n}"))

    return {"st": sb("st", [P, NT, 6]), "mv": sb("mv", [P, NT, 2]), "ve": sb("ve", [P, NT]),
            "rstd": sb("rstd", [P, NT]), "gate": sb("gate", [P, 1]),
            "dve": sem("ln_dve"), "pool": sem("ln_pool"), "x_done": sem("x_done")}


def layernorm_stats(nc, dve, ln, b, y):
    for k in range(NT):
        nc.vector.bn_stats(ln["st"][:, k, :], y[:, k, :]).then_inc(ln["dve"], 1)
    dve.wait_ge(ln["dve"], 2 * NT * b + NT)
    nc.vector.memset(ln["gate"][:, :], 0.0)
    for k in range(NT):
        nc.vector.bn_aggr(ln["mv"][:, k, :], ln["st"][:, k, :]).then_inc(ln["dve"], 1)


def layernorm_apply(nc, dve, g, ln, b, y):
    X = g["X"]
    dve.wait_ge(ln["pool"], 2 * b + 2)
    for k in range(NT):
        ins = nc.vector.tensor_scalar(X[:, b, k, :], y[:, k, :], ln["mv"][:, k, 0:1], ln["rstd"][:, k:k + 1],
                                      ALU.subtract, ALU.mult)
    ins.then_inc(ln["x_done"], 1)


def layernorm_pool(nc, pool, g, ln, b):
    pool.wait_ge(ln["dve"], 2 * NT * (b + 1))
    nc.gpsimd.tensor_tensor(ln["ve"][:, :], ln["mv"][:, :, 1], g["eps"][:, :], ALU.add).then_inc(ln["pool"], 1)
    pool.wait_ge(ln["pool"], 2 * b + 1)
    nc.gpsimd.tensor_tensor(ln["rstd"][:, :], ln["ve"][:, :], g["neg_half"][:, :], ALU.pow).then_inc(ln["pool"], 1)


def split_in_parts(eng, ops, src, rest, parts, k, split, parts_done, zero=None):
    def copy(dst, a):
        if zero is None:
            return ops.tensor_copy(dst, a)
        return ops.tensor_tensor(dst, a, zero, ALU.add)

    copy(parts[:, 0, :], src).then_inc(split, 1)
    eng.wait_ge(split, 3 * k + 1)
    ops.tensor_tensor(rest, src, parts[:, 0, :], ALU.subtract).then_inc(split, 1)
    eng.wait_ge(split, 3 * k + 2)
    copy(parts[:, 1, :], rest).then_inc(split, 1)
    eng.wait_ge(split, 3 * k + 3)
    ops.tensor_tensor(parts[:, 2, :], rest, parts[:, 1, :], ALU.subtract).then_inc(parts_done, 1)


def walk(eng, units, loop_u=LOOP_U, qk_first=False):
    if qk_first:
        units(-2, 0, 0, NU, True, False, False, False)
    units(-1, 1, 0, NU, True, True, False, False)
    units(0, 0, 0, loop_u, False, True, True, False)
    with eng.Fori(0, (NB - 2) // 2) as i:
        for q in range(2):
            units(2 * i + q, q, loop_u, NU, True, True, True, False)
            units(2 * i + q + 1, 1 - q, 0, loop_u, False, True, True, True)
    units(NB - 2, 0, loop_u, NU, False, True, True, False)
    units(NB - 1, 1, 0, loop_u, False, False, True, True)
    units(NB - 1, 1, loop_u, NU, False, False, True, False)


def attention0(nc, g, x_t, w_qkv, load_more, more_in):
    X, ident = g["X"], g["ident"]
    scratch = [[nc.dram_tensor(f"parts_{n}{i}", [5, P, T], BF16).ap() for i in range(2)] for n in "qk"]
    with ExitStack() as ctx:
        def sb(name, shape, dt=F32):
            return ctx.enter_context(nc.sbuf_tensor("a0_" + name, shape, dt))

        def sem(name):
            return ctx.enter_context(nc.semaphore("a0_" + name))

        w = sb("w", [P, 3, P])
        xt = [sb(f"xt{i}", [P, T]) for i in range(2)]
        qk = sb("qk", [P, 2, T])
        rest = sb("rest", [P, 2, T])
        parts = sb("parts", [P, 2, PARTS, T], BF16)
        qs = [sb(f"qs{i}", [P, H, T], BF16) for i in range(2)]
        ks = [sb(f"ks{i}", [P, H, T], BF16) for i in range(2)]
        va = [sb(f"va{i}", [P, NT, H, CT]) for i in range(2)]
        prob = sb("prob", [P, PSLOTS, UN, T])
        osb = sb("osb", [P, 2, T])
        nmax = sb("nmax", [P, H, NT])
        mrest = sb("mrest", [HH * NT, P])
        mparts = sb("mparts", [HH * NT, PARTS, P], BF16)
        rec = sb("rec", [P, NT, HG])
        att = sb("att", [P, NT, P])
        ln = layernorm_buffers(ctx, nc, "a0")
        ps_s = ctx.enter_context(nc.psum_tensor("a0_ps_s", [P, 2, UN, T], F32))
        ps_f = ctx.enter_context(nc.psum_tensor("a0_ps_f", [P, FB, T], F32))
        ps_o = ctx.enter_context(nc.psum_tensor("a0_ps_o", [P, T], F32))

        w_in, x_in, xt_in = sem("w_in"), g["x_in"], [sem(f"xt_in{i}") for i in range(2)]
        cleared = sem("cleared")
        q_done, k_done, v_done = sem("q_done"), sem("k_done"), sem("v_done")
        q_taken, k_taken, v_taken = sem("q_taken"), sem("k_taken"), sem("v_taken")
        split, parts_done = sem("split"), sem("parts_done")
        parts_out, fill_in, max_in = sem("parts_out"), sem("fill_in"), sem("max_in")
        stack_in = [sem(f"stack_in{i}") for i in range(NG)]
        s1_done, max_done = sem("s1_done"), sem("max_done")
        mt_done, mt_chain, mt_split, mt_parts = (sem(f"mt_{n}") for n in ("done", "chain", "split", "parts"))
        s2_done, exp_done, pv_done = sem("s2_done"), sem("exp_done"), sem("pv_done")
        o_taken, ot_done, rec_done, att_done, sum_done = (
            sem(n) for n in ("o_taken", "ot_done", "rec_done", "att_done", "sum_done"))
        S2_C, EXP_C, PV_C, O_C, OT_C, ATT_C = NU, 2, PSLOTS // 2, 1, 2, 1
        PARTS_C, OUT_C, MAX_C = 2, 3 * 16, PARTS * 16

        block = ctx.enter_context(nc.Block())

        @block.sync
        def _(sp):
            def load_xt(b, p):
                sp.dma_start(xt[p][:, :], x_t[:, bass.ds(b * T, T)]).then_inc(xt_in[p], 16)

            def parts_to_dram(b, p):
                for n, seg in ((0, 0), (1, 0), (1, 1)):
                    if seg == 0:
                        sp.wait_ge(parts_done, 2 * b + n + 1 + PARTS_C)
                    dst = scratch[n][p].rearrange("r p t -> p r t")
                    if seg == 0:
                        sp.dma_start(dst[:, 0:PARTS, :], parts[:, n, :, :]).then_inc(parts_out, 16)
                    else:
                        sp.dma_start(dst[:, PARTS:5, :], parts[:, n, 0:2, :]).then_inc(parts_out, 16)

            def stack(b, p, grp, before=False):
                if before:
                    sp.wait_ge(s2_done, NU * (b - 2) + (grp + 1) * (NU // NG) + S2_C)
                for n, dst in ((0, qs), (1, ks)):
                    src = scratch[n][p]
                    src = bass.AP(tensor=src.tensor, offset=grp * HG * T,
                                  ap=[[n * HD * H * T, PARTS], [H * T, PARTS * HD], [1, HG * T]])
                    sp.dma_start(dst[p][0:QKR, grp * HG:(grp + 1) * HG, :], src).then_inc(stack_in[grp], 16)

            def max_rows(b, p, half_no):
                sp.wait_ge(mt_parts, 2 * b + half_no + 1)
                for r in range(PARTS):
                    sp.dma_start(qs[p][QKP + r:QKP + r + 1, half_no * HH:(half_no + 1) * HH, :],
                                 mparts[:, r, :]).then_inc(max_in, 16)

            def step(b, p, qk_on, front, back):
                if back:
                    max_rows(b, p, 1)
                if front and back:
                    stack(b + 1, 1 - p, NG - 1, True)
                if qk_on:
                    sp.wait_ge(v_done, b + 1)
                    load_xt(b + 2, p)
                    parts_to_dram(b + 2, p)
                if front:
                    max_rows(b + 1, 1 - p, 0)
                if qk_on:
                    sp.wait_ge(parts_out, 48 * (b + 3) + OUT_C)
                    for grp in range(NG - 1):
                        stack(b + 2, p, grp, True)

            load_xt(0, 0)
            sp.dma_start(w[:, :, :], w_qkv.rearrange("d (a c) -> d a c", a=3)).then_inc(w_in, 16)
            load_xt(1, 1)
            for i in range(2):
                for dst, value, r0, r1 in ((qs, 0, QKR, QKP), (ks, 0, QKR, QKP), (ks, 1, QKP, MXR)):
                    src = bass.AP(tensor=g["fill"].tensor, offset=value * H * T, ap=[[0, r1 - r0], [1, H * T]])
                    sp.dma_start(dst[i][r0:r1, :, :], src).then_inc(fill_in, 16)
            parts_to_dram(0, 0)
            sp.wait_ge(parts_out, 48 + OUT_C)
            for grp in range(NG):
                stack(0, 0, grp)
            sp.dma_start(X[:, :, :, :], g["x"].rearrange("b (k p) d -> p b k d", p=P)).then_inc(x_in, 16)
            parts_to_dram(1, 1)
            max_rows(0, 0, 0)
            sp.wait_ge(parts_out, 96 + OUT_C)
            for grp in range(NG - 1):
                stack(1, 1, grp)
            load_more(sp)
            with sp.Fori(0, (NB - 2) // 2) as i:
                step(2 * i, 0, True, True, True)
                step(2 * i + 1, 1, True, True, True)
            step(NB - 2, 0, False, True, True)
            step(NB - 1, 1, False, False, True)
            more_in(sp)

        @block.scalar
        def _(act):
            def take(dst, src, ready, value, done):
                act.wait_ge(ready, value)
                nc.scalar.activation(dst, src, ACT.Copy).then_inc(done, 1)

            def take_v(b, p):
                take(va[p][:, :, :, 0:HD],
                     ps_f[:, BANK["v"], :].rearrange("p (k h d) -> p k h d", k=NT, h=H), v_done, b + 1, v_taken)

            def take_qk(b, n):
                act.wait_ge(parts_done, 2 * b + n - 1 + PARTS_C)
                take(qk[:, n, :], ps_f[:, BANK["qk"[n]], :], (q_done, k_done)[n], b + 1, (q_taken, k_taken)[n])

            def take_o(b, grp):
                act.wait_ge(ot_done, NG * b + grp - 1 + OT_C)
                take(osb[:, grp % 2, :], ps_o[:, :], pv_done, NE * b + NT * (grp + 1) + PV_C, o_taken)

            def units(b, p, u0, u1, qk_on, front, back, tail):
                for u in range(u0, u1):
                    if back:
                        act.wait_ge(s2_done, NU * b + u + 1 + S2_C)
                        if u % 2 == 0:
                            act.wait_ge(pv_done, NE * b + u // 2 - PSLOTS // 2 + 1 + PV_C)
                        nc.scalar.activation(prob[:, u % PSLOTS, :, :], ps_s[:, u % 2, :, :], ACT.Exp,
                                             scale=float(P) ** -0.5).then_inc(exp_done, 1)
                    for second in range(2):
                        if second and u % 8 == 1 and (back if u > 8 else tail):
                            take_o(*((b, u // 8 - 1) if u > 8 else (b - 1, NG - 1)))
                        for t in turns_of(u, second):
                            if front and t == "v":
                                take_v(b + 1, 1 - p)
                            if qk_on and t == "q":
                                take_qk(b + 2, 0)
                            if qk_on and t == "k":
                                take_qk(b + 2, 1)

            act.sem_inc(exp_done, EXP_C)
            act.sem_inc(o_taken, O_C)
            act.wait_ge(cleared, 4)
            take_qk(0, 0)
            take_qk(0, 1)
            walk(act, units)
            take_o(NB - 1, NG - 1)

        @block.tensor
        def _(pe):
            pe.sem_inc(s2_done, S2_C)
            pe.sem_inc(pv_done, PV_C)
            pe.sem_inc(ot_done, OT_C)
            pe.wait_ge(w_in, 16)

            def turn_max(b, half_no):
                pe.wait_ge(max_done, S1_N * b + HH * NT * (half_no + 1))
                nc.tensor.transpose(ps_f[0:HH * NT, BANK[f"max{half_no}"], 0:P], nmax[:, half_no * HH:(half_no + 1) * HH, :],
                                    ident[:, :]).then_inc(mt_done, 1)

            def v_product(b, p):
                pe.wait_ge(xt_in[p], 8 * (b - p) + 16)
                for kt in range(NT):
                    mm = nc.tensor.matmul(ps_f[:, BANK["v"], kt * P:(kt + 1) * P], xt[p][:, kt * P:(kt + 1) * P],
                                          w[:, 2, :], start=True, stop=True)
                mm.then_inc(v_done, 1)

            def qk_product(b, p, n):
                pe.wait_ge(xt_in[p], 8 * (b - p) + 16)
                nc.tensor.matmul(ps_f[:, BANK["qk"[n]], :], w[:, n, :], xt[p][:, :], start=True,
                                 stop=True).then_inc((q_done, k_done)[n], 1)

            def s1(b, p, n, bank):
                h, qt = n // NT, n % NT
                if n % (S1_N // NG) == 0:
                    pe.wait_ge(stack_in[h // HG], 32 * (b + 1))
                nc.tensor.matmul(ps_f[:, bank, :], qs[p][0:QKP, h, qt * P:(qt + 1) * P], ks[p][0:QKP, h, :],
                                 start=True, stop=True).then_inc(s1_done, 1)

            def free_bank(b, t):
                before = turn_before(t, b)
                if before is None:
                    return
                t, b = before[0], b - before[1]
                if isinstance(t, int):
                    pe.wait_ge(max_done, S1_N * b + t - LATE + 1)
                elif t in "qk":
                    pe.wait_ge(q_taken if t == "q" else k_taken, b + 2)
                elif t == "v":
                    pe.wait_ge(v_taken, b + 1)
                elif t in ("max0", "max1"):
                    pe.wait_ge(mt_split, 2 * b + (t == "max0"))
                else:
                    pe.wait_ge(att_done, NG * (b - 1) + (int(t[1]) + 1) % NG + ATT_C)

            def take_turn(b, p, t, qk_on, front, back, tail):
                if isinstance(t, int):
                    if back if t < LATE else front:
                        free_bank(b, t)
                        score_b, n = score_of(t, b - 1)
                        s1(score_b, 1 - p if t < LATE else p, n, BANK[t])
                elif t == "v":
                    if front:
                        free_bank(b, t)
                        v_product(b, p)
                elif t in "qk":
                    if qk_on:
                        free_bank(b, t)
                        qk_product(b + 1, 1 - p, "qk".index(t))
                elif t == "max0":
                    if front:
                        free_bank(b, t)
                        turn_max(b, 0)
                elif t == "max1":
                    if back:
                        free_bank(b, t)
                        turn_max(b - 1, 1)
                elif t == "o3":
                    if tail:
                        free_bank(b, t)
                        turn_o(b - 2, NG - 1)
                elif back:
                    free_bank(b, t)
                    turn_o(b - 1, int(t[1]))

            def s2(b, p, u):
                grp, kt, pair = u // (2 * NT), u // 2 % NT, u % 2
                if u in (0, NU // 2):
                    pe.wait_ge(max_in, MAX_C * (2 * b + u // (NU // 2) + 1) + MAX_C)
                pe.wait_ge(exp_done, NU * b + u - 1 + EXP_C)
                for i in range(UN):
                    h = grp * HG + pair * UN + i
                    mm = nc.tensor.matmul(ps_s[:, u % 2, i, :], ks[p][0:MXR, h, kt * P:(kt + 1) * P],
                                          qs[p][0:MXR, h, :], start=True, stop=True)
                mm.then_inc(s2_done, 1)

            def pv(b, p, e):
                grp, kt = e // NT, e % NT
                if e == 0:
                    pe.wait_ge(v_taken, b + 1)
                if kt == 0:
                    pe.wait_ge(o_taken, NG * b + grp + O_C)
                pe.wait_ge(exp_done, NU * b + 2 * e + 2 + EXP_C)
                for j in range(HG):
                    mm = nc.tensor.matmul(ps_o[j * CT:(j + 1) * CT, :], va[p][:, kt, grp * HG + j, :],
                                          prob[:, (2 * e + j // UN) % PSLOTS, j % UN, :],
                                          start=(kt == 0), stop=(kt == NT - 1))
                mm.then_inc(pv_done, 1)

            def turn_o(b, grp):
                pe.wait_ge(o_taken, NG * b + grp + 1 + O_C)
                for qt in range(NT):
                    mm = nc.tensor.transpose(ps_f[:, BANK[f"o{grp}"], qt * P:(qt + 1) * P],
                                             osb[:, grp % 2, qt * P:(qt + 1) * P], ident[:, :])
                mm.then_inc(ot_done, 1)

            def units(b, p, u0, u1, qk_on, front, back, tail):
                for u in range(u0, u1):
                    if back:
                        s2(b, p, u)
                    for second in range(2):
                        if second and u % 2 and (back if u > 1 else tail):
                            if u > 1:
                                pv(b, p, u // 2 - 1)
                            else:
                                pv(b - 1, 1 - p, NE - 1)
                        for t in turns_of(u, second):
                            take_turn(b + 1, 1 - p, t, qk_on, front, back, tail)

            qk_product(0, 0, 0)
            if BANK["q"] == BANK["k"]:
                pe.wait_ge(q_taken, 1)
            qk_product(0, 0, 1)
            pe.wait_ge(q_taken, 1)
            pe.wait_ge(k_taken, 1)
            pe.wait_ge(g["consts_in"], 16)
            pe.wait_ge(fill_in, 6 * 16)
            walk(pe, units)
            pv(NB - 1, 1, NE - 1)
            pe.wait_ge(att_done, NG * NB - 1 + ATT_C)
            turn_o(NB - 1, NG - 1)

        @block.vector
        def _(dve):
            dve.sem_inc(max_in, MAX_C)
            dve.sem_inc(att_done, ATT_C)

            for i in range(2):
                nc.vector.memset(va[i][:, :, :, HD + 1:CT], 0.0).then_inc(cleared, 1)
                nc.vector.memset(va[i][:, :, :, HD:HD + 1], 1.0).then_inc(cleared, 1)

            def reduce_max(b, n, bank):
                dve.wait_ge(s1_done, S1_N * b + n + 1)
                nc.vector.tensor_reduce(nmax[:, n // NT, n % NT:n % NT + 1], ps_f[:, bank, :], AX.X, ALU.max,
                                        negate=True).then_inc(max_done, 1)

            def split_max(b, half_no):
                k = 2 * b + half_no
                src = ps_f[0:HH * NT, BANK[f"max{half_no}"], 0:P]
                dve.wait_ge(max_in, MAX_C * k + MAX_C)
                dve.wait_ge(mt_done, k + 1)
                nc.vector.tensor_copy(mparts[:, 0, :], src).then_inc(mt_chain, 1)
                dve.wait_ge(mt_chain, 2 * k + 1)
                nc.vector.tensor_tensor(mrest[:, :], src, mparts[:, 0, :], ALU.subtract).then_inc(mt_split, 1)
                dve.wait_ge(mt_split, k + 1)
                nc.vector.tensor_copy(mparts[:, 1, :], mrest[:, :]).then_inc(mt_chain, 1)
                dve.wait_ge(mt_chain, 2 * k + 2)
                nc.vector.tensor_tensor(mparts[:, 2, :], mrest[:, :], mparts[:, 1, :],
                                        ALU.subtract).then_inc(mt_parts, 1)

            def divide(b, grp):
                o = ps_f[:, BANK[f"o{grp}"], :].rearrange("p (k j c) -> p k j c", k=NT, c=CT)
                dve.wait_ge(ot_done, NG * b + grp + 1 + OT_C)
                dve.wait_ge(att_done, NG * b + grp + ATT_C)
                nc.vector.reciprocal(rec[:, :, :], o[:, :, :, HD]).then_inc(rec_done, 1)
                dve.wait_ge(rec_done, NG * b + grp + 1)
                dst = att[:, :, grp * HG * HD:(grp + 1) * HG * HD].rearrange("p k (j c) -> p k j c", c=HD)
                nc.vector.tensor_tensor(dst, o[:, :, :, 0:HD],
                                        rec[:, :, :].unsqueeze(3).broadcast_to([P, NT, HG, HD]),
                                        ALU.mult).then_inc(att_done, 1)

            def stats(b):
                dve.wait_ge(sum_done, b + 1)
                layernorm_stats(nc, dve, ln, b, att)

            def units(b, p, u0, u1, qk_on, front, back, tail):
                for u in range(u0, u1):
                    for second in range(2):
                        for t in turns_of(u, second):
                            if front and t == "max0":
                                split_max(b + 1, 0)
                            if back and t == "max1":
                                split_max(b, 1)
                            if back and t in ("o0", "o1", "o2"):
                                divide(b, int(t[1]))
                            if tail and t == "o3":
                                divide(b - 1, NG - 1)
                            if tail and t == STATS_AT:
                                stats(b - 1)
                            if tail and t == NORM_AT:
                                layernorm_apply(nc, dve, g, ln, b - 1, att)
                            if isinstance(t, int) and (back if t < LATE else front):
                                reduce_max(*score_of(t, b), BANK[t])

            for n in range(2):
                dve.wait_ge((q_taken, k_taken)[n], 1)
                split_in_parts(dve, nc.vector, qk[:, n, :], rest[:, n, :], parts[:, n, :, :], n, split, parts_done)
            walk(dve, units)
            divide(NB - 1, NG - 1)
            stats(NB - 1)
            layernorm_apply(nc, dve, g, ln, NB - 1, att)

        @block.gpsimd
        def _(pool):
            pool.sem_inc(parts_done, PARTS_C)
            pool.sem_inc(parts_out, OUT_C)

            def add_x(b):
                pool.wait_ge(att_done, NG * (b + 1) + ATT_C)
                nc.gpsimd.tensor_tensor(att[:, :, :], att[:, :, :], X[:, b, :, :], ALU.add).then_inc(sum_done, 1)

            def split_qk(b, n):
                pool.wait_ge(parts_out, OUT_C * b + OUT_C)
                pool.wait_ge((q_taken, k_taken)[n], b + 1)
                split_in_parts(pool, nc.gpsimd, qk[:, n, :], rest[:, n, :], parts[:, n, :, :], 2 * b + n, split,
                               parts_done, g["zero"][:, :].broadcast_to([P, T]))

            def units(b, p, u0, u1, qk_on, front, back, tail):
                if u0 == 0 and tail:
                    add_x(b - 1)
                    layernorm_pool(nc, pool, g, ln, b - 1)
                if u1 == NU and qk_on:
                    split_qk(b + 2, 0)
                    split_qk(b + 2, 1)

            pool.wait_ge(x_in, 16)
            walk(pool, units)
            add_x(NB - 1)
            layernorm_pool(nc, pool, g, ln, NB - 1)


def attention1(nc, g, c, xh, xl, ff):
    X, ident = g["X"], g["ident"]
    scratch = [[nc.dram_tensor(f"parts1_{n}{i}", [5, P, T], BF16).ap() for i in range(2)] for n in "qk"]
    with ExitStack() as ctx:
        def sb(name, shape, dt=F32):
            return ctx.enter_context(nc.sbuf_tensor("a1_" + name, shape, dt))

        def sem(name):
            return ctx.enter_context(nc.semaphore("a1_" + name))

        w, bqk, norm_scale, vb, ob, cos, sin = (c[n] for n in ATT1_SHAPES)
        xb = sb("xb", [P, NT, P])
        xn = xb
        xr = sb("xr", [P, NT, P])
        ms = sb("ms", [P, NT])
        rr = sb("rr", [P, NT])
        xrh, xrl = sb("xrh", [P, T], F32R), sb("xrl", [P, T], F32R)
        wh, wl = sb("wh", [P, 4, P], F32R), sb("wl", [P, 4, P], F32R)
        turned = sb("turned", [P, 2, T])
        att_t = sb("att_t", [P, T])
        xt = [sb(f"xt{i}", [P, T]) for i in range(2)]
        qk = sb("qk", [P, 2, T])
        rest = sb("rest", [P, T])
        parts = sb("parts", [P, 2, PARTS, T], BF16)
        qs = [sb(f"qs{i}", [P, H, T], BF16) for i in range(2)]
        ks = [sb(f"ks{i}", [P, H, T], BF16) for i in range(2)]
        va = [sb(f"va{i}", [P, NT, H, CT]) for i in range(2)]
        prob = sb("prob", [P, PSLOTS, UN, T])
        osb = sb("osb", [P, 2, T])
        rec = sb("rec", [P, NT, HG])
        att = sb("att", [P, NT, P])
        ln = layernorm_buffers(ctx, nc, "a1")
        ps_s = ctx.enter_context(nc.psum_tensor("a1_ps_s", [P, 2, UN, T], F32))
        ps_f = ctx.enter_context(nc.psum_tensor("a1_ps_f", [P, 2, T], F32))
        ps_o = ctx.enter_context(nc.psum_tensor("a1_ps_o", [P, T], F32))
        ps_t = ctx.enter_context(nc.psum_tensor("a1_ps_t", [P, NT, P], F32))

        fill_in, w_scaled, cleared = sem("fill_in"), sem("w_scaled"), sem("cleared")
        x_step, x_pow, xr_done = sem("x_step"), sem("x_pow"), sem("xr_done")
        xrh_done = sem("xrh_done")
        f_done, f_taken, rope_step, rope_done = sem("f_done"), sem("f_taken"), sem("rope_step"), sem("rope_done")
        v_done, v_taken, split, parts_done = sem("v_done"), sem("v_taken"), sem("split"), sem("parts_done")
        parts_out, stack_in = sem("parts_out"), [[sem(f"stack_in{i}{j}") for j in range(NG)] for i in range(2)]
        at_done, at_taken, y_done, y_taken = sem("at_done"), sem("at_taken"), sem("y_done"), sem("y_taken")
        xn_done, x_turned, x_hi, x_parted = sem("xn_done"), sem("x_turned"), sem("x_hi"), sem("x_parted")
        s2_done, exp_done, pv_done = sem("s2_done"), sem("exp_done"), sem("pv_done")
        o_taken, ot_done, rec_done, att_done, sum_done = (
            sem(n) for n in ("o_taken", "ot_done", "rec_done", "att_done", "sum_done"))
        S2_C, EXP_C, PV_C, O_C, OT_C, ATT_C = NU, 2, PSLOTS // 2, 1, 2, 1
        PARTS_C, OUT_C = 2, 3 * 16
        FN = 6
        Y_C, R_C, XP_C = 1, 1, 1

        block = ctx.enter_context(nc.Block())

        @block.sync
        def _(sp):
            def parts_to_dram(b, p):
                for n, seg in ((0, 0), (1, 0), (1, 1)):
                    if seg == 0:
                        sp.wait_ge(parts_done, 2 * b + n + 1 + PARTS_C)
                    dst = scratch[n][p].rearrange("r p t -> p r t")
                    if seg == 0:
                        sp.dma_start(dst[:, 0:PARTS, :], parts[:, n, :, :]).then_inc(parts_out, 16)
                    else:
                        sp.dma_start(dst[:, PARTS:5, :], parts[:, n, 0:2, :]).then_inc(parts_out, 16)

            def stack(b, p):
                sp.wait_ge(parts_out, 48 * (b + 1) + OUT_C)
                for grp in range(NG):
                    for n, dst in ((0, qs), (1, ks)):
                        src = scratch[n][p]
                        src = bass.AP(tensor=src.tensor, offset=grp * HG * T,
                                      ap=[[n * HD * H * T, PARTS], [H * T, PARTS * HD], [1, HG * T]])
                        sp.dma_start(dst[p][0:QKR, grp * HG:(grp + 1) * HG, :], src).then_inc(stack_in[p][grp], 16)

            def step(b, p, qk_on, front):
                if front:
                    sp.wait_ge(s2_done, NU * b + S2_C)
                    stack(b + 1, 1 - p)
                if qk_on:
                    parts_to_dram(b + 2, p)

            for i in range(2):
                for dst in (qs, ks):
                    src = bass.AP(tensor=g["fill"].tensor, offset=0, ap=[[0, QKP - QKR], [1, H * T]])
                    sp.dma_start(dst[i][QKR:QKP, :, :], src).then_inc(fill_in, 16)
            parts_to_dram(0, 0)
            stack(0, 0)
            for src, ints, _, _ in ff["weights"]:
                sp.dma_start(ints[:, :, :], src).then_inc(ff["in"], 16)
            parts_to_dram(1, 1)
            with sp.Fori(0, (NB - 2) // 2) as i:
                step(2 * i, 0, True, True)
                step(2 * i + 1, 1, True, True)
            step(NB - 2, 0, False, True)

        @block.scalar
        def _(act):
            def take(dst, src, ready, value, done):
                act.wait_ge(ready, value)
                nc.scalar.activation(dst, src, ACT.Copy).then_inc(done, 1)

            def take_o(b, grp):
                act.wait_ge(ot_done, NG * b + grp - 1 + OT_C)
                take(osb[:, grp % 2, :], ps_o[:, :], pv_done, NE * b + NT * (grp + 1) + PV_C, o_taken)

            def units(b, p, u0, u1, qk_on, front, back, tail):
                for u in range(u0, u1):
                    if back:
                        act.wait_ge(s2_done, NU * b + u + 1 + S2_C)
                        if u % 2 == 0:
                            act.wait_ge(pv_done, NE * b + u // 2 - PSLOTS // 2 + 1 + PV_C)
                        nc.scalar.activation(prob[:, u % PSLOTS, :, :], ps_s[:, u % 2, :, :], ACT.Sigmoid,
                                             scale=float(HD) ** -0.5).then_inc(exp_done, 1)
                    if u % 8 == 1 and (back if u > 8 else tail):
                        take_o(*((b, u // 8 - 1) if u > 8 else (b - 1, NG - 1)))

            act.sem_inc(exp_done, EXP_C)
            act.sem_inc(o_taken, O_C)
            walk(act, units, LOOP_U1, True)
            take_o(NB - 1, NG - 1)

        @block.tensor
        def _(pe):
            pe.sem_inc(s2_done, S2_C)
            pe.sem_inc(pv_done, PV_C)
            pe.sem_inc(ot_done, OT_C)
            pe.wait_ge(w_scaled, 4)

            def v_product(b, p):
                pe.wait_ge(f_taken, FN * (b + 1))
                for kt in range(NT):
                    mm = nc.tensor.matmul(ps_f[:, 1, kt * P:(kt + 1) * P], xt[p][:, kt * P:(kt + 1) * P],
                                          w[:, 4, :], start=True, stop=True)
                mm.then_inc(v_done, 1)

            def front_use(b, p, k, v_too):
                if k == 0:
                    pe.wait_ge(x_step, 4 * b + 1)
                elif k == 1:
                    pe.wait_ge(xr_done, b + 1)
                    if v_too:
                        pe.wait_ge(v_taken, b)
                if k >= 2:
                    pe.wait_ge(f_taken, FN * b + max(k - 1, 2))
                if k < 2:
                    src = (xb, xr)[k]
                    for kt in range(NT):
                        mm = nc.tensor.transpose(ps_f[:, k, kt * P:(kt + 1) * P], src[:, kt, :], g["ident"][:, :])
                else:
                    dst = ps_f[:, k % 2, :]
                    nc.tensor.matmul(dst, wh[:, k - 2, :], xrh[:, :], start=True, stop=False)
                    nc.tensor.matmul(dst, wl[:, k - 2, :], xrh[:, :], start=False, stop=False)
                    mm = nc.tensor.matmul(dst, wh[:, k - 2, :], xrl[:, :], start=False, stop=True)
                mm.then_inc(f_done, 1)

            def s2(b, p, u):
                grp, kt, pair = u // (2 * NT), u // 2 % NT, u % 2
                if u % (2 * NT) == 0:
                    pe.wait_ge(stack_in[p][grp], 16 * (b - p) + 32)
                pe.wait_ge(exp_done, NU * b + u - 1 + EXP_C)
                for i in range(UN):
                    h = grp * HG + pair * UN + i
                    mm = nc.tensor.matmul(ps_s[:, u % 2, i, :], ks[p][0:QKP, h, kt * P:(kt + 1) * P],
                                          qs[p][0:QKP, h, :], start=True, stop=True)
                mm.then_inc(s2_done, 1)

            def pv(b, p, e):
                grp, kt = e // NT, e % NT
                if e == 0:
                    pe.wait_ge(v_taken, b + 1)
                if kt == 0:
                    pe.wait_ge(o_taken, NG * b + grp + O_C)
                pe.wait_ge(exp_done, NU * b + 2 * e + 2 + EXP_C)
                for j in range(HG):
                    mm = nc.tensor.matmul(ps_o[j * CT:(j + 1) * CT, :], va[p][:, kt, grp * HG + j, :],
                                          prob[:, (2 * e + j // UN) % PSLOTS, j % UN, :],
                                          start=(kt == 0), stop=(kt == NT - 1))
                mm.then_inc(pv_done, 1)

            def turn_o(b, grp):
                pe.wait_ge(o_taken, NG * b + grp + 1 + O_C)
                if grp == 0:
                    pe.wait_ge(y_taken, b + Y_C)
                elif grp == 1:
                    pe.wait_ge(x_parted, b + XP_C)
                else:
                    pe.wait_ge(att_done, NG * b + grp + ATT_C)
                for qt in range(NT):
                    mm = nc.tensor.transpose(ps_t[:, qt, :], osb[:, grp % 2, qt * P:(qt + 1) * P], ident[:, :])
                mm.then_inc(ot_done, 1)

            def turn_all(b):
                pe.wait_ge(att_done, NG * (b + 1) + ATT_C)
                for kt in range(NT):
                    mm = nc.tensor.transpose(ps_t[:, kt, :], att[:, kt, :], ident[:, :])
                mm.then_inc(at_done, 1)

            def project(b):
                pe.wait_ge(at_taken, b + 1)
                for kt in range(NT):
                    mm = nc.tensor.matmul(ps_t[:, kt, :], att_t[:, kt * P:(kt + 1) * P], w[:, 5, :],
                                          start=True, stop=True)
                mm.then_inc(y_done, 1)

            def turn_x_next(b, held):
                pe.wait_ge(xn_done, b + 1)
                pe.wait_ge(att_done, held)
                for kt in range(NT):
                    mm = nc.tensor.transpose(ps_t[:, kt, :], xn[:, kt, :], ident[:, :])
                mm.then_inc(x_turned, 1)

            def units(b, p, u0, u1, qk_on, front, back, tail):
                if isinstance(b, int) and b == 0 and u0 == 0:
                    pe.wait_ge(fill_in, 4 * 16)
                for u in range(u0, u1):
                    if front and u == V1_AT:
                        v_product(b + 1, 1 - p)
                    if back:
                        s2(b, p, u)
                    if u % 2 == 1 and (back if u > 1 else tail):
                        pv(*((b, p, u // 2 - 1) if u > 1 else (b - 1, 1 - p, NE - 1)))
                    if u % 8 == TURN_AT and (back if u > 8 else tail):
                        turn_o(*((b, u // 8 - 1) if u > 8 else (b - 1, NG - 1)))
                    if u == ALL_AT and tail:
                        turn_all(b - 1)
                    if u == PROJECT_AT and tail:
                        project(b - 1)
                    if u == X_AT and tail:
                        turn_x_next(b - 1, NG * b + 1 + ATT_C)
                    if u in FRONT_AT and qk_on:
                        front_use(b + 2, p, FRONT_AT.index(u), front)

            walk(pe, units, LOOP_U1, True)
            pv(NB - 1, 1, NE - 1)
            turn_o(NB - 1, NG - 1)
            turn_all(NB - 1)
            project(NB - 1)
            pe.wait_ge(y_taken, NB + Y_C)
            turn_x_next(NB - 1, NG * NB + ATT_C)

        @block.vector
        def _(dve):
            dve.sem_inc(y_taken, Y_C)
            dve.sem_inc(x_parted, XP_C)
            dve.sem_inc(rope_done, R_C)
            dve.sem_inc(att_done, ATT_C)

            for n in range(2):
                nc.vector.tensor_scalar(w[:, 2 * n:2 * n + 2, :], w[:, 2 * n:2 * n + 2, :], norm_scale[:, n:n + 1],
                                        None, ALU.mult).then_inc(w_scaled, 1)
            dve.wait_ge(w_scaled, 2)
            nc.vector.tensor_copy(wh[:, :, :], w[:, 0:4, :]).then_inc(w_scaled, 1)
            dve.wait_ge(w_scaled, 3)
            nc.vector.tensor_tensor(wl[:, :, :], w[:, 0:4, :], wh[:, :, :], ALU.subtract).then_inc(w_scaled, 1)

            def rms(b):
                c = 4 * b
                nc.vector.tensor_copy(xb[:, :, :], X[:, b, :, :]).then_inc(x_step, 1)
                dve.wait_ge(x_step, c + 1)
                nc.vector.tensor_tensor(xr[:, :, :], xb[:, :, :], xb[:, :, :], ALU.mult).then_inc(x_step, 1)
                dve.wait_ge(x_step, c + 2)
                nc.vector.tensor_reduce(ms[:, :], xr[:, :, :], AX.X, ALU.add).then_inc(x_step, 1)
                dve.wait_ge(x_step, c + 3)
                nc.vector.tensor_scalar(ms[:, :], ms[:, :], 1.0 / P, RMS_EPS, ALU.mult, ALU.add).then_inc(x_step, 1)

            def scale_x(b):
                dve.wait_ge(x_pow, b + 1)
                nc.vector.tensor_tensor(xr[:, :, :], xb[:, :, :],
                                        rr[:, :].unsqueeze(2).broadcast_to([P, NT, P]), ALU.mult).then_inc(xr_done, 1)

            def take_front(b, p, k):
                dve.wait_ge(f_done, FN * b + k + 1)
                if k == 0:
                    nc.vector.tensor_copy(xt[p][:, :], ps_f[:, k, :]).then_inc(f_taken, 1)
                    return
                if k == 1:
                    nc.vector.tensor_copy(xrh[:, :], ps_f[:, k, :]).then_inc(xrh_done, 1)
                    dve.wait_ge(xrh_done, b + 1)
                    nc.vector.tensor_tensor(xrl[:, :], ps_f[:, k, :], xrh[:, :], ALU.subtract).then_inc(f_taken, 1)
                    return
                n = (k - 2) // 2
                if k % 2 == 0:
                    dve.wait_ge(parts_done, 2 * b + n - 1 + PARTS_C)
                    dve.wait_ge(rope_done, 2 * b + n + R_C)
                nc.vector.scalar_tensor_tensor(turned[:, k % 2, :], ps_f[:, k % 2, :], bqk[:, k - 2:k - 1],
                                               (cos, sin)[k % 2][:, :], ALU.add, ALU.mult).then_inc(f_taken, 1)
                if k % 2:
                    dve.wait_ge(f_taken, FN * b + k + 1)
                    nc.vector.tensor_tensor(qk[:, n, :], turned[:, 0, :], turned[:, 1, :],
                                            ALU.add).then_inc(rope_done, 1)

            def take_v(b, p):
                if not isinstance(b, int) or b >= 2:
                    dve.wait_ge(pv_done, NE * (b - 1) + PV_C)
                dve.wait_ge(v_done, b + 1)
                nc.vector.tensor_tensor(va[p][:, :, :, 0:HD],
                                        ps_f[:, 1, :].rearrange("p (k h d) -> p k h d", k=NT, h=H),
                                        vb[:, :].rearrange("p (h d) -> p h d", h=H).unsqueeze(1).broadcast_to(
                                            [P, NT, H, HD]), ALU.add).then_inc(v_taken, 1)

            def divide(b, grp):
                o = ps_t[:, :, :].rearrange("p k (j c) -> p k j c", c=CT)
                dve.wait_ge(ot_done, NG * b + grp + 1 + OT_C)
                nc.vector.tensor_scalar_add(rec[:, :, :], o[:, :, :, HD], RENORM_EPS).then_inc(rec_done, 1)
                dve.wait_ge(rec_done, 2 * (NG * b + grp) + 1)
                nc.vector.reciprocal(rec[:, :, :], rec[:, :, :]).then_inc(rec_done, 1)
                dve.wait_ge(rec_done, 2 * (NG * b + grp) + 2)
                dst = att[:, :, grp * HG * HD:(grp + 1) * HG * HD].rearrange("p k (j c) -> p k j c", c=HD)
                nc.vector.tensor_tensor(dst, o[:, :, :, 0:HD],
                                        rec[:, :, :].unsqueeze(3).broadcast_to([P, NT, HG, HD]),
                                        ALU.mult).then_inc(att_done, 1)

            def take_all(b):
                dve.wait_ge(at_done, b + 1)
                nc.vector.tensor_copy(att_t[:, :], ps_t[:, :, :]).then_inc(at_taken, 1)

            def add_x(b):
                dve.wait_ge(y_done, b + 1)
                nc.vector.tensor_tensor(att[:, :, :], ps_t[:, :, :],
                                        ob[:, :].unsqueeze(1).broadcast_to([P, NT, P]), ALU.add).then_inc(y_taken, 1)
                dve.wait_ge(y_taken, b + 1 + Y_C)
                nc.vector.tensor_tensor(att[:, :, :], att[:, :, :], X[:, b, :, :], ALU.add).then_inc(sum_done, 1)
                dve.wait_ge(sum_done, b + 1)
                layernorm_stats(nc, dve, ln, b, att)

            def split_first(n):
                dve.wait_ge(rope_done, n + 1 + R_C)
                split_in_parts(dve, nc.vector, qk[:, n, :], rest[:, :], parts[:, n, :, :], n, split, parts_done)

            def norm(b):
                layernorm_apply(nc, dve, g, ln, b, att)
                dve.wait_ge(ln["x_done"], b + 1)
                nc.vector.memset(ln["gate"][:, :], 0.0)
                nc.vector.tensor_copy(xn[:, :, :], X[:, b, :, :]).then_inc(xn_done, 1)

            def part_x(b):
                src = ps_t[:, :, :].rearrange("p k d -> p (k d)")
                dve.wait_ge(x_turned, b + 1)
                nc.vector.memset(ln["gate"][:, :], 0.0)
                nc.vector.tensor_copy(xh[:, b, :], src).then_inc(x_hi, 1)
                dve.wait_ge(x_hi, b + 1)
                nc.vector.tensor_tensor(xl[:, b, :], src, xh[:, b, :], ALU.subtract).then_inc(x_parted, 1)

            def units(b, p, u0, u1, qk_on, front, back, tail):
                if isinstance(b, int) and b == 0 and u0 == 0:
                    dve.wait_ge(rope_done, 4 + R_C)
                    prepare_ffn_weights(nc, dve, ff, turned[:, 0, 0:HID].rearrange("p (n d) -> p n d", n=NH3))
                for u in range(u0, u1):
                    if front and u == V1_AT:
                        take_v(b + 1, 1 - p)
                    if u % 8 == TURN_AT and (back if u > 8 else tail):
                        divide(*((b, u // 8 - 1) if u > 8 else (b - 1, NG - 1)))
                    if u == ALL_AT and tail:
                        take_all(b - 1)
                    if u == PROJECT_AT and tail:
                        add_x(b - 1)
                    if u == NORM1_AT and tail:
                        norm(b - 1)
                    if u == X_AT and tail:
                        part_x(b - 1)
                    if u == RMS_AT and qk_on:
                        rms(b + 2)
                    if u == SCALE_AT and qk_on:
                        scale_x(b + 2)
                    if u in FRONT_AT and qk_on:
                        take_front(b + 2, p, FRONT_AT.index(u))
                        if isinstance(b, int) and b == -2 and u in FRONT_AT[3::2]:
                            split_first(FRONT_AT.index(u) // 2 - 1)
                if isinstance(b, int) and b == -2:
                    dve.wait_ge(cleared, 4)

            walk(dve, units, LOOP_U1, True)
            divide(NB - 1, NG - 1)
            take_all(NB - 1)
            add_x(NB - 1)
            norm(NB - 1)
            part_x(NB - 1)

        @block.gpsimd
        def _(pool):
            pool.sem_inc(parts_done, PARTS_C)
            pool.sem_inc(parts_out, OUT_C)

            def split_qk(b, n):
                pool.wait_ge(parts_out, OUT_C * b + OUT_C)
                pool.wait_ge(rope_done, 2 * b + n + 1 + R_C)
                split_in_parts(pool, nc.gpsimd, qk[:, n, :], rest[:, :], parts[:, n, :, :], 2 * b + n, split,
                               parts_done, g["zero"][:, :].broadcast_to([P, T]))

            def units(b, p, u0, u1, qk_on, front, back, tail):
                if u0 == 0 and tail:
                    layernorm_pool(nc, pool, g, ln, b - 1)
                if u1 == NU and qk_on:
                    pool.wait_ge(x_step, 4 * (b + 3))
                    nc.gpsimd.tensor_tensor(rr[:, :], ms[:, :], g["neg_half"][:, :], ALU.pow).then_inc(x_pow, 1)
                    if isinstance(b, int) and b == -2:
                        for i in range(2):
                            nc.gpsimd.memset(va[i][:, :, :, HD + 1:CT], 0.0).then_inc(cleared, 1)
                            nc.gpsimd.memset(va[i][:, :, :, HD:HD + 1], 1.0).then_inc(cleared, 1)
                    else:
                        split_qk(b + 2, 0)
                        split_qk(b + 2, 1)

            walk(pool, units, LOOP_U1, True)
            layernorm_pool(nc, pool, g, ln, NB - 1)


def shared(ctx, nc, x, ident_in, fill):
    def sb(name, shape):
        return ctx.enter_context(nc.sbuf_tensor("g_" + name, shape, F32))

    def sem(name):
        return ctx.enter_context(nc.semaphore(name))

    return {"X": sb("X", [P, NB, NT, P]), "ident": sb("ident", [P, P]), "eps": sb("eps", [P, NT]),
            "neg_half": sb("neg_half", [P, NT]), "zero": sb("zero", [P, 1]), "x": x, "fill": fill, "ident_in": ident_in,
            "x_in": sem("x_in"), "x_out": sem("x_out"), "consts_in": sem("consts_in"), "consts": sem("consts")}


def setup(nc, g):
    with nc.Block() as block:
        @block.sync
        def _(sp):
            sp.dma_start(g["ident"][:, :], g["ident_in"]).then_inc(g["consts_in"], 16)

        @block.gpsimd
        def _(pool):
            nc.gpsimd.memset(g["eps"][:, :], LN_EPS).then_inc(g["consts"], 1)
            nc.gpsimd.memset(g["neg_half"][:, :], -0.5).then_inc(g["consts"], 1)
            nc.gpsimd.memset(g["zero"][:, :], 0.0).then_inc(g["consts"], 1)
            pool.wait_ge(g["consts"], 3)


def turn_x_and_route(nc, g, r, ctx, xh, xl, weights, gate):
    X, exp_logits = g["X"], g["exp_logits"]
    xt = ctx.enter_context(nc.sbuf_tensor("moe_xt", [P, NB, T], F32))
    ps = ctx.enter_context(nc.psum_tensor("moe_ps_x", [P, 2, T], F32))
    ps_l0 = ctx.enter_context(nc.psum_tensor("moe_ps_l0", [P, T], F32))
    ps_l = ctx.enter_context(nc.psum_tensor("moe_ps_l", [P, 2 * T // E, E], F32))
    turned, copied, x_hi, w_hi, parted, logits, exp_done = (
        ctx.enter_context(nc.semaphore("moe_" + n))
        for n in ("turned", "copied", "x_hi", "w_hi", "parted", "logits", "exp_done"))
    W_POOL, X_POOL = (1, 2), range(5)
    with nc.Block() as block:
        @block.tensor
        def _(pe):
            for b in range(NB):
                if b >= 2:
                    pe.wait_ge(copied, b - 1)
                for k in range(NT):
                    mm = nc.tensor.transpose(ps[:, b % 2, k * P:(k + 1) * P], X[:, b, k, :], g["ident"][:, :])
                mm.then_inc(turned, 1)
            for b in range(NB):
                pe.wait_ge(copied, b + 1)
                for k in range(NT):
                    dst = ps_l0[:, k * E:(k + 1) * E] if b == 0 else ps_l[:, (b - 1) * NT + k, :]
                    mm = nc.tensor.matmul(dst, xt[:, b, k * P:(k + 1) * P], gate[:, :], start=True, stop=True)
                if b in (0, NB - 1):
                    mm.then_inc(logits, 1)

        @block.scalar
        def _(act):
            def weight_hi(n):
                nc.scalar.activation(weights[n][1][:, :, :], weights[n][0][:, :, :], ACT.Copy).then_inc(w_hi, 1)

            def x_part(b):
                act.wait_ge(copied, b + 1)
                nc.scalar.activation(xh[:, b, :], xt[:, b, :], ACT.Copy).then_inc(x_hi, 1)

            weight_hi(0)
            weight_hi(1)
            x_part(0)
            weight_hi(2)
            act.wait_ge(logits, 1)
            nc.scalar.activation(exp_logits[:, 0:NT, :], ps_l0[:, 0:NT * E].rearrange("p (t e) -> p t e", e=E),
                                 ACT.Exp, scale=-1.0).then_inc(exp_done, 1)
            for b in range(1, NB):
                x_part(b)
            act.wait_ge(logits, 2)
            nc.scalar.activation(exp_logits[:, NT:, :], ps_l[:, 0:(NB - 1) * NT, :], ACT.Exp,
                                 scale=-1.0).then_inc(exp_done, 1)

        @block.vector
        def _(dve):
            nc.vector.tensor_copy(r["identb"][:, :], g["ident"][:, :])
            for b in range(NB):
                dve.wait_ge(turned, b + 1)
                nc.vector.tensor_copy(xt[:, b, :], ps[:, b % 2, :]).then_inc(copied, 1)
            for n, (raw, hi, lo) in enumerate(weights):
                if n not in W_POOL:
                    dve.wait_ge(w_hi, n + 1)
                    nc.vector.tensor_tensor(lo[:, :, :], raw[:, :, :], hi[:, :, :], ALU.subtract).then_inc(parted, 1)
            dve.wait_ge(exp_done, 1)
            for k in range(STEPS):
                route_step(nc, dve, g, r, 0, k)
            for b in range(NB):
                if b not in X_POOL:
                    dve.wait_ge(x_hi, b + 1)
                    nc.vector.tensor_tensor(xl[:, b, :], xt[:, b, :], xh[:, b, :], ALU.subtract).then_inc(parted, 1)

        @block.gpsimd
        def _(pool):
            for n in W_POOL:
                raw, hi, lo = weights[n]
                pool.wait_ge(w_hi, n + 1)
                nc.gpsimd.tensor_tensor(lo[:, :, :], raw[:, :, :], hi[:, :, :], ALU.subtract).then_inc(parted, 1)
            for b in X_POOL:
                pool.wait_ge(x_hi, b + 1)
                nc.gpsimd.tensor_tensor(xl[:, b, :], xt[:, b, :], xh[:, b, :], ALU.subtract).then_inc(parted, 1)


def router_buffers(ctx, nc, g):
    def sb(name, shape, dt=F32):
        return ctx.enter_context(nc.sbuf_tensor("r_" + name, shape, dt))

    r = {n: sb(n, shape) for n, shape in (
        ("e1", [P, NT, E]), ("score", [P, NT, E]), ("sfc", [P, NT, E]), ("gmax", [P, NT, NGRP]),
        ("top", [P, NT, 8]), ("topf", [P, NT, 8]), ("gmask", [P, NT, NGRP]), ("hit", [P, NT, TOPK, E]),
        ("den", [P, NT]), ("carrier", [P, 1]))}
    r["topi"] = sb("topi", [P, NT, 8], U32)
    r["cpart"] = sb("cpart", [P, NT, PARTS, E], BF16)
    r["identb"] = sb("identb", [P, P], BF16)
    r["vec"] = ctx.enter_context(nc.semaphore("r_vec"))
    return r


STEPS = 25
STEPS_BEHIND = (4, 6, 8, 8, 8, 10, 10, 12, 13, 14, 15, 18, 22, STEPS)


def route_step(nc, dve, g, r, b, k):
    v, vec = nc.vector, r["vec"]
    e1, score, sfc, den, cpart = r["e1"], r["score"], r["sfc"], r["den"], r["cpart"]
    groups = "p t (g e) -> p t g e"

    def largest(values):
        for t in range(NT):
            ins = v.max(r["top"][:, t, :], values[:, t, :])
        return ins

    def places(values):
        for t in range(NT):
            ins = v.max_index(r["topi"][:, t, :], r["top"][:, t, :], values[:, t, :])
        return ins

    def hits(n, width):
        shape = [P, NT, n, width]
        return v.tensor_tensor(r["hit"][:, :, 0:n, 0:width], r["topf"][:, :, 0:n].unsqueeze(3).broadcast_to(shape),
                               g["iota"][:, 0:width].unsqueeze(1).unsqueeze(1).broadcast_to(shape), ALU.is_equal)

    def any_hit(dst, n, width):
        return v.tensor_reduce(dst, r["hit"][:, :, 0:n, 0:width].rearrange("p t k e -> p t e k"), AX.X, ALU.add)

    if not (isinstance(b, int) and b == 0 and k == 0):
        dve.wait_ge(vec, STEPS * b + k)
    if k == 0:
        v.memset(r["carrier"][:, :], 0.0)
        ins = v.tensor_scalar(e1[:, :, :], g["exp_logits"][:, bass.ds(b * NT, NT), :], 1.0, None, ALU.add)
    elif k == 1:
        ins = v.reciprocal(score[:, :, :], e1[:, :, :])
    elif k == 2:
        ins = v.tensor_tensor(sfc[:, :, :], score[:, :, :], g["bias"][:, :].unsqueeze(1).broadcast_to([P, NT, E]),
                              ALU.add)
    elif k == 3:
        ins = v.tensor_reduce(r["gmax"][:, :, :], sfc[:, :, :].rearrange(groups, g=NGRP), AX.X, ALU.max)
    elif k in (4, 10):
        v.memset(r["carrier"][:, :], 0.0)
        ins = largest(r["gmax"] if k == 4 else sfc)
    elif k in (5, 11):
        v.memset(r["carrier"][:, :], 0.0)
        ins = places(r["gmax"] if k == 5 else sfc)
    elif k in (6, 12):
        ins = v.tensor_copy(r["topf"][:, :, :], r["topi"][:, :, :])
    elif k == 7:
        ins = hits(TOPG, NGRP)
    elif k == 8:
        ins = any_hit(r["gmask"][:, :, :], TOPG, NGRP)
    elif k == 9:
        ins = v.tensor_tensor(sfc[:, :, :].rearrange(groups, g=NGRP), sfc[:, :, :].rearrange(groups, g=NGRP),
                              r["gmask"][:, :, :].unsqueeze(3).broadcast_to([P, NT, NGRP, E // NGRP]), ALU.mult)
    elif k == 13:
        ins = hits(TOPK, E)
    elif k == 14:
        ins = any_hit(e1[:, :, :], TOPK, E)
    elif k == 15:
        ins = v.tensor_tensor(score[:, :, :], score[:, :, :], e1[:, :, :], ALU.mult)
    elif k == 16:
        ins = v.tensor_reduce(den[:, :], score[:, :, :], AX.X, ALU.add)
    elif k == 17:
        ins = v.tensor_scalar_add(den[:, :], den[:, :], 1e-20)
    elif k == 18:
        ins = v.reciprocal(den[:, :], den[:, :])
    elif k == 19:
        ins = v.tensor_scalar(den[:, :], den[:, :], ROUTE_SCALE, None, ALU.mult)
    elif k == 20:
        ins = v.tensor_tensor(score[:, :, :], score[:, :, :], den[:, :].unsqueeze(2).broadcast_to([P, NT, E]),
                              ALU.mult)
    elif k == 21:
        ins = v.tensor_copy(cpart[:, :, 0, :], score[:, :, :])
    elif k == 22:
        ins = v.tensor_tensor(e1[:, :, :], score[:, :, :], cpart[:, :, 0, :], ALU.subtract)
    elif k == 23:
        ins = v.tensor_copy(cpart[:, :, 1, :], e1[:, :, :])
    elif k == 24:
        ins = v.tensor_tensor(cpart[:, :, 2, :], e1[:, :, :], cpart[:, :, 1, :], ALU.subtract)
    ins.then_inc(vec, 1)


def feed_forward(nc, g, name, n_un, xh, xl, wg, wu, wd, routed=None, out=None):
    with ExitStack() as ctx:
        def sb(n, shape, dt=F32):
            return ctx.enter_context(nc.sbuf_tensor(f"{name}_{n}", shape, dt))

        def sem(n):
            return ctx.enter_context(nc.semaphore(f"{name}_{n}"))

        X = g["X"]
        LAG = 3
        END = n_un + LAG
        CT_TURN, CT_COPY = 15, 16
        RG = 2 if routed else 3
        RH = min(4, n_un)
        n_c = n_un - 1 if routed else 0
        gated = sb("gated", [P, RG, T])
        prod = sb("prod", [P, RG, T])
        hid = sb("hid", [P, 3, T])
        hh = sb("hh", [P, RH + n_un % RH, T], F32R)
        hl = sb("hl", [P, RH + n_un % RH, T], F32R)
        dsb = sb("dsb", [P, T])
        y = sb("y", [P, NT, P])
        ln = layernorm_buffers(ctx, nc, name)
        ps = ctx.enter_context(nc.psum_tensor(f"{name}_ps", [P, 8, T], F32))
        ps_g, ps_u, ps_d, ps_t = ps[:, 0:RG, :], ps[:, RG:2 * RG, :], ps[:, 6, :], ps[:, 7, :]
        if routed:
            r, sel = routed
            ct = sb("ct", [PARTS * E, NB, T], BF16)
            ps_c = ps[:, 4:6, :]
            ps_ct = ps[0:PARTS * E, 7, :].bitcast(BF16)
        g_done, u_done, c_done, silu_done, prod_done, hid_done, hh_done, hl_done, d_done, d_taken = (
            sem(n) for n in ("g_done", "u_done", "c_done", "silu_done", "prod_done", "hid_done", "hh_done",
                             "hl_done", "d_done", "d_taken"))
        t_done, t_taken, ct_turned, ct_taken = (sem(n) for n in ("t_done", "t_taken", "ct_turned", "ct_taken"))
        C = 6

        def place(j, ring):
            even = n_un - n_un % ring
            return j % ring if j < even else ring + j - even

        def since(j, place_of, limit=n_un):
            same = [q for q in range(limit) if place_of(q) == place_of(j)]
            before = [j - q for q in same if q < j]
            return min(before or [n_un + j - q for q in same])

        bank = lambda j: 1 if RG == 2 and j == n_un - 1 else j % RG
        hid_at = lambda j: j % 3
        part_at = lambda j: place(j, RH)

        def at(b, j, delay=0):
            back, j = -((j - delay) // n_un), (j - delay) % n_un
            if isinstance(b, int) and not 0 <= b - back < NB:
                return None
            return b - back, j

        def end_of(b, j, delay=0):
            unit = at(b, j, END + delay)
            return unit[0] if unit is not None and unit[1] == 0 else None

        def walk(eng, step):
            peel = (END + 3) // n_un
            for b in range(peel):
                for j in range(n_un):
                    step(b, j)
            with eng.Fori(peel, NB - 1) as b:
                for j in range(n_un):
                    step(b, j)
            for k in range(n_un + END + 4):
                step(NB - 1 + k // n_un, k % n_un)

        def routes(b):
            return routed and not (isinstance(b, int) and b + 1 >= NB)

        block = ctx.enter_context(nc.Block())

        if out is not None:
            @block.sync
            def _(sp):
                rows = out.rearrange("b (k p) d -> p b k d", p=P)
                with sp.Fori(0, NB) as b:
                    sp.wait_ge(ln["x_done"], b + 2)
                    sp.dma_start(rows[:, bass.ds(b, 1), :, :], X[:, bass.ds(b, 1), :, :]).then_inc(g["x_out"], 16)
                sp.wait_ge(g["x_out"], 16 * NB)

        @block.tensor
        def _(pe):
            pe.sem_inc(d_done, C)

            def product(dst, w, x_parts, j):
                hi, lo = x_parts
                nc.tensor.matmul(dst, w[0][:, j, :], hi, start=True, stop=False)
                nc.tensor.matmul(dst, w[1][:, j, :], hi, start=False, stop=False)
                return nc.tensor.matmul(dst, w[0][:, j, :], lo, start=False, stop=True)

            def unit(b, j):
                n = n_un * b + j
                x_parts = (xh[:, b, :], xl[:, b, :])
                pe.wait_ge(silu_done, n - since(j, bank) + 1 + C)
                product(ps_g[:, bank(j), :], wg, x_parts, j).then_inc(g_done, 1)
                pe.wait_ge(prod_done, n - since(j, bank) + 1 + C)
                product(ps_u[:, bank(j), :], wu, x_parts, j).then_inc(u_done, 1)
                if j < n_c:
                    if j == 0:
                        pe.wait_ge(ct_taken, b + 1)
                    pe.wait_ge(hid_done, n - since(j, bank, n_c) + 1 + C)
                    nc.tensor.matmul(ps_c[:, j % 2, :], sel[:, j, :], ct[:, b, :], start=True,
                                     stop=True).then_inc(c_done, 1)

            def down(b, j):
                n = n_un * b + j
                pe.wait_ge(hh_done, n + 1 + C)
                if j == 0:
                    pe.wait_ge(d_taken, b + C)
                k = part_at(j)
                nc.tensor.matmul(ps_d, wd[0][:, j, :], hh[:, k, :], start=(j == 0), stop=False)
                nc.tensor.matmul(ps_d, wd[1][:, j, :], hh[:, k, :], start=False, stop=False)
                pe.wait_ge(hl_done, n + 1 + C)
                nc.tensor.matmul(ps_d, wd[0][:, j, :], hl[:, k, :], start=False,
                                 stop=(j == n_un - 1)).then_inc(d_done, 1)

            def turn(b):
                pe.wait_ge(d_taken, b + 1 + C)
                pe.wait_ge(t_taken, b + C)
                if routed:
                    pe.wait_ge(ct_taken, min(b + 2, NB) if isinstance(b, int) else b + 2)
                for q in range(NT):
                    mm = nc.tensor.transpose(ps_t[:, q * P:(q + 1) * P], dsb[:, q * P:(q + 1) * P], g["ident"][:, :])
                mm.then_inc(t_done, 1)

            def turn_ct(b):
                pe.wait_ge(r["vec"], STEPS * (b + 1))
                if not isinstance(b, int) or b >= 2:
                    pe.wait_ge(t_taken, b - 1 + C)
                for k in range(NT):
                    mm = nc.tensor.transpose(ps_ct[:, k * P:(k + 1) * P], r["cpart"][:, k, :, :], r["identb"][:, :])
                mm.then_inc(ct_turned, 1)

            def step(b, j):
                if at(b, j) is not None:
                    unit(b, j)
                if at(b, j, LAG) is not None:
                    down(*at(b, j, LAG))
                if end_of(b, j) is not None:
                    turn(end_of(b, j))
                if j == CT_TURN and routes(b):
                    turn_ct(b + 1)

            if routed:
                turn_ct(0)
            walk(pe, step)

        @block.scalar
        def _(act):
            act.sem_inc(silu_done, C)
            act.sem_inc(d_taken, C)
            act.sem_inc(hh_done, C)

            def silu(b, j):
                n = n_un * b + j
                act.wait_ge(g_done, n + 1)
                act.wait_ge(prod_done, n - since(j, bank) + 1 + C)
                nc.scalar.activation(gated[:, bank(j), :], ps_g[:, bank(j), :], ACT.Silu).then_inc(silu_done, 1)

            def hidden_hi(b, j):
                n = n_un * b + j
                act.wait_ge(hid_done, n + 1 + C)
                act.wait_ge(d_done, n - since(j, part_at) + 1 + C)
                nc.scalar.activation(hh[:, part_at(j), :], hid[:, hid_at(j), :], ACT.Copy).then_inc(hh_done, 1)

            def step(b, j):
                if end_of(b, j) is not None:
                    act.wait_ge(d_done, n_un * (end_of(b, j) + 1) + C)
                    nc.scalar.activation(dsb[:, :], ps_d, ACT.Copy).then_inc(d_taken, 1)
                if at(b, j) is not None:
                    silu(b, j)
                if at(b, j, 1) is not None:
                    hidden_hi(*at(b, j, 1))

            walk(act, step)

        @block.vector
        def _(dve):
            dve.sem_inc(prod_done, C)
            dve.sem_inc(hid_done, C)
            dve.sem_inc(t_taken, C)
            dve.sem_inc(ln["x_done"], 1)

            def unit(b, j):
                n = n_un * b + j
                dve.wait_ge(silu_done, n + 1 + C)
                dve.wait_ge(u_done, n + 1)
                dst, src = hid[:, hid_at(j), :], (gated[:, bank(j), :], ps_u[:, bank(j), :])
                if j < n_c:
                    nc.vector.tensor_tensor(prod[:, bank(j), :], *src, ALU.mult).then_inc(prod_done, 1)
                    dve.wait_ge(prod_done, n + 1 + C)
                    dve.wait_ge(c_done, n_c * b + j + 1)
                    dve.wait_ge(hl_done, n - since(j, hid_at) + 1 + C)
                    nc.vector.tensor_tensor(dst, prod[:, bank(j), :], ps_c[:, j % 2, :],
                                            ALU.mult).then_inc(hid_done, 1)
                else:
                    dve.wait_ge(hl_done, n - since(j, hid_at) + 1 + C)
                    nc.vector.tensor_tensor(dst, *src, ALU.mult).then_inc(prod_done, 1)
                    dve.wait_ge(prod_done, n + 1 + C)
                    nc.vector.memset(ln["gate"][:, :], 0.0).then_inc(hid_done, 1)

            def copy_ct(b):
                dve.wait_ge(ct_turned, b + 1)
                nc.vector.memset(r["carrier"][:, :], 0.0)
                nc.vector.tensor_copy(ct[:, b, :], ps_ct[:, 0:T]).then_inc(ct_taken, 1)

            def step(b, j):
                if at(b, j) is not None:
                    unit(b, j)
                if end_of(b, j, 3) is not None:
                    layernorm_apply(nc, dve, g, ln, end_of(b, j, 3), y)
                if end_of(b, j) is not None:
                    e = end_of(b, j)
                    dve.wait_ge(ln["x_done"], e + 1)
                    dve.wait_ge(t_done, e + 1)
                    nc.vector.tensor_tensor(y[:, :, :], ps_t.rearrange("p (k d) -> p k d", k=NT), X[:, e, :, :],
                                            ALU.add).then_inc(t_taken, 1)
                if end_of(b, j, 1) is not None:
                    dve.wait_ge(t_taken, end_of(b, j, 1) + 1 + C)
                    layernorm_stats(nc, dve, ln, end_of(b, j, 1), y)
                if routes(b):
                    if j < len(STEPS_BEHIND):
                        for k in range(STEPS_BEHIND[j - 1] if j else 0, STEPS_BEHIND[j]):
                            route_step(nc, dve, g, r, b + 1, k)
                    if j == CT_COPY:
                        copy_ct(b + 1)

            if routed:
                copy_ct(0)
            walk(dve, step)

        @block.gpsimd
        def _(pool):
            pool.sem_inc(hl_done, C)

            def hidden_lo(b, j):
                n = n_un * b + j
                pool.wait_ge(hh_done, n + 1 + C)
                nc.gpsimd.tensor_tensor(hl[:, part_at(j), :], hid[:, hid_at(j), :], hh[:, part_at(j), :],
                                        ALU.subtract).then_inc(hl_done, 1)

            def step(b, j):
                if at(b, j, 1) is not None:
                    hidden_lo(*at(b, j, 1))
                if end_of(b, j, 2) is not None:
                    layernorm_pool(nc, pool, g, ln, end_of(b, j, 2))

            walk(pool, step)


def prepare_ffn_weights(nc, dve, ff, w):
    done, n = ff["done"], 0
    dve.wait_ge(ff["in"], 16 * len(ff["weights"]))
    for _, ints, hi, lo in ff["weights"]:
        nc.vector.tensor_copy(w, ints[:, :, :]).then_inc(done, 1)
        dve.wait_ge(done, n + 1)
        nc.vector.tensor_scalar(w, w, WEIGHT_SCALE, None, ALU.mult).then_inc(done, 1)
        dve.wait_ge(done, n + 2)
        nc.vector.tensor_copy(hi[:, :, :], w).then_inc(done, 1)
        dve.wait_ge(done, n + 3)
        nc.vector.tensor_tensor(lo[:, :, :], w, hi[:, :, :], ALU.subtract).then_inc(done, 1)
        n += 4
        dve.wait_ge(done, n)


def program(nc, ident, fill, iota, sel, x, x_t, w_qkv, gate_t, bias, wg, wu, wd, w1, b1, v_b, o_b, qn, kn, cos, sin,
            fg, fu, fd, out):
    with ExitStack() as ctx:
        g = shared(ctx, nc, x, ident, fill)
        c1 = {n: ctx.enter_context(nc.sbuf_tensor("a1_" + n, shape, F32)) for n, shape in ATT1_SHAPES.items()}
        c1_in = ctx.enter_context(nc.semaphore("a1_in"))
        setup(nc, g)
        with ExitStack() as part:
            def sb(name, shape, dt=F32, ctx=part):
                return ctx.enter_context(nc.sbuf_tensor(name, shape, dt))

            raw = [sb(f"moe_w{n}", [P, FF, P]) for n in "gud"]
            sel_sb = sb("moe_sel", [PARTS * E, NPAIR, P], BF16)
            gate_sb = sb("router_gate", [P, E])
            g["bias"], g["iota"] = sb("moe_bias", [P, E]), sb("moe_iota", [P, E])
            moe_in = part.enter_context(nc.semaphore("moe_in"))

            def load_moe(sp):
                for dst, src in zip(raw + [sel_sb], (wg, wu, wd, sel)):
                    sp.dma_start(dst[:, :, :], src).then_inc(moe_in, 16)
                sp.dma_start(gate_sb[:, :], gate_t).then_inc(moe_in, 16)
                for dst, src in ((g["bias"], bias), (g["iota"], iota)):
                    sp.dma_start(dst[:, :], bass.AP(tensor=src.tensor, offset=0,
                                                    ap=[[0, P], [1, E]])).then_inc(moe_in, 16)

            def load_attention1(sp):
                for dst, src in ((c1["w"][:, :, :], w1), (c1["bqk"][:, :], b1), (c1["cos"][:, :], cos),
                                 (c1["sin"][:, :], sin), (c1["norm_scale"][:, 0:1], qn),
                                 (c1["norm_scale"][:, 1:2], kn),
                                 (c1["vb"][:, :], bass.AP(tensor=v_b.tensor, offset=0, ap=[[0, P], [1, P]])),
                                 (c1["ob"][:, :], bass.AP(tensor=o_b.tensor, offset=0, ap=[[0, P], [1, P]]))):
                    sp.dma_start(dst, src).then_inc(c1_in, 16)

            def load_more(sp):
                load_moe(sp)
                load_attention1(sp)

            def all_in(sp):
                sp.wait_ge(moe_in, 7 * 16)
                sp.wait_ge(c1_in, 8 * 16)

            attention0(nc, g, x_t, w_qkv, load_more, all_in)
            weights = [(w, sb(f"moe_hi{n}", [P, FF, P], F32R), sb(f"moe_lo{n}", [P, FF, P], F32R))
                       for n, w in enumerate(raw)]
            xh, xl = sb("moe_xh", [P, NB, T], F32R), sb("moe_xl", [P, NB, T], F32R)
            g["exp_logits"] = sb("moe_exp", [P, NB * NT, E])
            r = router_buffers(part, nc, g)
            with ExitStack() as turning:
                turn_x_and_route(nc, g, r, turning, xh, xl, weights, gate_sb)
            feed_forward(nc, g, "moe", FF, xh, xl, *(w[1:] for w in weights),
                         routed=(r, sel_sb))
        with ExitStack() as part:
            def sb(name, shape, dt=F32):
                return part.enter_context(nc.sbuf_tensor(name, shape, dt))

            shape = [P, NH3, P]
            ff = {"in": part.enter_context(nc.semaphore("ff_in")), "done": part.enter_context(nc.semaphore("ff_done")),
                  "weights": [(src, sb("ff_i" + n, shape, I32), sb("ff_whi" + n, shape, F32R),
                               sb("ff_wlo" + n, shape, F32R)) for n, src in (("g", fg), ("u", fu), ("d", fd))]}
            xh, xl = sb("ff_xh", [P, NB, T], F32R), sb("ff_xl", [P, NB, T], F32R)
            attention1(nc, g, c1, xh, xl, ff)
            feed_forward(nc, g, "ff", NH3, xh, xl, *(w[2:] for w in ff["weights"]), out=out)


def layouts(i):
    import numpy as np
    r = {}
    r["ident"] = np.eye(P, dtype=np.float32)
    r["fill"] = np.stack([np.zeros(H * T), np.ones(H * T)]).astype("bfloat16")
    r["iota"] = np.arange(E, dtype=np.float32)
    sel = np.zeros((PARTS, E, NPAIR, P), np.float32)
    for j in range(NPAIR):
        sel[:, 2 * j, j, :EI] = 1
        sel[:, 2 * j + 1, j, EI:] = 1
    r["sel"] = sel.reshape(PARTS * E, NPAIR, P).astype("bfloat16")
    x = np.asarray(i["L0_attn_x"])
    r["x"] = x
    r["x_t"] = np.ascontiguousarray(x.reshape(NB * T, P).T)
    dims, heads = np.divmod(np.arange(P), H)
    order = heads * HD + dims
    turned = heads * HD + (dims ^ 1)
    w = np.asarray(i["L0_attn_W_qkv"])
    r["w_qkv"] = np.ascontiguousarray(np.concatenate([w[:, :P][:, order], w[:, P:2 * P][:, order], w[:, 2 * P:]], 1))
    r["gate_t"] = np.ascontiguousarray(np.asarray(i["L0_ffn_gate_weight"]).T)
    r["bias"] = np.asarray(i["L0_ffn_e_score_correction_bias"])
    gu = np.asarray(i["L0_ffn_experts_gate_up"])
    for n, (a, shared_w) in {"wg": (gu[:, :EI], i["L0_ffn_shared_gate_w"]),
                             "wu": (gu[:, EI:], i["L0_ffn_shared_up_w"])}.items():
        rows = np.concatenate([a.reshape(E * EI, P), np.asarray(shared_w)], 0)
        r[n] = np.ascontiguousarray(rows.T.reshape(P, FF, P))
    down = np.asarray(i["L0_ffn_experts_down"]).transpose(0, 2, 1).reshape(E * EI, P)
    down = np.concatenate([down, np.asarray(i["L0_ffn_shared_down_w"]).T], 0)
    r["wd"] = np.ascontiguousarray(down.reshape(FF, P, P).transpose(1, 0, 2))
    q, k, v, o = (np.asarray(i[f"L1_attn_{n}_w"]).T for n in "qkvo")
    r["w1"] = np.ascontiguousarray(np.stack([q[:, order], q[:, turned], k[:, order], k[:, turned], v, o], 1))
    qb, kb = np.asarray(i["L1_attn_q_b"]), np.asarray(i["L1_attn_k_b"])
    r["b1"] = np.ascontiguousarray(np.stack([qb[order], qb[turned], kb[order], kb[turned]], 1))
    r["v_b"], r["o_b"] = np.asarray(i["L1_attn_v_b"]), np.asarray(i["L1_attn_o_b"])
    r["qn"] = np.asarray(i["L1_attn_qn_scale"]).reshape(P, 1)
    r["kn"] = np.asarray(i["L1_attn_kn_scale"]).reshape(P, 1)
    inv = (1.0 / np.float32(10000.0) ** (np.arange(0, HD, 2, dtype=np.float32) / np.float32(HD))).astype(np.float32)
    freq = inv[dims % (HD // 2)][:, None] * np.arange(T, dtype=np.float32)[None, :]
    r["cos"] = np.cos(freq).astype(np.float32)
    r["sin"] = (np.sin(freq) * np.where(dims % 2, 1, -1)[:, None]).astype(np.float32)
    for n, a in (("fg", "gate"), ("fu", "up")):
        r[n] = np.ascontiguousarray(np.asarray(i["L1_ffn_w_" + a]).T.reshape(P, NH3, P))
    r["fd"] = np.ascontiguousarray(np.asarray(i["L1_ffn_w_down"]).T.reshape(NH3, P, P).transpose(1, 0, 2))
    return r


def kernel(**inputs):
    import concourse.bacc as _bacc
    from concourse import mybir as _mybir
    from concourse.bass_utils import run_bass_kernel_spmd as _run

    nc = _bacc.Bacc("TRN2", target_bir_lowering=False, num_devices=1)
    arrays, args = {}, []
    for name, a in layouts(inputs).items():
        arrays[f"in_{name}"] = a
        args.append(nc.dram_tensor(f"in_{name}", a.shape, _mybir.dt.from_np(a.dtype), kind="ExternalInput").ap())
    out = nc.dram_tensor("out_x", (NB, T, P), F32, kind="ExternalOutput").ap()
    program(nc, *args, out)
    r = _run(nc, [arrays], core_ids=[0])
    return r.results[0]["out_x"]
```
